# Optimizing a Trainium2 kernel written in Bass

```python
import numpy as np
import jax
import jax.numpy as jnp

def _softmax(x, axis=-1):
    return jax.nn.softmax(x, axis=axis)

def _gelu(x):
    return jax.nn.gelu(x, approximate=True)

def _silu(x):
    return jax.nn.silu(x)

def _sigmoid(x):
    return jax.nn.sigmoid(x)

def _layernorm(x, axis=-1, eps=1e-05):
    m = jnp.mean(x, axis=axis, keepdims=True)
    v = jnp.var(x, axis=axis, keepdims=True)
    return (x - m) / jnp.sqrt(v + eps)

def _scatter_add(tgt, idx, src, axis=0):
    return tgt.at[idx].add(src)

def _segment_sum(src, seg, n):
    return jax.ops.segment_sum(src, seg, n)
kernel_name = 'mk_gnn_ffn_d2_gnn_r32_690c3f'

def setup_inputs(seed: int=0):
    np.random.seed(seed)
    _w = jnp.asarray

    def _rec_inputs():
        import jax
        import jax.numpy as jnp
        _gk = jax.random.key(seed)
        x = -0.0003713 + 1 * jax.random.normal(jax.random.fold_in(_gk, 1), (3125, 256), jnp.float32)
        _s = jax.random.randint(jax.random.fold_in(_gk, 2), (25000,), 0, 3125, jnp.int32)
        _d = jax.random.randint(jax.random.fold_in(_gk, 3), (25000,), 0, 3125, jnp.int32)
        _loop = jnp.arange(3125, dtype=jnp.int32)
        src = jnp.concatenate([_s, _d, _loop])
        dst = jnp.concatenate([_d, _s, _loop])
        _o = jnp.argsort(dst, stable=True)
        src = src[_o]
        dst = dst[_o]
        edge_weight = jax.random.uniform(jax.random.fold_in(_gk, 12), (53125,), jnp.float32, 0.0, 0.999998)
        node_vec = jax.random.uniform(jax.random.fold_in(_gk, 13), (3125,), jnp.float32, 0.0, 0.999833)
        return (x, src, dst, edge_weight, node_vec)
    x, src, dst, edge_weight, node_vec = _rec_inputs()

    def _L0_gnn_setup():
        import jax, jax.numpy as jnp
        import numpy as np
        N = 50000
        E = 25000
        IN = 256
        HD = 4
        D = 64
        key = jax.random.key(seed)
        k1, k2, k3, k4, k5 = jax.random.split(key, 5)
        h = jax.random.normal(k1, (N, IN), dtype=jnp.float32)
        edge_index = jax.random.randint(k2, (2, E), 0, N)
        W = jax.random.normal(k3, (IN, HD * D), dtype=jnp.float32) * (1.0 / np.sqrt(IN))
        a_src = jax.random.normal(k4, (HD, D), dtype=jnp.float32) * 0.1
        a_dst = jax.random.normal(k5, (HD, D), dtype=jnp.float32) * 0.1
        return {'h': h, 'edge_index': edge_index, 'W': W, 'a_src': a_src, 'a_dst': a_dst}
    _L0_gnn_all = _L0_gnn_setup()
    _L0_gnn_in = {k: v for k, v in _L0_gnn_all.items() if k in ('W', 'a_src', 'a_dst')}
    del _L0_gnn_all

    def _L0_ffn_setup():
        import jax, jax.numpy as jnp
        import numpy as np
        DIM = 256
        H = 8
        D = 64
        G = 64
        INNER = H * D
        SCALE = D ** (-0.5)
        key = jax.random.key(seed)
        ks = jax.random.split(key, 12)
        B, N = (4, 512)
        x = jax.random.normal(ks[0], (B, N, DIM), dtype=jnp.float32)
        s = lambda fan_in: 1.0 / np.sqrt(fan_in)
        W_fx = jax.random.normal(ks[1], (DIM, INNER), dtype=jnp.float32) * s(DIM)
        b_fx = jnp.zeros((INNER,), dtype=jnp.float32)
        W_x = jax.random.normal(ks[2], (DIM, INNER), dtype=jnp.float32) * s(DIM)
        b_x = jnp.zeros((INNER,), dtype=jnp.float32)
        A = jax.random.normal(ks[3], (G, D), dtype=jnp.float32)
        Q, _ = jnp.linalg.qr(A.T)
        W_slice = Q[:, :G].astype(jnp.float32)
        b_slice = jnp.zeros((G,), dtype=jnp.float32)
        W_q = jax.random.normal(ks[4], (D, D), dtype=jnp.float32) * s(D)
        W_k = jax.random.normal(ks[5], (D, D), dtype=jnp.float32) * s(D)
        W_v = jax.random.normal(ks[6], (D, D), dtype=jnp.float32) * s(D)
        W_out = jax.random.normal(ks[7], (INNER, DIM), dtype=jnp.float32) * s(INNER)
        b_out = jnp.zeros((DIM,), dtype=jnp.float32)
        temperature = jnp.ones((1, H, 1, 1), dtype=jnp.float32) * 0.5
        return {'x': x, 'W_fx': W_fx, 'b_fx': b_fx, 'W_x': W_x, 'b_x': b_x, 'W_slice': W_slice, 'b_slice': b_slice, 'W_q': W_q, 'W_k': W_k, 'W_v': W_v, 'W_out': W_out, 'b_out': b_out, 'temperature': temperature}
    _L0_ffn_all = _L0_ffn_setup()
    _L0_ffn_in = {k: v for k, v in _L0_ffn_all.items() if k in ('W_fx', 'b_fx', 'W_x', 'b_x', 'W_slice', 'b_slice', 'W_q', 'W_k', 'W_v', 'W_out', 'b_out', 'temperature')}
    del _L0_ffn_all

    def _L1_gnn_setup():
        import jax, jax.numpy as jnp
        import numpy as np
        from jax import lax
        N, E, D = (256, 8192, 256)
        NH, FOUT = (4, 64)
        D_STATE, D_CONV, DT_RANK = (16, 4, 16)

        def _layer_norm(x, g, b, eps=1e-05):
            mu = jnp.mean(x, -1, keepdims=True)
            var = jnp.var(x, -1, keepdims=True)
            return (x - mu) * lax.rsqrt(var + eps) * g + b

        def _mamba(xs, in_proj_w, conv_w, conv_b, x_proj_w, dt_proj_w, dt_proj_b, A_log, D_param, out_proj_w):
            n = xs.shape[0]
            xz = xs @ in_proj_w.T
            xc, z = jnp.split(xz, 2, axis=-1)
            K = conv_w.shape[1]
            xp = jnp.pad(xc, ((K - 1, 0), (0, 0)))
            xc = sum((xp[k:k + n] * conv_w[:, k] for k in range(K))) + conv_b
            xc = jax.nn.silu(xc)
            dbc = xc @ x_proj_w.T
            dt = jax.nn.softplus(dbc[:, :DT_RANK] @ dt_proj_w.T + dt_proj_b)
            Bm = dbc[:, DT_RANK:DT_RANK + D_STATE]
            Cm = dbc[:, DT_RANK + D_STATE:]
            A = -jnp.exp(A_log)
            dA = jnp.exp(dt[:, :, None] * A)
            dBx = (dt * xc)[:, :, None] * Bm[:, None, :]

            def step(h, t):
                dA_t, dBx_t, C_t = t
                h = dA_t * h + dBx_t
                return (h, h @ C_t)
            _, y = lax.scan(step, jnp.zeros((xc.shape[1], D_STATE), xs.dtype), (dA, dBx, Cm))
            y = y + xc * D_param
            y = y * jax.nn.silu(z)
            return y @ out_proj_w.T

        def _forward(x, edge_index, deg_noise, gat_w, gat_a_src, gat_a_tgt, gat_b, ln_local_g, ln_local_b, ln_global_g, ln_global_b, ln2_g, ln2_b, in_proj_w, conv_w, conv_b, x_proj_w, dt_proj_w, dt_proj_b, A_log, D_param, out_proj_w, wl, wg, ff1_w, ff1_b, ff2_w, ff2_b):
            n = x.shape[0]
            src, tgt = (edge_index[0], edge_index[1])
            proj = (x @ gat_w.T).reshape(n, NH, FOUT)
            s_src = jnp.sum(proj * gat_a_src, -1)
            s_tgt = jnp.sum(proj * gat_a_tgt, -1)
            e = jax.nn.leaky_relu(s_src[src] + s_tgt[tgt], 0.2)
            exp_e = jnp.exp(e - jnp.max(e))
            denom = jax.ops.segment_sum(exp_e, tgt, num_segments=n)
            attn = exp_e / (denom[tgt] + 1e-16)
            agg = jax.ops.segment_sum(proj[src] * attn[:, :, None], tgt, num_segments=n)
            h_local = jax.nn.elu((agg + x.reshape(n, NH, FOUT)).reshape(n, NH * FOUT) + gat_b)
            h_local = _layer_norm(h_local, ln_local_g, ln_local_b)
            deg = jax.ops.segment_sum(jnp.ones((src.shape[0],), x.dtype), src, num_segments=n)
            perm = jnp.argsort(deg + deg_noise, stable=True)
            inv = jnp.argsort(perm)
            y = _mamba(x[perm], in_proj_w, conv_w, conv_b, x_proj_w, dt_proj_w, dt_proj_b, A_log, D_param, out_proj_w)
            h_attn = _layer_norm(x + y[inv], ln_global_g, ln_global_b)
            gate = jax.nn.sigmoid(h_local @ wl.T + h_attn @ wg.T)
            h = gate * h_local + (1.0 - gate) * h_attn
            ff = jax.nn.relu(h @ ff1_w.T + ff1_b) @ ff2_w.T + ff2_b
            return _layer_norm(h + ff, ln2_g, ln2_b)
        key = jax.random.key(seed)
        ks = jax.random.split(key, 24)
        w = lambda i, shape, s=0.05: jax.random.normal(ks[i], shape, dtype=jnp.float32) * s
        return {'x': jax.random.normal(ks[0], (N, D), dtype=jnp.float32), 'edge_index': jax.random.randint(ks[1], (2, E), 0, N, dtype=jnp.int32), 'edge_prob': jax.random.uniform(ks[2], (E,), dtype=jnp.float32), 'deg_noise': jax.random.uniform(ks[3], (N,), dtype=jnp.float32), 'gat_w': w(4, (NH * FOUT, D)), 'gat_a_src': w(5, (NH, FOUT)), 'gat_a_tgt': w(6, (NH, FOUT)), 'gat_b': jnp.zeros((NH * FOUT,), jnp.float32), 'ln_local_g': jnp.ones((D,), jnp.float32), 'ln_local_b': jnp.zeros((D,), jnp.float32), 'ln_global_g': jnp.ones((D,), jnp.float32), 'ln_global_b': jnp.zeros((D,), jnp.float32), 'ln2_g': jnp.ones((D,), jnp.float32), 'ln2_b': jnp.zeros((D,), jnp.float32), 'in_proj_w': w(7, (2 * D, D)), 'conv_w': w(8, (D, D_CONV), 0.2), 'conv_b': jnp.zeros((D,), jnp.float32), 'x_proj_w': w(9, (DT_RANK + 2 * D_STATE, D)), 'dt_proj_w': w(10, (D, DT_RANK)), 'dt_proj_b': w(11, (D,), 0.1) - 4.0, 'A_log': jnp.log(jnp.tile(jnp.arange(1, D_STATE + 1, dtype=jnp.float32), (D, 1))), 'D_param': jnp.ones((D,), jnp.float32), 'out_proj_w': w(12, (D, D)), 'wl': w(13, (D, D)), 'wg': w(14, (D, D)), 'ff1_w': w(15, (2 * D, D)), 'ff1_b': jnp.zeros((2 * D,), jnp.float32), 'ff2_w': w(16, (D, 2 * D)), 'ff2_b': jnp.zeros((D,), jnp.float32)}
    _L1_gnn_all = _L1_gnn_setup()
    _L1_gnn_in = {k: v for k, v in _L1_gnn_all.items() if k in ('gat_w', 'gat_a_src', 'gat_a_tgt', 'gat_b', 'ln_local_g', 'ln_local_b', 'ln_global_g', 'ln_global_b', 'ln2_g', 'ln2_b', 'in_proj_w', 'conv_w', 'conv_b', 'x_proj_w', 'dt_proj_w', 'dt_proj_b', 'A_log', 'D_param', 'out_proj_w', 'wl', 'wg', 'ff1_w', 'ff1_b', 'ff2_w', 'ff2_b')}
    del _L1_gnn_all

    def _L1_ffn_setup():
        import jax, jax.numpy as jnp
        import numpy as np
        BN_EPS = 0.001

        def _bn(h, g, b, m, v):
            return g * (h - m) * jax.lax.rsqrt(v + BN_EPS) + b
        key = jax.random.key(seed)
        ks = jax.random.split(key, 8)
        B, F, Df = (256, 64, 256)
        E, H, D = (8, 256, 256)
        s1 = 1.0 / np.sqrt(Df)
        s2 = 1.0 / np.sqrt(H)
        return {'x': jax.random.normal(ks[0], (B, F, Df), jnp.float32), 'Wr': jax.random.normal(ks[1], (Df, E), jnp.float32) * s1, 'br': jnp.zeros((E,), jnp.float32), 'W1': jax.random.normal(ks[2], (E, Df, H), jnp.float32) * s1, 'b1': jnp.zeros((E, H), jnp.float32), 'g1': jnp.ones((E, H), jnp.float32), 'be1': jnp.zeros((E, H), jnp.float32), 'm1': jnp.zeros((E, H), jnp.float32), 'v1': jnp.ones((E, H), jnp.float32), 'W2': jax.random.normal(ks[3], (E, H, H), jnp.float32) * s2, 'b2': jnp.zeros((E, H), jnp.float32), 'g2': jnp.ones((E, H), jnp.float32), 'be2': jnp.zeros((E, H), jnp.float32), 'm2': jnp.zeros((E, H), jnp.float32), 'v2': jnp.ones((E, H), jnp.float32), 'Wo': jax.random.normal(ks[4], (E, H, D), jnp.float32) * s2, 'bo': jnp.zeros((E, D), jnp.float32)}
    _L1_ffn_all = _L1_ffn_setup()
    _L1_ffn_in = {k: v for k, v in _L1_ffn_all.items() if k in ('Wr', 'br', 'W1', 'b1', 'g1', 'be1', 'm1', 'v1', 'W2', 'b2', 'g2', 'be2', 'm2', 'v2', 'Wo', 'bo')}
    del _L1_ffn_all
    return {'x': x, 'src': src, 'dst': dst, 'edge_weight': edge_weight, 'node_vec': node_vec, 'L0_gnn_W': _L0_gnn_in['W'], 'L0_gnn_a_src': _L0_gnn_in['a_src'], 'L0_gnn_a_dst': _L0_gnn_in['a_dst'], 'L0_ffn_W_fx': _L0_ffn_in['W_fx'], 'L0_ffn_b_fx': _L0_ffn_in['b_fx'], 'L0_ffn_W_x': _L0_ffn_in['W_x'], 'L0_ffn_b_x': _L0_ffn_in['b_x'], 'L0_ffn_W_slice': _L0_ffn_in['W_slice'], 'L0_ffn_b_slice': _L0_ffn_in['b_slice'], 'L0_ffn_W_q': _L0_ffn_in['W_q'], 'L0_ffn_W_k': _L0_ffn_in['W_k'], 'L0_ffn_W_v': _L0_ffn_in['W_v'], 'L0_ffn_W_out': _L0_ffn_in['W_out'], 'L0_ffn_b_out': _L0_ffn_in['b_out'], 'L0_ffn_temperature': _L0_ffn_in['temperature'], 'L1_gnn_gat_w': _L1_gnn_in['gat_w'], 'L1_gnn_gat_a_src': _L1_gnn_in['gat_a_src'], 'L1_gnn_gat_a_tgt': _L1_gnn_in['gat_a_tgt'], 'L1_gnn_gat_b': _L1_gnn_in['gat_b'], 'L1_gnn_ln_local_g': _L1_gnn_in['ln_local_g'], 'L1_gnn_ln_local_b': _L1_gnn_in['ln_local_b'], 'L1_gnn_ln_global_g': _L1_gnn_in['ln_global_g'], 'L1_gnn_ln_global_b': _L1_gnn_in['ln_global_b'], 'L1_gnn_ln2_g': _L1_gnn_in['ln2_g'], 'L1_gnn_ln2_b': _L1_gnn_in['ln2_b'], 'L1_gnn_in_proj_w': _L1_gnn_in['in_proj_w'], 'L1_gnn_conv_w': _L1_gnn_in['conv_w'], 'L1_gnn_conv_b': _L1_gnn_in['conv_b'], 'L1_gnn_x_proj_w': _L1_gnn_in['x_proj_w'], 'L1_gnn_dt_proj_w': _L1_gnn_in['dt_proj_w'], 'L1_gnn_dt_proj_b': _L1_gnn_in['dt_proj_b'], 'L1_gnn_A_log': _L1_gnn_in['A_log'], 'L1_gnn_D_param': _L1_gnn_in['D_param'], 'L1_gnn_out_proj_w': _L1_gnn_in['out_proj_w'], 'L1_gnn_wl': _L1_gnn_in['wl'], 'L1_gnn_wg': _L1_gnn_in['wg'], 'L1_gnn_ff1_w': _L1_gnn_in['ff1_w'], 'L1_gnn_ff1_b': _L1_gnn_in['ff1_b'], 'L1_gnn_ff2_w': _L1_gnn_in['ff2_w'], 'L1_gnn_ff2_b': _L1_gnn_in['ff2_b'], 'L1_ffn_Wr': _L1_ffn_in['Wr'], 'L1_ffn_br': _L1_ffn_in['br'], 'L1_ffn_W1': _L1_ffn_in['W1'], 'L1_ffn_b1': _L1_ffn_in['b1'], 'L1_ffn_g1': _L1_ffn_in['g1'], 'L1_ffn_be1': _L1_ffn_in['be1'], 'L1_ffn_m1': _L1_ffn_in['m1'], 'L1_ffn_v1': _L1_ffn_in['v1'], 'L1_ffn_W2': _L1_ffn_in['W2'], 'L1_ffn_b2': _L1_ffn_in['b2'], 'L1_ffn_g2': _L1_ffn_in['g2'], 'L1_ffn_be2': _L1_ffn_in['be2'], 'L1_ffn_m2': _L1_ffn_in['m2'], 'L1_ffn_v2': _L1_ffn_in['v2'], 'L1_ffn_Wo': _L1_ffn_in['Wo'], 'L1_ffn_bo': _L1_ffn_in['bo']}

def reference(x, src, dst, edge_weight, node_vec, L0_gnn_W, L0_gnn_a_src, L0_gnn_a_dst, L0_ffn_W_fx, L0_ffn_b_fx, L0_ffn_W_x, L0_ffn_b_x, L0_ffn_W_slice, L0_ffn_b_slice, L0_ffn_W_q, L0_ffn_W_k, L0_ffn_W_v, L0_ffn_W_out, L0_ffn_b_out, L0_ffn_temperature, L1_gnn_gat_w, L1_gnn_gat_a_src, L1_gnn_gat_a_tgt, L1_gnn_gat_b, L1_gnn_ln_local_g, L1_gnn_ln_local_b, L1_gnn_ln_global_g, L1_gnn_ln_global_b, L1_gnn_ln2_g, L1_gnn_ln2_b, L1_gnn_in_proj_w, L1_gnn_conv_w, L1_gnn_conv_b, L1_gnn_x_proj_w, L1_gnn_dt_proj_w, L1_gnn_dt_proj_b, L1_gnn_A_log, L1_gnn_D_param, L1_gnn_out_proj_w, L1_gnn_wl, L1_gnn_wg, L1_gnn_ff1_w, L1_gnn_ff1_b, L1_gnn_ff2_w, L1_gnn_ff2_b, L1_ffn_Wr, L1_ffn_br, L1_ffn_W1, L1_ffn_b1, L1_ffn_g1, L1_ffn_be1, L1_ffn_m1, L1_ffn_v1, L1_ffn_W2, L1_ffn_b2, L1_ffn_g2, L1_ffn_be2, L1_ffn_m2, L1_ffn_v2, L1_ffn_Wo, L1_ffn_bo):
    import jax
    import jax.numpy as jnp

    def _L0_gnn_ref(h, edge_index, W, a_src, a_dst):
        import jax, jax.numpy as jnp
        import numpy as np
        N = 50000
        E = 25000
        IN = 256
        HD = 4
        D = 64
        n = h.shape[0]
        src, dst = (edge_index[0], edge_index[1])
        hp = (h @ W).reshape(n, HD, D)
        e_src = jnp.einsum('ehd,hd->eh', hp[src], a_src)
        e_dst = jnp.einsum('ehd,hd->eh', hp[dst], a_dst)
        e = jax.nn.leaky_relu(e_src + e_dst, negative_slope=0.2)
        e_max = jax.ops.segment_max(e, dst, num_segments=n)
        ex = jnp.exp(e - e_max[dst])
        e_sum = jax.ops.segment_sum(ex, dst, num_segments=n)
        alpha = ex / (e_sum[dst] + 1e-16)
        msg = hp[src] * alpha[..., None]
        out = jax.ops.segment_sum(msg, dst, num_segments=n)
        return out.reshape(n, HD * D)

    def _L0_ffn_ref(x, W_fx, b_fx, W_x, b_x, W_slice, b_slice, W_q, W_k, W_v, W_out, b_out, temperature):
        import jax, jax.numpy as jnp
        import numpy as np
        DIM = 256
        H = 8
        D = 64
        G = 64
        INNER = H * D
        SCALE = D ** (-0.5)
        B, N, _ = x.shape
        fx_mid = (x @ W_fx + b_fx).reshape(B, N, H, D).transpose(0, 2, 1, 3)
        x_mid = (x @ W_x + b_x).reshape(B, N, H, D).transpose(0, 2, 1, 3)
        temp = jnp.clip(temperature, 0.1, 5.0)
        slice_weights = jax.nn.softmax((x_mid @ W_slice + b_slice) / temp, axis=-1)
        slice_norm = slice_weights.sum(axis=2)
        slice_token = jnp.einsum('bhnc,bhng->bhgc', fx_mid, slice_weights)
        slice_token = slice_token / (slice_norm[..., None] + 1e-05)
        q = slice_token @ W_q
        k = slice_token @ W_k
        v = slice_token @ W_v
        attn = jax.nn.softmax(jnp.einsum('bhgc,bhkc->bhgk', q, k) * SCALE, axis=-1)
        out_slice = jnp.einsum('bhgk,bhkc->bhgc', attn, v)
        out_x = jnp.einsum('bhgc,bhng->bhnc', out_slice, slice_weights)
        out_x = out_x.transpose(0, 2, 1, 3).reshape(B, N, INNER)
        return out_x @ W_out + b_out

    def _L1_gnn_ref(x, edge_index, edge_prob, deg_noise, gat_w, gat_a_src, gat_a_tgt, gat_b, ln_local_g, ln_local_b, ln_global_g, ln_global_b, ln2_g, ln2_b, in_proj_w, conv_w, conv_b, x_proj_w, dt_proj_w, dt_proj_b, A_log, D_param, out_proj_w, wl, wg, ff1_w, ff1_b, ff2_w, ff2_b):
        import jax, jax.numpy as jnp
        import numpy as np
        from jax import lax
        N, E, D = (256, 8192, 256)
        NH, FOUT = (4, 64)
        D_STATE, D_CONV, DT_RANK = (16, 4, 16)

        def _layer_norm(x, g, b, eps=1e-05):
            mu = jnp.mean(x, -1, keepdims=True)
            var = jnp.var(x, -1, keepdims=True)
            return (x - mu) * lax.rsqrt(var + eps) * g + b

        def _mamba(xs, in_proj_w, conv_w, conv_b, x_proj_w, dt_proj_w, dt_proj_b, A_log, D_param, out_proj_w):
            n = xs.shape[0]
            xz = xs @ in_proj_w.T
            xc, z = jnp.split(xz, 2, axis=-1)
            K = conv_w.shape[1]
            xp = jnp.pad(xc, ((K - 1, 0), (0, 0)))
            xc = sum((xp[k:k + n] * conv_w[:, k] for k in range(K))) + conv_b
            xc = jax.nn.silu(xc)
            dbc = xc @ x_proj_w.T
            dt = jax.nn.softplus(dbc[:, :DT_RANK] @ dt_proj_w.T + dt_proj_b)
            Bm = dbc[:, DT_RANK:DT_RANK + D_STATE]
            Cm = dbc[:, DT_RANK + D_STATE:]
            A = -jnp.exp(A_log)
            dA = jnp.exp(dt[:, :, None] * A)
            dBx = (dt * xc)[:, :, None] * Bm[:, None, :]

            def step(h, t):
                dA_t, dBx_t, C_t = t
                h = dA_t * h + dBx_t
                return (h, h @ C_t)
            _, y = lax.scan(step, jnp.zeros((xc.shape[1], D_STATE), xs.dtype), (dA, dBx, Cm))
            y = y + xc * D_param
            y = y * jax.nn.silu(z)
            return y @ out_proj_w.T

        def _forward(x, edge_index, deg_noise, gat_w, gat_a_src, gat_a_tgt, gat_b, ln_local_g, ln_local_b, ln_global_g, ln_global_b, ln2_g, ln2_b, in_proj_w, conv_w, conv_b, x_proj_w, dt_proj_w, dt_proj_b, A_log, D_param, out_proj_w, wl, wg, ff1_w, ff1_b, ff2_w, ff2_b):
            n = x.shape[0]
            src, tgt = (edge_index[0], edge_index[1])
            proj = (x @ gat_w.T).reshape(n, NH, FOUT)
            s_src = jnp.sum(proj * gat_a_src, -1)
            s_tgt = jnp.sum(proj * gat_a_tgt, -1)
            e = jax.nn.leaky_relu(s_src[src] + s_tgt[tgt], 0.2)
            exp_e = jnp.exp(e - jnp.max(e))
            denom = jax.ops.segment_sum(exp_e, tgt, num_segments=n)
            attn = exp_e / (denom[tgt] + 1e-16)
            agg = jax.ops.segment_sum(proj[src] * attn[:, :, None], tgt, num_segments=n)
            h_local = jax.nn.elu((agg + x.reshape(n, NH, FOUT)).reshape(n, NH * FOUT) + gat_b)
            h_local = _layer_norm(h_local, ln_local_g, ln_local_b)
            deg = jax.ops.segment_sum(jnp.ones((src.shape[0],), x.dtype), src, num_segments=n)
            perm = jnp.argsort(deg + deg_noise, stable=True)
            inv = jnp.argsort(perm)
            y = _mamba(x[perm], in_proj_w, conv_w, conv_b, x_proj_w, dt_proj_w, dt_proj_b, A_log, D_param, out_proj_w)
            h_attn = _layer_norm(x + y[inv], ln_global_g, ln_global_b)
            gate = jax.nn.sigmoid(h_local @ wl.T + h_attn @ wg.T)
            h = gate * h_local + (1.0 - gate) * h_attn
            ff = jax.nn.relu(h @ ff1_w.T + ff1_b) @ ff2_w.T + ff2_b
            return _layer_norm(h + ff, ln2_g, ln2_b)
        return _forward(x, edge_index, deg_noise, gat_w, gat_a_src, gat_a_tgt, gat_b, ln_local_g, ln_local_b, ln_global_g, ln_global_b, ln2_g, ln2_b, in_proj_w, conv_w, conv_b, x_proj_w, dt_proj_w, dt_proj_b, A_log, D_param, out_proj_w, wl, wg, ff1_w, ff1_b, ff2_w, ff2_b)

    def _L1_ffn_ref(x, Wr, br, W1, b1, g1, be1, m1, v1, W2, b2, g2, be2, m2, v2, Wo, bo):
        import jax, jax.numpy as jnp
        import numpy as np
        BN_EPS = 0.001

        def _bn(h, g, b, m, v):
            return g * (h - m) * jax.lax.rsqrt(v + BN_EPS) + b
        feat = jnp.mean(x, axis=0)
        w = jax.nn.softmax(feat @ Wr + br, axis=-1)
        h = jnp.einsum('bfd,edh->bfeh', x, W1) + b1
        h = jax.nn.relu(_bn(h, g1, be1, m1, v1))
        h = jnp.einsum('bfeh,ehk->bfek', h, W2) + b2
        h = jax.nn.relu(_bn(h, g2, be2, m2, v2))
        y = jnp.einsum('bfeh,ehd->bfed', h, Wo) + bo
        return jnp.einsum('bfed,fe->bfd', y, w)
    edge_index = jnp.stack([src, dst])
    x = x + _L0_gnn_ref(_layernorm(x, axis=-1), edge_index, L0_gnn_W, L0_gnn_a_src, L0_gnn_a_dst)
    x = x + _L0_ffn_ref(_layernorm(x, axis=-1)[None], L0_ffn_W_fx, L0_ffn_b_fx, L0_ffn_W_x, L0_ffn_b_x, L0_ffn_W_slice, L0_ffn_b_slice, L0_ffn_W_q, L0_ffn_W_k, L0_ffn_W_v, L0_ffn_W_out, L0_ffn_b_out, L0_ffn_temperature)[0]
    x = x + _L1_gnn_ref(_layernorm(x, axis=-1), edge_index, edge_weight, node_vec, L1_gnn_gat_w, L1_gnn_gat_a_src, L1_gnn_gat_a_tgt, L1_gnn_gat_b, L1_gnn_ln_local_g, L1_gnn_ln_local_b, L1_gnn_ln_global_g, L1_gnn_ln_global_b, L1_gnn_ln2_g, L1_gnn_ln2_b, L1_gnn_in_proj_w, L1_gnn_conv_w, L1_gnn_conv_b, L1_gnn_x_proj_w, L1_gnn_dt_proj_w, L1_gnn_dt_proj_b, L1_gnn_A_log, L1_gnn_D_param, L1_gnn_out_proj_w, L1_gnn_wl, L1_gnn_wg, L1_gnn_ff1_w, L1_gnn_ff1_b, L1_gnn_ff2_w, L1_gnn_ff2_b)
    x = x + _L1_ffn_ref(_layernorm(x, axis=-1)[None], L1_ffn_Wr, L1_ffn_br, L1_ffn_W1, L1_ffn_b1, L1_ffn_g1, L1_ffn_be1, L1_ffn_m1, L1_ffn_v1, L1_ffn_W2, L1_ffn_b2, L1_ffn_g2, L1_ffn_be2, L1_ffn_m2, L1_ffn_v2, L1_ffn_Wo, L1_ffn_bo)[0]
    return x

_drawn_inputs = setup_inputs


def setup_inputs(seed=0):
    import zlib

    import numpy as np

    out = dict(_drawn_inputs(seed))
    spreads = {'L0_ffn_b_fx': (0.0, 0.1),
     'L0_ffn_b_x': (0.0, 0.8),
     'L0_ffn_b_slice': (0.0, 0.8),
     'L0_ffn_b_out': (0.0, 0.1),
     'L0_ffn_temperature': (0.5, 0.6),
     'L1_gnn_gat_b': (0.0, 0.287),
     'L1_gnn_ln_local_g': (1.0, 0.2),
     'L1_gnn_ln_local_b': (0.0, 0.278),
     'L1_gnn_ln_global_g': (1.0, 0.2),
     'L1_gnn_ln_global_b': (0.0, 0.314),
     'L1_gnn_ln2_g': (1.0, 0.2),
     'L1_gnn_ln2_b': (0.0, 0.1),
     'L1_gnn_conv_b': (0.0, 0.8),
     'L1_gnn_D_param': (1.0, 0.6),
     'L1_gnn_ff1_b': (0.0, 0.1),
     'L1_gnn_ff2_b': (0.0, 0.1),
     'L1_ffn_br': (0.0, 0.8),
     'L1_ffn_b1': (0.0, 0.604),
     'L1_ffn_g1': (1.0, 0.6),
     'L1_ffn_be1': (0.0, 0.644),
     'L1_ffn_m1': (0.0, 0.604),
     'L1_ffn_v1': (1.0, 0.6),
     'L1_ffn_b2': (0.0, 0.442),
     'L1_ffn_g2': (1.0, 0.6),
     'L1_ffn_be2': (0.0, 0.484),
     'L1_ffn_m2': (0.0, 0.44),
     'L1_ffn_v2': (1.0, 0.6),
     'L1_ffn_bo': (0.0, 0.336)}
    factors = {'node_vec': 3.563,
     'L0_ffn_W_x': 8.0,
     'L0_ffn_W_slice': 8.0,
     'L0_ffn_W_q': 8.0,
     'L0_ffn_W_k': 8.0,
     'L1_gnn_gat_a_src': 3.567,
     'L1_gnn_gat_a_tgt': 8.0,
     'L1_gnn_in_proj_w': 2.937,
     'L1_gnn_conv_w': 3.113,
     'L1_gnn_x_proj_w': 8.0,
     'L1_gnn_dt_proj_w': 8.0,
     'L1_gnn_dt_proj_b': 8.0,
     'L1_gnn_A_log': 8.0,
     'L1_gnn_out_proj_w': 2.919}
    for name, (base, spread) in spreads.items():
        noise = np.random.default_rng([zlib.crc32(name.encode()), seed]).standard_normal(out[name].shape)
        drawn = base * np.exp(spread * noise) if base else spread * noise
        out[name] = jnp.asarray(drawn.astype(out[name].dtype))
    for name, factor in factors.items():
        out[name] = (out[name] * factor).astype(out[name].dtype)
    return out
```

```python
from contextlib import ExitStack, contextmanager

import concourse.bass as bass
from concourse import mybir

P = 128
NODES, DIM = 3125, 256
EDGES = 53125
TILES = -(-NODES // P)
ROWS = TILES * P
STREAM = -(-EDGES // (P * 16)) * 16
HEADS, HD = 4, 64
HSUM = HEADS * (HD + 1)
HROW = HSUM + HEADS
GROUP = 8
RING = 4
GROUPS = STREAM // GROUP
CHUNK = 400
CHUNKS = ROWS // CHUNK
KT = DIM // P
SH, SD = 8, 64
SLICES = SH * SD
TAPS, RANK, STATES, SPANS = 4, 16, 16, 2
EXPERTS = 8
BIG = 1.0e30
FAR = 200000.0

ALU = mybir.AluOpType
ACT = mybir.ActivationFunctionType
F32 = mybir.dt.float32
BF16 = mybir.dt.bfloat16
I32 = mybir.dt.int32
AX_X = mybir.AxisListType.X
RMAX = bass.bass_isa.ReduceOp.max
ds = bass.ds


class Steps:

    def __init__(self, eng, sem, passed):
        self.per, self.looping = 0, False
        self.eng, self.sem, self.passed, self.base, self.n, self.offset = eng, sem, passed, 0, 0, 0

    def turn(self, t, per):
        if not self.looping:
            self.base, self.looping = self.base + self.n, True
        self.offset, self.n, self.per = t * per, 0, per

    def end_turn(self):
        assert self.n == self.per, (self.n, self.per)

    def end_loop(self, turns):
        self.base, self.offset, self.n, self.looping = self.base + turns * self.per, 0, 0, False

    def did(self, ins):
        ins.then_inc(self.sem, 1)
        self.n += 1

    def wait(self):
        self.eng.wait_ge(self.sem, self.offset + (self.base + self.n))

    def __call__(self, ins):
        self.did(ins)
        self.wait()

    def hold_last(self):
        hold(self.eng, self.passed, self.sem, self.offset + (self.base + self.n))

    def hold(self, ins):
        self.did(ins)
        hold(self.eng, self.passed, self.sem, self.offset + (self.base + self.n))


def hold(eng, passed, sem, value):
    eng.wait_ge(sem, value)
    eng.sem_inc(passed, 1)


def each_tile(eng, body):
    body(0, 0, True)
    body(1, 1, True)
    with eng.Fori(1, TILES // 2) as i:
        body(i * 2, 0, False)
        body(i * 2 + 1, 1, False)
    if TILES % 2:
        body(TILES - 1, 0, False)


def each_group(eng, groups, body):
    body(0, 0, True)
    body(1, 1, True)
    with eng.Fori(1, groups // 2) as i:
        body(i * 2, 0, False)
        body(i * 2 + 1, 1, False)


class Lasting:

    def __init__(self, sem):
        self.sem, self.base = sem, 0


class Stage:

    def __init__(self, nc, ctx, name, passed, shared=None):
        self.nc, self.ctx, self.name, self.passed, self.sems, self.shared = nc, ctx, name, passed, [], shared

    @contextmanager
    def block(self):
        if self.shared is not None:
            yield self.shared
        else:
            with self.nc.Block() as block:
                yield block

    def sb(self, name, shape, dt=F32):
        return self.ctx.enter_context(self.nc.sbuf_tensor(f"{self.name}_{name}", shape, dt))

    def ps(self, name, shape, dt=F32):
        return self.ctx.enter_context(self.nc.psum_tensor(f"{self.name}_{name}", shape, dt))

    def sem(self, name):
        sem = self.ctx.enter_context(self.nc.semaphore(f"{self.name}_{name}"))
        self.sems.append(sem)
        return sem

    def end(self):
        for sem in self.sems:
            self.nc.gpsimd.sem_clear(sem)
        self.nc.all_engine_barrier()

    def steps(self, eng, sem):
        return Steps(eng, sem, self.passed)


def constants_stage(nc, st, C, G, X, x, src, dst):
    load, made = st.sem("load"), st.sem("made")
    with st.block() as block:
        @block.sync
        def _(sp):
            sp.dma_start(X[:], x.rearrange("(t p) d -> p t d", p=P)).then_inc(load, 16)
            sp.dma_start(C["src_idx"][:], src).then_inc(load, 16)
            sp.dma_start(C["dst_idx"][:], dst).then_inc(load, 16)
            sp.dma_start(C["tile_start"][:], G["tile_starts"].rearrange("a t -> (a t)").partition_broadcast(P)).then_inc(load, 16)
            sp.wait_ge(load, 64)

        @block.gpsimd
        def _(pool):
            step = st.steps(pool, made)
            pool.memset(C["ones"][:], 1.0)
            pool.memset(C["eps5"][:], 1.0e-5)
            step(pool.memset(C["ident"][:], 0.0))
            step(pool.affine_select(out=C["ident"][:], in_=C["ident"][:], compare_op=ALU.not_equal, fill=1.0,
                                    base=0, pattern=[[-1, P]], channel_multiplier=1))
            step(pool.affine_select(out=C["above"][:], in_=C["ones"][:], compare_op=ALU.is_gt, fill=0.0,
                                    base=0, pattern=[[1, P]], channel_multiplier=-1))
            step(pool.affine_select(out=C["below"][:], in_=C["ones"][:], compare_op=ALU.is_gt, fill=0.0,
                                    base=0, pattern=[[-1, P]], channel_multiplier=1))


def norm_stage(nc, st, C, src, XN=None, XT=None, gain=None, shift=None, BANKS=4, after=None, rows_ready=None, ready=None):
    SLOTS, SPAN = 4, 2
    raw, mv = st.sb("raw", [P, TILES, 6]), st.sb("mv", [P, TILES, 2])
    rstd, std = st.sb("rstd", [P, TILES]), st.sb("std", [P, TILES])
    rows = XN if XN is not None else st.sb("rows", [P, SLOTS, DIM])
    slot_of = lambda t: t if XN is not None else t % SLOTS
    affine = gain is not None
    assert not (affine and XN is not None and XT is not None)
    if affine:
        extent = [P, DIM] if XN is not None else [P, KT]
        gain_row, shift_row = st.sb("gain_row", extent), st.sb("shift_row", extent)
    pt = [st.ps(f"pt{i}", [P, KT, SPAN, P]) for i in range(BANKS)] if XT is not None else None
    chain, stats, means, std_ok, loads, normed, turned, copied = (st.sem(n) for n in (
        "chain", "stats", "means", "std_ok", "loads", "normed", "turned", "copied"))
    spans = [(t, min(SPAN, TILES - t)) for t in range(0, TILES, SPAN)]
    with st.block() as block:
        @block.sync
        def _(sp):
            if affine:
                sp.dma_start(gain_row[:], gain.partition_broadcast(P) if XN is not None else gain).then_inc(loads, 16)
                sp.dma_start(shift_row[:], shift.partition_broadcast(P) if XN is not None else shift).then_inc(loads, 16)
                sp.wait_ge(loads, 32)

        @block.vector
        def _(v):
            step = st.steps(v, chain)
            if after is not None:
                v.wait_ge(*after)
            for t in range(TILES):
                v.bn_stats(raw[:, t, :], src[:, t, :]).then_inc(stats, 1)
            for t in range(TILES):
                v.wait_ge(stats, t + 1)
                v.bn_aggr(mv[:, t, :], raw[:, t, :]).then_inc(means, 1)
            v.wait_ge(std_ok, 1)
            step(v.reciprocal(rstd[:], std[:]))
            for t in range(TILES):
                if XN is None and t >= SLOTS:
                    v.wait_ge(turned, t - SLOTS + 1)
                v.tensor_scalar(rows[:, slot_of(t), :], src[:, t, :], mv[:, t, 0:1], rstd[:, t:t + 1], ALU.subtract, ALU.mult).then_inc(normed, 1)
            if rows_ready is not None:
                v.wait_ge(normed, TILES)
                v.sem_inc(rows_ready, 1)
            if affine and XN is not None:
                v.wait_ge(loads, 32)
                v.wait_ge(normed, TILES)
                step(v.tensor_tensor(XN[:], XN[:], gain_row[:].unsqueeze(1).to_broadcast([P, TILES, DIM]), ALU.mult))
                step(v.tensor_tensor(XN[:], XN[:], shift_row[:].unsqueeze(1).to_broadcast([P, TILES, DIM]), ALU.add))

        @block.scalar
        def _(act):
            act.wait_ge(means, TILES)
            act.activation(std[:], mv[:, :, 1], ACT.Sqrt, bias=C["eps5"][:]).then_inc(std_ok, 1)
            if XT is None:
                return
            if affine:
                act.wait_ge(loads, 32)
            for n, (t, tiles) in enumerate(spans):
                act.wait_ge(turned, t + tiles)
                bank, cols = pt[n % BANKS], slice(t * P, (t + tiles) * P)
                if affine:
                    for k in range(KT):
                        ins = act.activation(XT[:, k, cols], bank[:, k, 0:tiles, :].rearrange("p s n -> p (s n)"), ACT.Identity,
                                             scale=gain_row[:, k:k + 1], bias=shift_row[:, k:k + 1])
                else:
                    ins = act.activation(XT[:, :, cols], bank[:, :, 0:tiles, :].rearrange("p k s n -> p k (s n)"), ACT.Copy)
                ins.then_inc(copied, 1)
            if ready is not None:
                act.wait_ge(copied, len(spans))
                act.sem_inc(ready, 1)

        @block.tensor
        def _(pe):
            if XT is None:
                return
            for n, (t0, tiles) in enumerate(spans):
                if n >= BANKS:
                    pe.wait_ge(copied, n - BANKS + 1)
                for i in range(tiles):
                    pe.wait_ge(normed, t0 + i + 1)
                    for k in range(KT):
                        ins = pe.transpose(pt[n % BANKS][:, k, i, :], rows[:, slot_of(t0 + i), k * P:(k + 1) * P], C["ident"][:])
                    ins.then_inc(turned, 1)


def turn_stage(nc, st, C, XT, rows_out, done):
    BANKS, SPAN = 4, 2
    pt = [st.ps(f"pt{i}", [P, SPAN, KT, P]) for i in range(BANKS)]
    turned = st.sem("turned")
    spans = [(t, min(SPAN, TILES - t)) for t in range(0, TILES, SPAN)]
    with st.block() as block:
        @block.tensor
        def _(pe):
            for n, (t0, tiles) in enumerate(spans):
                if n >= BANKS:
                    pe.wait_ge(done, n - BANKS + 1)
                for i in range(tiles):
                    for k in range(KT):
                        ins = pe.transpose(pt[n % BANKS][:, i, k, :], XT[:, k, (t0 + i) * P:(t0 + i + 1) * P], C["ident"][:])
                ins.then_inc(turned, 1)

        @block.scalar
        def _(act):
            for n, (t0, tiles) in enumerate(spans):
                act.wait_ge(turned, n + 1)
                act.activation(rows_out[:, t0:t0 + tiles, :], pt[n % BANKS][:, 0:tiles].rearrange("p s k n -> p s (k n)"), ACT.Copy).then_inc(done, 1)


def graph_stage(nc, st, C, D, G, node_vec, known):
    lo = {k: st.sb(f"{k}_lo", [P, STREAM], I32) for k in ("src", "dst")}
    hi = {k: st.sb(f"{k}_hi", [P, STREAM], I32) for k in ("src", "dst")}
    lo16 = {k: st.sb(f"{k}_lo16", [P, STREAM], BF16) for k in ("src", "dst")}
    hi16 = {k: st.sb(f"{k}_hi16", [P, STREAM], BF16) for k in ("src", "dst")}
    iota16 = st.sb("iota16", [P, P], BF16)
    iota32 = st.sb("iota32", [P, P], I32)
    hot_lo = {k: st.sb(f"{k}_hot_lo", [P, 2, GROUP, P], BF16) for k in ("src", "dst")}
    hot_hi = {k: st.sb(f"{k}_hot_hi", [P, 2, GROUP, TILES], BF16) for k in ("src", "dst")}
    zero16 = st.sb("zero16", [P, P], BF16)
    hist_ps = {k: st.ps(f"{k}_hist_ps", [TILES, P]) for k in ("src", "dst")}
    tab = st.sb("tab", [TILES, 4, P])
    count = st.sb("count", [TILES, P])
    cum = st.sb("cum", [TILES, P])
    none = st.sb("none", [TILES, P])
    off = st.sb("off", [TILES, 1])
    noise = st.sb("noise", [TILES, P])
    small_ps = st.ps("small_ps", [P, 512])
    off_ps, tab_ps, row_ps = small_ps[0:TILES, 0:1], small_ps[:, 128:256].rearrange("p (a t) -> p a t", a=4), small_ps[:, 256:512].rearrange("p (a n) -> p a n", a=2)
    tabT = st.sb("tabT", [P, 4, TILES])
    dst_next = st.sb("dst_next", [P, 2], I32)
    edge3 = st.sb("edge3", [P, 3])
    spread = st.sb("spread", [P, 2, P])
    gt = st.sb("gt", [P, P])
    key_row = st.sb("key_row", [P, ROWS])
    junk = st.sb("junk", [P, ROWS])
    part = st.sb("part", [P, 3, TILES])
    rank = st.sb("rank", [P, TILES])
    loads, chain, setup, hots, used, counted = (st.sem(n) for n in ("loads", "chain", "setup", "hots", "used", "counted"))
    pe_done, keys, stored, back, iotas = (st.sem(n) for n in ("pe_done", "keys", "stored", "back", "iotas"))
    dve_done = st.sem("dve_done")
    with st.block() as block:
        @block.sync
        def _(sp):
            sp.dma_start(noise[:], node_vec.rearrange("(t p) -> t p", p=P)).then_inc(loads, 16)
            sp.dma_start(dst_next[0:P - 1, :], G["dst"][1:P, 0:2]).then_inc(loads, 16)
            sp.dma_start(dst_next[P - 1:P, :], G["minus_one"]).then_inc(loads, 16)
            sp.wait_ge(keys, 1)
            sp.dma_start(D["key"].rearrange("(t p) -> t p", p=P), tab[:, 3, :]).then_inc(stored, 16)
            sp.wait_ge(stored, 16)
            sp.dma_start(key_row[:], D["key"].partition_broadcast(P)).then_inc(back, 16)
            sp.wait_ge(back, 16)

        @block.gpsimd
        def _(pool):
            pool.iota(iota32[:], [[1, P]], base=0, channel_multiplier=0).then_inc(iotas, 1)
            pool.wait_ge(dve_done, 1)
            pool.affine_select(out=tab[:, 3, :], in_=tab[:, 3, :], compare_op=ALU.is_ge, fill=3.0e38,
                               base=NODES - 1, pattern=[[-1, P]], channel_multiplier=-P).then_inc(keys, 1)

        @block.vector
        def _(v):
            step = st.steps(v, chain)
            v.memset(zero16[:], 0.0).then_inc(setup, 1)
            for k in ("src", "dst"):
                v.tensor_scalar(lo[k][:], C[f"{k}_idx"][:], P - 1, None, ALU.bitwise_and)
                step(v.tensor_scalar(hi[k][:], C[f"{k}_idx"][:], 7, None, ALU.logical_shift_right))
                v.tensor_copy(hi16[k][:], hi[k][:])
                step(v.tensor_copy(lo16[k][:], lo[k][:]))
            v.wait_ge(iotas, 1)
            step(v.tensor_copy(iota16[:], iota32[:]))

            def one_hots(g, slot, first):
                if not first:
                    hold(v, st.passed, used, g - 1)
                for k in ("src", "dst"):
                    v.tensor_tensor(hot_lo[k][:, slot], lo16[k][:, ds(g * GROUP, GROUP)].unsqueeze(2).to_broadcast([P, GROUP, P]),
                                    iota16[:].unsqueeze(1).to_broadcast([P, GROUP, P]), ALU.is_equal).then_inc(hots, 1)
                    v.tensor_tensor(hot_hi[k][:, slot], hi16[k][:, ds(g * GROUP, GROUP)].unsqueeze(2).to_broadcast([P, GROUP, TILES]),
                                    iota16[:, 0:TILES].unsqueeze(1).to_broadcast([P, GROUP, TILES]), ALU.is_equal).then_inc(hots, 1)
            each_group(v, GROUPS, one_hots)
            for name, a, b in (("same_prev", 0, 1), ("same_next", 1, 0)):
                step(v.memset(C[name][:], 0.0))
                step(v.tensor_tensor(C[name][:, b:b + STREAM - 1], C["dst_idx"][:, 1:STREAM], C["dst_idx"][:, 0:STREAM - 1], ALU.is_equal))
            for name, cost, at in (("same_prev", "cut_prev", 0), ("same_next", "cut_next", STREAM - 1)):
                step(v.tensor_scalar(C[cost][:], C[name][:], 1.0, BIG, ALU.subtract, ALU.mult))
                step(v.memset(C[cost][:, at:at + 1], 0.0))
            v.wait_ge(loads, 48)
            v.tensor_copy(edge3[:, 0:1], C["dst_idx"][:, 0:1])
            v.tensor_copy(edge3[:, 1:2], C["dst_idx"][:, STREAM - 1:STREAM])
            step(v.tensor_copy(edge3[:, 2:3], dst_next[:, 0:1]))
            step(v.tensor_tensor(C["ends_in"][:], edge3[:, 2:3], edge3[:, 0:1], ALU.not_equal))
            step(v.tensor_copy(C["dst_first"][:], edge3[:, 0:1]))
            for a in range(2):
                step(v.tensor_scalar(spread[:, a, :], C["ones"][:], edge3[:, a:a + 1], None, ALU.mult))
            v.sem_inc(setup, 1)
            v.wait_ge(counted, 1)
            v.tensor_copy(count[:], hist_ps["dst"][:])
            step(v.tensor_copy(tab[:, 3, :], hist_ps["src"][:]))
            step(v.tensor_tensor(tab[:, 3, :], tab[:, 3, :], noise[:], ALU.add))
            v.sem_inc(dve_done, 1)
            step(v.tensor_tensor_scan(cum[:], C["ones"][0:TILES, :], count[:], 0.0, ALU.mult, ALU.add))
            v.sem_inc(setup, 1)
            v.wait_ge(pe_done, 1)
            step(v.tensor_copy(off[:], off_ps[:]))
            step(v.tensor_scalar(cum[:], cum[:], off[:], None, ALU.add))
            step(v.tensor_scalar(tab[:, 0, :], cum[:], 1.0, 0.0, ALU.subtract, ALU.max))
            step(v.tensor_tensor(tab[:, 1, :], cum[:], count[:], ALU.subtract))
            step(v.tensor_scalar(none[:], count[:], 0.0, FAR, ALU.is_equal, ALU.mult))
            step(v.tensor_tensor(tab[:, 1, :], tab[:, 1, :], none[:], ALU.add))
            step(v.tensor_scalar(tab[:, 2, :], count[:], 0.0, None, ALU.is_gt))
            v.sem_inc(setup, 1)
            v.wait_ge(pe_done, 2)
            step(v.tensor_copy(tabT[:], tab_ps[:, :, 0:TILES]))
            v.tensor_copy(C["last_edge"][:], tabT[:, 0, :])
            v.tensor_copy(C["first_edge"][:], tabT[:, 1, :]).then_inc(known, 1)
            v.tensor_copy(C["has_edge"][:], tabT[:, 2, :])
            step(v.scalar_tensor_tensor(C["carry"][:], row_ps[:, 0, :], edge3[:, 1:2], C["above"][:], ALU.is_equal, ALU.mult))
            step(v.tensor_scalar(C["not_after"][:], C["carry"][:], 1.0, BIG, ALU.subtract, ALU.mult))
            step(v.scalar_tensor_tensor(gt[:], row_ps[:, 1, :], edge3[:, 0:1], C["below"][:], ALU.is_equal, ALU.mult))
            step(v.tensor_scalar(C["not_before"][:], gt[:], 1.0, BIG, ALU.subtract, ALU.mult))
            v.wait_ge(back, 16)
            step(v.memset(part[:, 0, 0:1], 0.0))
            for i in range(TILES):
                own = tabT[:, 3, i:i + 1]
                if i:
                    step(v.tensor_scalar(junk[:, 0:i * P], key_row[:, 0:i * P], own, None, ALU.is_le, ALU.add, accum_out=part[:, 0, i:i + 1]))
                step(v.tensor_scalar(junk[:, i * P:ROWS], key_row[:, i * P:ROWS], own, None, ALU.is_lt, ALU.add, accum_out=part[:, 1, i:i + 1]))
                step(v.scalar_tensor_tensor(gt[:], key_row[:, i * P:(i + 1) * P], own, C["below"][:], ALU.is_equal, ALU.mult, accum_out=part[:, 2, i:i + 1]))
            step(v.tensor_tensor(rank[:], part[:, 0, :], part[:, 1, :], ALU.add))
            step(v.tensor_tensor(rank[:], rank[:], part[:, 2, :], ALU.add))
            step(v.tensor_copy(C["rank"][:], rank[:]))

        @block.tensor
        def _(pe):
            pe.wait_ge(setup, 1)
            for k in ("src", "dst"):
                pe.matmul(hist_ps[k][:], zero16[:, 0:TILES], zero16[:], start=True, stop=False, skip_group_check=True)

            def add_counts(g, slot, first):
                hold(pe, st.passed, hots, g * 4 + 4)
                for u in range(GROUP):
                    for k in ("src", "dst"):
                        ins = pe.matmul(hist_ps[k][:], hot_hi[k][:, slot, u, :], hot_lo[k][:, slot, u, :], start=False, stop=False, skip_group_check=True)
                ins.then_inc(used, 1)
            each_group(pe, GROUPS, add_counts)
            for k in ("src", "dst"):
                ins = pe.matmul(hist_ps[k][:], zero16[:, 0:TILES], zero16[:], start=False, stop=True, skip_group_check=True)
            ins.then_inc(counted, 1)
            pe.wait_ge(setup, 3)
            pe.matmul(off_ps[:], C["above"][0:TILES, 0:TILES], cum[:, P - 1:P], start=True, stop=True).then_inc(pe_done, 1)
            pe.wait_ge(setup, 4)
            pe.wait_ge(keys, 1)
            for a in range(4):
                pe.transpose(tab_ps[:, a, 0:TILES], tab[:, a, :], C["ident"][0:TILES, 0:TILES])
            for a in range(2):
                ins = pe.matmul(row_ps[:, a, :], spread[:, a, :], C["ident"][:], start=True, stop=True)
            ins.then_inc(pe_done, 1)


def table_stage(nc, st, C, D, XT, W, a_src, a_dst, esd, xt_ready, esd_ready, ed_stored):
    SLOTS, BANKS = 4, 2
    w_raw = st.sb("w_raw", [P, KT, DIM])
    w = st.sb("w", [P, KT, DIM + 2 * HEADS])
    a_row = st.sb("a_row", [P, 2, DIM])
    prod = st.sb("prod", [P, KT, DIM])
    rows = st.sb("rows", [P, SLOTS, HROW])
    pj = [st.ps(f"pj{i}", [P, DIM + 2 * HEADS]) for i in range(BANKS)]
    loads, chain, ready, projected, copied = (st.sem(n) for n in ("loads", "chain", "ready", "projected", "copied"))
    out = [st.sem(f"out{i}") for i in range(SLOTS)]
    with st.block() as block:
        @block.sync
        def _(sp):
            sp.dma_start(w_raw[:], W.rearrange("(k p) n -> p k n", p=P)).then_inc(loads, 16)
            sp.dma_start(a_row[:, 0, :], a_src.rearrange("h d -> (h d)").partition_broadcast(P)).then_inc(loads, 16)
            sp.dma_start(a_row[:, 1, :], a_dst.rearrange("h d -> (h d)").partition_broadcast(P)).then_inc(loads, 16)
            for t in range(TILES):
                sp.wait_ge(copied, t * 3 + 3)
                sp.dma_start(D["table"][t * P:(t + 1) * P, :], rows[:, t % SLOTS, :]).then_inc(out[t % SLOTS], 16)
            sp.dma_start(D["ed"].rearrange("(t p) h -> p t h", p=P), esd[:, :, HEADS:2 * HEADS]).then_inc(ed_stored, 16)
            for slot in range(SLOTS):
                sp.wait_ge(out[slot], 16 * len(range(slot, TILES, SLOTS)))
            sp.wait_ge(ed_stored, 16)

        @block.vector
        def _(v):
            step = st.steps(v, chain)
            step(v.memset(rows[:], 1.0))
            v.wait_ge(loads, 48)
            step(v.tensor_copy(w[:, :, 0:DIM], w_raw[:]))
            for a in range(2):
                step(v.tensor_tensor(prod[:], w_raw[:], a_row[:, a:a + 1, :].to_broadcast([P, KT, DIM]), ALU.mult))
                for k in range(KT):
                    step(v.tensor_reduce(w[:, k, DIM + a * HEADS:DIM + (a + 1) * HEADS],
                                         prod[:, k, :].rearrange("p (h d) -> p h d", h=HEADS), AX_X, ALU.add))
            v.sem_inc(ready, 1)

        @block.scalar
        def _(act):
            act.wait_ge(ready, 1)
            for t in range(TILES):
                act.wait_ge(projected, t + 1)
                if t >= SLOTS:
                    act.wait_ge(out[t % SLOTS], 16 * (t // SLOTS))
                bank, row = pj[t % BANKS], rows[:, t % SLOTS, :]
                act.activation(row[:, HSUM:HROW], bank[:, DIM:DIM + HEADS], ACT.Copy).then_inc(copied, 1)
                act.activation(row[:, 0:HSUM].rearrange("p (h d) -> p h d", h=HEADS)[:, :, 0:HD], bank[:, 0:DIM].rearrange("p (h d) -> p h d", h=HEADS), ACT.Copy).then_inc(copied, 1)
                act.activation(esd[:, t, :], bank[:, DIM:DIM + 2 * HEADS], ACT.Copy).then_inc(copied, 1)
            act.wait_ge(copied, 3 * TILES)
            act.sem_inc(esd_ready, 1)

        @block.tensor
        def _(pe):
            pe.wait_ge(ready, 1)
            pe.wait_ge(xt_ready, 1)
            for t in range(TILES):
                if t >= BANKS:
                    pe.wait_ge(copied, 3 * (t - BANKS + 1))
                for k in range(KT):
                    ins = pe.matmul(pj[t % BANKS][:], XT[:, k, t * P:(t + 1) * P], w[:, k, :], start=(k == 0), stop=(k == KT - 1))
                ins.then_inc(projected, 1)


def scores_stage(nc, st, C, D, esd, ed, known, esd_ready, ed_stored):
    ed_first = st.sb("ed_first", [P, HEADS])
    raw = st.sb("raw", [P, STREAM, HEADS])
    placed, ed_in = C["placed"], C["ed_in"]
    zeroed, loads, chain, first = (st.sem(n) for n in ("zeroed", "loads", "chain", "first"))
    with st.block() as block:
        @block.sync
        def _(sp):
            sp.wait_ge(first, 1)
            sp.dma_start(D["by_edge"].rearrange("(p j) h -> p (j h)", p=P), raw[:].rearrange("p j h -> p (j h)")).then_inc(zeroed, 16)
            sp.wait_ge(placed.sem, placed.base + 16 * TILES)
            sp.dma_start(raw[:].rearrange("p j h -> p (j h)"), D["by_edge"].rearrange("(p j) h -> p (j h)", p=P)).then_inc(loads, 16)
            sp.wait_ge(loads, 16)

        @block.gpsimd
        def _(pool):
            pool.memset(raw[:], 0.0).then_inc(first, 1)
            pool.wait_ge(ed_stored, 16)
            pool.indirect_dma_start(ed_first[:], None, D["ed"], bass.IndirectOffsetOnAxis(C["dst_idx"][:, 0:1], 0)).then_inc(ed_in.sem, 16)
            pool.wait_ge(zeroed, 16)
            pool.wait_ge(esd_ready, 1)
            if known is not None:
                pool.wait_ge(known, 1)
            for t in range(TILES):
                pool.indirect_dma_start(D["by_edge"], bass.IndirectOffsetOnAxis(C["first_edge"][:, t:t + 1], 0),
                                        esd[:, t, HEADS:2 * HEADS], None, bounds_check=P * STREAM - 1, oob_is_err=False).then_inc(placed.sem, 16)

        @block.vector
        def _(v):
            step = st.steps(v, chain)
            v.wait_ge(loads, 16)
            v.wait_ge(ed_in.sem, ed_in.base + 16)
            step(v.tensor_copy(raw[:, 0, :], ed_first[:]))
            for h in range(HEADS):
                step(v.tensor_tensor_scan(ed[:, :, h], C["same_prev"][:], raw[:, :, h], 0.0, ALU.mult, ALU.add))
    placed.base += 16 * TILES
    ed_in.base += 16


def sum_stage(nc, st, C, D, ed):
    got = st.sb("got", [P, RING, GROUP, HROW])
    weighed = st.sb("weighed", [P, 2, GROUP, HSUM])
    run = st.sb("run", [P, 2, GROUP, HROW])
    scaled = st.sb("scaled", [P, HSUM])
    idx = st.sb("idx", [P, RING, GROUP], I32)
    cut = st.sb("cut", [P, 2, GROUP + 2])
    score = st.sb("score", [P, 2, GROUP + 1, HEADS])
    ahead = st.sb("ahead", [P, 2, GROUP + 1, HEADS])
    top = st.sb("top", [P, 2, GROUP + 1, HEADS])
    less = st.sb("less", [P, 2, GROUP + 1, HEADS])
    weight = st.sb("weight", [P, 2, GROUP + 1, HEADS])
    wide = st.sb("wide", [P, HEADS, P])
    masked = st.sb("masked", [P, HEADS, P])
    masked_t = st.sb("masked_t", [P, HEADS, P])
    row_ps = st.ps("row_ps", [P, HEADS, P])
    turn_ps = st.ps("turn_ps", [P, HEADS, P])
    carry_ps = st.ps("carry_ps", [P, HSUM])
    arrived = C["arrived"]
    stored = [st.sem(f"stored{s}") for s in range(2)]
    names = ("staged", "summed", "chain", "adds", "argued", "exped", "weighs", "carried", "crossing", "shifted", "powers")
    staged, summed, chain, adds, argued, exped, weighs, carried, crossing, shifted, powers = (st.sem(n) for n in names)
    sums = D["sums"].rearrange("(p j) n -> p (j n)", p=P)
    with st.block() as block:
        @block.sync
        def _(sp):
            def store(g, slot, first):
                hold(sp, st.passed, summed, g + 1)
                sp.dma_start(sums[:, ds(g * (GROUP * HROW), GROUP * HROW)], run[:, slot].rearrange("p u n -> p (u n)")).then_inc(stored[slot], 16)
            each_group(sp, GROUPS, store)
            for s in range(2):
                sp.wait_ge(stored[s], 16 * (GROUPS // 2))

        @block.gpsimd
        def _(pool):
            def fetch(g, slot):
                hold(pool, st.passed, staged, g + 1)
                for u in range(GROUP):
                    pool.indirect_dma_start(got[:, slot, u, :], None, D["table"], bass.IndirectOffsetOnAxis(idx[:, slot, u:u + 1], 0)).then_inc(arrived[slot][u].sem, 16)
            with pool.Fori(0, GROUPS // RING) as i:
                for slot in range(RING):
                    fetch(i * RING + slot, slot)

        @block.scalar
        def _(act):
            def power(g, slot, first):
                hold(act, st.passed, argued, g + 1)
                act.activation(weight[:, slot], less[:, slot], ACT.Exp).then_inc(exped, 1)
            each_group(act, GROUPS, power)
            act.wait_ge(shifted, 1)
            act.activation(masked[:], masked[:], ACT.Exp).then_inc(powers, 1)

        @block.vector
        def _(v):
            step = st.steps(v, chain)
            add = st.steps(v, adds)
            step(v.memset(run[:, 1, GROUP - 1, :], 0.0))
            step(v.memset(top[:, 1, GROUP, :], -BIG))
            step(v.memset(cut[:], -BIG))

            def stage(g, slot):
                v.tensor_copy(idx[:, slot, :], C["src_idx"][:, ds(g * GROUP, GROUP)]).then_inc(staged, 1)
            for slot in range(RING):
                stage(slot, slot)

            def tops(g, slot):
                s = slot % 2
                return (
                    lambda: v.tensor_copy(cut[:, s, 1:GROUP + 1], C["cut_prev"][:, ds(g * GROUP, GROUP)]),
                    lambda: v.tensor_tensor(score[:, s, 1:, :], got[:, slot, :, HSUM:], ed[:, ds(g * GROUP, GROUP), :], ALU.add),
                    lambda: v.scalar_tensor_tensor(score[:, s, 1:, :], score[:, s, 1:, :], 0.2, score[:, s, 1:, :], ALU.mult, ALU.max),
                    lambda: v.tensor_copy(score[:, s, 0, :], top[:, 1 - s, GROUP, :]),
                    lambda: [v.tensor_tensor_scan(ahead[:, s, :, h], cut[:, s, 0:GROUP + 1], score[:, s, :, h], -BIG, ALU.add, ALU.max) for h in range(HEADS)][-1],
                    lambda: [v.tensor_tensor_scan(top[:, s, ::-1, h], cut[:, s, GROUP + 1:0:-1], ahead[:, s, ::-1, h], -BIG, ALU.add, ALU.max) for h in range(HEADS)][-1],
                    lambda: v.tensor_tensor(less[:, s], score[:, s], top[:, s], ALU.subtract),
                )

            def arrive(i, slot):
                for u in range(GROUP):
                    hold(v, st.passed, arrived[slot][u].sem, i * 16 + (arrived[slot][u].base + 16))

            def weigh(u, slot):
                s = slot % 2
                v.tensor_tensor(weighed[:, s, u, :].rearrange("p (h d) -> p h d", h=HEADS), got[:, slot, u, 0:HSUM].rearrange("p (h d) -> p h d", h=HEADS),
                                weight[:, s, u + 1, :].unsqueeze(2).to_broadcast([P, HEADS, HD + 1]), ALU.mult).then_inc(weighs, 1)

            def group(i, slot, first=False, last=False):
                g, s = i * RING + slot, slot % 2
                find = not (last and slot >= RING - 2)
                weighs_next = not (last and slot == RING - 1)
                then, next_slot = (i + 1, slot - 2) if slot >= 2 else (i, slot + 2)
                if find:
                    step.turn(g + 2, TOPS)
                    pending = list(tops(g + 2, next_slot))
                add.turn(g, GROUP + 2)
                hold(v, st.passed, weighs, g * GROUP + GROUP)
                if not last:
                    stage(g + RING, slot)
                if not (first and slot < 2):
                    hold(v, st.passed, stored[s], i * (16 * RING // 2) + slot // 2 * 16)
                add.did(v.tensor_copy(run[:, s, :, HSUM:], top[:, s, 1:, :]))
                add.did(v.tensor_tensor(scaled[:].rearrange("p (h d) -> p h d", h=HEADS), run[:, 1 - s, GROUP - 1, 0:HSUM].rearrange("p (h d) -> p h d", h=HEADS),
                                        weight[:, s, 0, :].unsqueeze(2).to_broadcast([P, HEADS, HD + 1]), ALU.mult))
                if weighs_next:
                    hold(v, st.passed, exped, g + 2)
                if find:
                    arrive(then, next_slot)
                for u in range(GROUP):
                    if find and u < TOPS:
                        if u:
                            step.wait()
                        step.did(pending[u]())
                    if weighs_next:
                        weigh(u, (slot + 1) % RING)
                    before = run[:, s, u - 1, 0:HSUM] if u else scaled[:]
                    add.hold_last()
                    add.did(v.scalar_tensor_tensor(run[:, s, u, 0:HSUM], before, C["same_prev"][:, ds(g * GROUP + u, 1)], weighed[:, s, u, :], ALU.mult, ALU.add))
                if find:
                    step.wait()
                    step.end_turn()
                    v.sem_inc(argued, 1)
                add.hold_last()
                add.end_turn()
                v.sem_inc(summed, 1)

            TOPS = 7
            for g in range(2):
                step.turn(g, TOPS)
                arrive(0, g)
                for f in tops(g, g):
                    step(f())
                v.sem_inc(argued, 1)
            v.wait_ge(exped, 1)
            for u in range(GROUP):
                weigh(u, 0)
            for slot in range(RING):
                group(0, slot, first=True)
            with v.Fori(1, GROUPS // RING - 1) as i:
                for slot in range(RING):
                    group(i, slot)
            for slot in range(RING):
                group(GROUPS // RING - 1, slot, last=True)
            step.end_loop(GROUPS)
            step(v.tensor_copy(wide[:], top[:, 1, GROUP, :].unsqueeze(2).to_broadcast([P, HEADS, P])))
            v.sem_inc(crossing, 1)
            v.wait_ge(carried, 1)
            mask = C["not_before"][:].unsqueeze(1).to_broadcast([P, HEADS, P])
            step(v.tensor_tensor(masked[:], row_ps[:], mask, ALU.add))
            step(v.tensor_reduce(C["carried"][:, HSUM:HROW], masked[:], AX_X, ALU.max))
            step(v.tensor_tensor(masked[:], masked[:], C["carried"][:, HSUM:HROW].unsqueeze(2).to_broadcast([P, HEADS, P]), ALU.subtract))
            v.sem_inc(shifted, 1)
            v.wait_ge(powers, 1)
            step(v.scalar_tensor_tensor(masked[:], mask, -1.0, masked[:], ALU.is_ge, ALU.mult))
            v.sem_inc(crossing, 1)
            v.wait_ge(carried, 2)
            step(v.tensor_copy(masked_t[:], turn_ps[:]))
            v.sem_inc(crossing, 1)
            v.wait_ge(carried, 3)
            step(v.tensor_copy(C["carried"][:, 0:HSUM], carry_ps[:]))
            step(v.memset(C["carried"][:, HROW:HROW + 1], 1.0))

        @block.tensor
        def _(pe):
            pe.wait_ge(crossing, 1)
            for h in range(HEADS):
                ins = pe.matmul(row_ps[:, h, :], wide[:, h, :], C["ident"][:], start=True, stop=True)
            ins.then_inc(carried, 1)
            pe.wait_ge(crossing, 2)
            for h in range(HEADS):
                ins = pe.transpose(turn_ps[:, h, :], masked[:, h, :], C["ident"][:])
            ins.then_inc(carried, 1)
            pe.wait_ge(crossing, 3)
            pe.wait_ge(summed, GROUPS)
            for h in range(HEADS):
                cells = slice(h * (HD + 1), (h + 1) * (HD + 1))
                ins = pe.matmul(carry_ps[:, cells], masked_t[:, h, :], run[:, 1, GROUP - 1, cells], start=True, stop=True)
            ins.then_inc(carried, 1)
    for s in arrived:
        for u in s:
            u.base += GROUPS // RING * 16


def nodes_stage(nc, st, C, D, out, base, bias, global_top):
    SETS = 5
    numbers = st.sb("numbers", [P, ROWS], I32)
    gate = st.sb("gate", [P, 2, P])
    number = st.sb("number", [P, ROWS])
    got = st.sb("got", [P, TILES, HROW])
    into = st.sb("into", [P, TILES, HROW + 1])
    less = st.sb("less", [P, 2, TILES, HEADS])
    top = st.sb("top", [P, TILES, HEADS])
    den = st.sb("den", [P, TILES, HEADS])
    miss = st.sb("miss", [P, TILES])
    bias_row = st.sb("bias_row", [P, DIM])
    peak, peaks = st.sb("peak", [P, 1]), st.sb("peaks", [P, 1])
    in_ps = [st.ps(f"in_ps{i}", [P, HROW + 1]) for i in range(4)]
    arrived = C["arrived"][0][0]
    names = ("iotas", "loads", "chain", "gated", "crossed", "copied", "lessed", "exped", "topped", "selected")
    iotas, loads, chain, gated, crossed, copied, lessed, exped, topped, selected = (st.sem(n) for n in names)
    with st.block() as block:
        @block.sync
        def _(sp):
            if bias is not None:
                sp.dma_start(bias_row[:], bias.partition_broadcast(P)).then_inc(loads, 16)
                sp.wait_ge(loads, 16)

        @block.gpsimd
        def _(pool):
            pool.iota(numbers[:], [[1, ROWS]], base=0, channel_multiplier=0).then_inc(iotas, 1)
            for t in range(TILES):
                pool.indirect_dma_start(got[:, t, :], None, D["sums"], bass.IndirectOffsetOnAxis(C["last_edge"][:, t:t + 1], 0)).then_inc(arrived.sem, 16)
            if global_top:
                pool.wait_ge(topped, 1)
                pool.affine_select(out=den[:], in_=den[:], compare_op=ALU.is_ge, fill=-BIG, base=NODES - 1,
                                   pattern=[[-P, TILES], [0, HEADS]], channel_multiplier=-1).then_inc(selected, 1)
                pool.wait_ge(topped, 2)
                pool.partition_all_reduce(peaks[:], peak[:], P, RMAX).then_inc(selected, 1)

        @block.vector
        def _(v):
            step = st.steps(v, chain)
            v.wait_ge(iotas, 1)
            step(v.tensor_copy(number[:], numbers[:]))
            for t in range(TILES):
                if t >= 2:
                    v.wait_ge(crossed, t - 1)
                v.tensor_scalar(gate[:, t % 2, :], number[:, t * P:(t + 1) * P], C["dst_first"][:], C["ends_in"][:], ALU.is_equal, ALU.mult).then_inc(gated, 1)
            v.wait_ge(copied, TILES)
            v.wait_ge(arrived.sem, arrived.base + 16 * TILES)
            step(v.tensor_scalar(miss[:], into[:, :, HROW], 1.0, BIG, ALU.subtract, ALU.mult))
            step(v.tensor_tensor(less[:, 0], into[:, :, HSUM:HROW], miss[:].unsqueeze(2).to_broadcast([P, TILES, HEADS]), ALU.add))
            step(v.tensor_tensor(top[:], less[:, 0], got[:, :, HSUM:HROW], ALU.max))
            step(v.tensor_tensor(less[:, 0], less[:, 0], top[:], ALU.subtract))
            step(v.tensor_tensor(less[:, 1], got[:, :, HSUM:HROW], top[:], ALU.subtract))
            v.sem_inc(lessed, 1)
            if global_top:
                step(v.tensor_scalar(miss[:], C["has_edge"][:], 1.0, BIG, ALU.subtract, ALU.mult))
                step(v.tensor_tensor(den[:], top[:], miss[:].unsqueeze(2).to_broadcast([P, TILES, HEADS]), ALU.add))
                v.sem_inc(topped, 1)
                v.wait_ge(selected, 1)
                step(v.tensor_reduce(peak[:], den[:].rearrange("p t h -> p (t h)"), AX_X, ALU.max))
                v.sem_inc(topped, 1)
                v.wait_ge(selected, 2)
                step(v.tensor_scalar(top[:], top[:], -1.0, peaks[:], ALU.mult, ALU.add))
                v.sem_inc(topped, 1)
            v.wait_ge(exped, 1)
            cells = lambda a: a[:, :, 0:HSUM].rearrange("p t (h d) -> p t h d", h=HEADS)
            for a, each in ((0, into), (1, got)):
                v.tensor_tensor(cells(each), cells(each), less[:, a].unsqueeze(3).to_broadcast([P, TILES, HEADS, HD + 1]), ALU.mult).then_inc(chain, 1)
                step.n += 1
            step.wait()
            step(v.tensor_tensor(got[:, :, 0:HSUM], got[:, :, 0:HSUM], into[:, :, 0:HSUM], ALU.add))
            if global_top:
                v.wait_ge(exped, 2)
                step(v.scalar_tensor_tensor(den[:], top[:], 1.0e-16, cells(got)[:, :, :, HD], ALU.mult, ALU.add))
            else:
                step(v.tensor_scalar(den[:], cells(got)[:, :, :, HD], 1.0e-16, None, ALU.add))
            step(v.reciprocal(den[:], den[:]))
            step(v.tensor_tensor(den[:], den[:], C["has_edge"][:].unsqueeze(2).to_broadcast([P, TILES, HEADS]), ALU.mult))
            step(v.tensor_tensor(cells(got), cells(got), den[:].unsqueeze(3).to_broadcast([P, TILES, HEADS, HD + 1]), ALU.mult))
            heads = lambda a: a[:].rearrange("p t (h d) -> p t h d", h=HEADS)
            step(v.tensor_tensor(heads(out), heads(base), cells(got)[:, :, :, 0:HD], ALU.add))
            if bias is not None:
                v.wait_ge(loads, 16)
                step(v.tensor_tensor(out[:], out[:], bias_row[:].unsqueeze(1).to_broadcast([P, TILES, DIM]), ALU.add))

        @block.scalar
        def _(act):
            for t in range(TILES):
                act.wait_ge(crossed, t + 1)
                act.activation(into[:, t, :], in_ps[t % 4][:], ACT.Copy).then_inc(copied, 1)
            act.wait_ge(lessed, 1)
            act.activation(less[:], less[:], ACT.Exp).then_inc(exped, 1)
            if global_top:
                act.wait_ge(topped, 3)
                act.activation(top[:], top[:], ACT.Exp).then_inc(exped, 1)

        @block.tensor
        def _(pe):
            for t in range(TILES):
                pe.wait_ge(gated, t + 1)
                if t >= 4:
                    pe.wait_ge(copied, t - 3)
                pe.matmul(in_ps[t % 4][:], gate[:, t % 2, :], C["carried"][:], start=True, stop=True).then_inc(crossed, 1)
    arrived.base += 16 * TILES



def slice_weights_stage(nc, st, C, A, w_log, b_log):
    wxT = st.sb("wxT", [SD, SH, DIM])
    wsl = st.sb("wsl", [SD, SD])
    bx = st.sb("bx", [SD, SH])
    bx_wide = st.sb("bx_wide", [SD, SH, P])
    bsl = st.sb("bsl", [P, SD])
    temp = st.sb("temp", [P, SH])
    w_ps = [st.ps(f"w_ps{k}", [P, SLICES]) for k in range(KT)]
    b_ps = st.ps("b_ps", [P, SLICES])
    loads, chain, wide, made = (st.sem(n) for n in ("loads", "chain", "wide", "made"))
    heads = "p (h g) -> p h g"
    with st.block() as block:
        @block.sync
        def _(sp):
            sp.dma_start(wxT[:], A["L0_ffn_W_x"].rearrange("(h c) k -> c h k", c=SD)).then_inc(loads, 16)
            sp.dma_start(wsl[:], A["L0_ffn_W_slice"]).then_inc(loads, 16)
            sp.dma_start(bx[:], A["L0_ffn_b_x"]).then_inc(loads, 16)
            sp.dma_start(bsl[:], A["L0_ffn_b_slice"].partition_broadcast(P)).then_inc(loads, 16)
            sp.dma_start(temp[:], A["L0_ffn_temperature"].rearrange("a h b c -> (a h b c)").partition_broadcast(P)).then_inc(loads, 16)
            sp.wait_ge(loads, 80)

        @block.vector
        def _(v):
            step = st.steps(v, chain)
            v.wait_ge(loads, 80)
            step(v.tensor_copy(bx_wide[:], bx[:].unsqueeze(2).to_broadcast([SD, SH, P])))
            v.sem_inc(wide, 1)
            step(v.tensor_scalar(temp[:], temp[:], 0.1, 5.0, ALU.max, ALU.min))
            step(v.reciprocal(temp[:], temp[:]))
            v.wait_ge(made, 1)
            by_temp = temp[:].unsqueeze(2).to_broadcast([P, SH, SD])
            for k in range(KT):
                step(v.tensor_tensor(w_log[:, k, :].rearrange(heads, h=SH), w_ps[k][:].rearrange(heads, h=SH), by_temp, ALU.mult))
            step(v.tensor_tensor(b_log[:].rearrange(heads, h=SH), b_ps[:].rearrange(heads, h=SH), bsl[:].unsqueeze(1).to_broadcast([P, SH, SD]), ALU.add))
            step(v.tensor_tensor(b_log[:].rearrange(heads, h=SH), b_log[:].rearrange(heads, h=SH), by_temp, ALU.mult))

        @block.tensor
        def _(pe):
            pe.wait_ge(wide, 1)
            for h in range(SH):
                at = slice(h * SD, (h + 1) * SD)
                for k in range(KT):
                    pe.matmul(w_ps[k][:, at], wxT[:, h, k * P:(k + 1) * P], wsl[:], start=True, stop=True)
                ins = pe.matmul(b_ps[:, at], bx_wide[:, h, :], wsl[:], start=True, stop=True)
            ins.then_inc(made, 1)


def assign_stage(nc, st, C, XN, XT, w_log, b_log, SWT, Z):
    xt = st.sb("xt", [P, 2, KT, P])
    sw = st.sb("sw", [P, 2, SLICES])
    raw = st.sb("raw", [P, 2, SLICES])
    top, total = st.sb("top", [P, 2, SH]), st.sb("total", [P, 2, SH])
    NZ = SLICES // P
    log_ps = [st.ps(f"log_ps{i}", [P, SLICES]) for i in range(2)]
    turn_ps = [st.ps(f"turn_ps{i}", [P, NZ, P]) for i in range(2)]
    z_ps = [st.ps(f"z_ps{i}", [P, DIM + 1]) for i in range(NZ)]
    brought, logits, chain, shifted, exped, weighed, summed, copied, norm_chain = (st.sem(n) for n in (
        "brought", "logits", "chain", "shifted", "exped", "weighed", "summed", "copied", "norm_chain"))
    last_rows = NODES - (TILES - 1) * P
    heads = "p (h g) -> p h g"
    with st.block() as block:
        @block.gpsimd
        def _(pool):
            def bring(t, slot, first):
                if not first:
                    hold(pool, st.passed, logits, t - 1)
                pool.tensor_copy(xt[:, slot], XT[:, :, ds(t * P, P)]).then_inc(brought, 1)
            each_tile(pool, bring)

        @block.tensor
        def _(pe):
            def score(t, slot, first):
                hold(pe, st.passed, brought, t + 1)
                if not first:
                    hold(pe, st.passed, shifted, t - 1)
                for k in range(KT):
                    ins = pe.matmul(log_ps[slot][:], xt[:, slot, k, :], w_log[:, k, :], start=(k == 0), stop=(k == KT - 1))
                ins.then_inc(logits, 1)

            def collect(t, slot, first):
                hold(pe, st.passed, weighed, t + 1)
                if not first:
                    hold(pe, st.passed, copied, t - 1)
                for z in range(NZ):
                    pe.transpose(turn_ps[slot][:, z, :], sw[:, slot, z * P:(z + 1) * P], C["ident"][:])
                n = last_rows if isinstance(t, int) and t == TILES - 1 else P
                begins, ends = isinstance(t, int) and t == 0, isinstance(t, int) and t == TILES - 1
                for z in range(NZ):
                    mine = sw[0:n, slot, z * P:(z + 1) * P]
                    pe.matmul(z_ps[z][:, 0:DIM], mine, XN[0:n, ds(t, 1), :].rearrange("p a d -> p (a d)"), start=begins, stop=False)
                    ins = pe.matmul(z_ps[z][:, DIM:DIM + 1], mine, C["ones"][0:n, 0:1], start=False, stop=ends)
                ins.then_inc(summed, 1)
            score(0, 0, True)
            score(1, 1, True)
            score(2, 0, False)
            collect(0, 0, True)
            score(3, 1, False)
            collect(1, 1, True)
            with pe.Fori(1, TILES // 2 - 1) as i:
                score(i * 2 + 2, 0, False)
                collect(i * 2, 0, False)
                score(i * 2 + 3, 1, False)
                collect(i * 2 + 1, 1, False)
            score(TILES - 1, 0, False)
            collect(TILES - 3, 0, False)
            collect(TILES - 2, 1, False)
            collect(TILES - 1, 0, False)

        @block.vector
        def _(v):
            step = st.steps(v, chain)

            def shift(t, slot, first):
                step.turn(t, 2)
                hold(v, st.passed, logits, t + 1)
                if not first:
                    hold(v, st.passed, weighed, t - 1)
                cells = raw[:, slot, :].rearrange(heads, h=SH)
                step(v.tensor_tensor(raw[:, slot, :], log_ps[slot][:], b_log[:], ALU.add))
                step(v.tensor_reduce(top[:, slot, :], cells, AX_X, ALU.max))
                v.tensor_tensor(cells, cells, top[:, slot, :].unsqueeze(2).to_broadcast([P, SH, SD]), ALU.subtract).then_inc(shifted, 1)
                step.end_turn()

            chain2 = st.steps(v, norm_chain)

            def normalize(t, slot, first):
                chain2.turn(t, 2)
                hold(v, st.passed, exped, t + 1)
                cells = raw[:, slot, :].rearrange(heads, h=SH)
                chain2(v.tensor_reduce(total[:, slot, :], cells, AX_X, ALU.add))
                chain2(v.reciprocal(total[:, slot, :], total[:, slot, :]))
                if not first:
                    hold(v, st.passed, summed, t - 1)
                v.tensor_tensor(sw[:, slot, :].rearrange(heads, h=SH), cells, total[:, slot, :].unsqueeze(2).to_broadcast([P, SH, SD]), ALU.mult).then_inc(weighed, 1)
                chain2.end_turn()
            shift(0, 0, True)
            shift(1, 1, True)
            normalize(0, 0, True)
            with v.Fori(1, TILES // 2) as i:
                shift(i * 2, 0, False)
                normalize(i * 2 - 1, 1, False)
                shift(i * 2 + 1, 1, False)
                normalize(i * 2, 0, False)
            shift(TILES - 1, 0, False)
            normalize(TILES - 2, 1, False)
            normalize(TILES - 1, 0, False)
            v.wait_ge(summed, TILES)
            step2 = st.steps(v, norm_chain)
            step2.base = 2 * TILES
            for z in range(NZ):
                step2(v.tensor_copy(Z[:, z, 0:DIM + 1], z_ps[z][:]))

        @block.scalar
        def _(act):
            def exps(t, slot, first):
                hold(act, st.passed, shifted, t + 1)
                act.activation(raw[:, slot, :], raw[:, slot, :], ACT.Exp).then_inc(exped, 1)

            def copy(t, slot, first):
                hold(act, st.passed, summed, t + 1)
                act.activation(SWT[:, :, ds(t * P, P)], turn_ps[slot][:], ACT.Copy).then_inc(copied, 1)
            exps(0, 0, True)
            exps(1, 1, True)
            copy(0, 0, True)
            with act.Fori(1, TILES // 2) as i:
                exps(i * 2, 0, False)
                copy(i * 2 - 1, 1, False)
                exps(i * 2 + 1, 1, False)
                copy(i * 2, 0, False)
            exps(TILES - 1, 0, False)
            copy(TILES - 2, 1, False)
            copy(TILES - 1, 0, False)


def slice_attention_stage(nc, st, C, A, Z, mix):
    NZ = SLICES // P
    w_fx, w_q, w_k, w_v = st.sb("w_fx", [P, KT, SLICES]), st.sb("w_q", [SD, SD]), st.sb("w_k", [SD, SD]), st.sb("w_v", [SD, SD])
    w_out, b_fx = st.sb("w_out", [SD, SH, DIM]), st.sb("b_fx", [1, SLICES])
    ZT, norm_row = st.sb("ZT", [P, KT, SLICES]), st.sb("norm_row", [1, SLICES])
    inv_row, tokT = st.sb("inv_row", [1, SLICES]), st.sb("tokT", [SD, SLICES])
    inv = st.sb("inv", [SD, SLICES])
    qT, kT, vT = (st.sb(n, [SD, SLICES]) for n in ("qT", "kT", "vT"))
    prob, probT = st.sb("prob", [SD, SLICES]), st.sb("probT", [SD, SLICES])
    top, total = st.sb("top", [SD, SH]), st.sb("total", [SD, SH])
    vw = st.sb("vw", [SD, SH, DIM])
    a_ps, b_ps, c_ps, d_ps = (st.ps(n, [P, 512]) for n in ("a_ps", "b_ps", "c_ps", "d_ps"))
    e_ps = [st.ps(f"e_ps{i}", [P, 2, DIM]) for i in range(2)]
    loads, chain, pe_ok, dve_ok, act_ok = (st.sem(n) for n in ("loads", "chain", "pe_ok", "dve_ok", "act_ok"))
    heads = "p (h g) -> p h g"
    scale = float(SD) ** -0.5
    with st.block() as block:
        @block.sync
        def _(sp):
            sp.dma_start(w_fx[:], A["L0_ffn_W_fx"].rearrange("(k p) n -> p k n", p=P)).then_inc(loads, 16)
            for tile, name in ((w_q, "W_q"), (w_k, "W_k"), (w_v, "W_v")):
                sp.dma_start(tile[:], A[f"L0_ffn_{name}"]).then_inc(loads, 16)
            sp.dma_start(w_out[:], A["L0_ffn_W_out"].rearrange("(h c) n -> c h n", c=SD)).then_inc(loads, 16)
            sp.dma_start(b_fx[:], A["L0_ffn_b_fx"].rearrange("(a n) -> a n", a=1)).then_inc(loads, 16)
            sp.wait_ge(loads, 96)

        @block.tensor
        def _(pe):
            pe.wait_ge(loads, 96)
            for k in range(KT):
                for z in range(NZ):
                    pe.transpose((a_ps, b_ps)[k][:, z * P:(z + 1) * P], Z[:, z, k * P:(k + 1) * P], C["ident"][:])
            for z in range(NZ):
                ins = pe.transpose(c_ps[0:1, z * P:(z + 1) * P], Z[:, z, DIM:DIM + 1], C["ident"][:])
            ins.then_inc(pe_ok, 1)
            pe.wait_ge(dve_ok, 1)
            for h in range(SH):
                at = slice(h * SD, (h + 1) * SD)
                for k in range(KT):
                    pe.matmul(d_ps[0:SD, at], w_fx[:, k, at], ZT[:, k, at], start=(k == 0), stop=False)
                pe.matmul(d_ps[0:SD, at], b_fx[0:1, at], norm_row[0:1, at], start=False, stop=True)
            pe.matmul(c_ps[0:SD, :], C["ones"][0:1, 0:SD], inv_row[:], start=True, stop=True).then_inc(pe_ok, 1)
            pe.wait_ge(dve_ok, 2)
            for ps, w in ((a_ps, w_q), (b_ps, w_k), (c_ps, w_v)):
                ins = pe.matmul(ps[0:SD, :], w[:], tokT[:], start=True, stop=True)
            ins.then_inc(pe_ok, 1)
            pe.wait_ge(dve_ok, 3)
            for h in range(SH):
                at = slice(h * SD, (h + 1) * SD)
                pe.matmul(d_ps[0:SD, at], qT[:, at], kT[:, at], start=True, stop=True)
                ins = pe.matmul((a_ps, b_ps)[h % 2][0:SD, 0:DIM], vT[:, at], w_out[:, h, :], start=True, stop=True)
                ins.then_inc(pe_ok, 1)
                pe.wait_ge(dve_ok, 4 + h)
            pe.wait_ge(dve_ok, 4 + SH)
            for h in range(SH):
                at = slice(h * SD, (h + 1) * SD)
                ins = pe.transpose(c_ps[0:SD, at], prob[:, at], C["ident"][0:SD, 0:SD])
            ins.then_inc(pe_ok, 1)
            pe.wait_ge(dve_ok, 5 + SH)
            for h in range(SH):
                half = slice((h % 2) * SD, (h % 2 + 1) * SD)
                ins = pe.matmul(e_ps[h // 4][half, (h // 2) % 2, :], probT[:, h * SD:(h + 1) * SD], vw[:, h, :], start=True, stop=True)
            ins.then_inc(pe_ok, 1)

        @block.vector
        def _(v):
            step = st.steps(v, chain)
            v.wait_ge(pe_ok, 1)
            step(v.tensor_copy(ZT[:, 0, :], a_ps[:]))
            step(v.tensor_copy(ZT[:, 1, :], b_ps[:]))
            step(v.tensor_copy(norm_row[:], c_ps[0:1, :]))
            step(v.tensor_scalar(inv_row[:], norm_row[:], 1.0e-5, None, ALU.add))
            step(v.reciprocal(inv_row[:], inv_row[:]))
            v.sem_inc(dve_ok, 1)
            v.wait_ge(pe_ok, 2)
            step(v.tensor_copy(inv[:], c_ps[0:SD, :]))
            step(v.tensor_tensor(tokT[:], d_ps[0:SD, :], inv[:], ALU.mult))
            v.sem_inc(dve_ok, 1)
            v.wait_ge(pe_ok, 3)
            for tile, ps in ((qT, a_ps), (kT, b_ps), (vT, c_ps)):
                step(v.tensor_copy(tile[:], ps[0:SD, :]))
            v.sem_inc(dve_ok, 1)
            for h in range(SH):
                v.wait_ge(pe_ok, 4 + h)
                step(v.tensor_copy(vw[:, h, :], (a_ps, b_ps)[h % 2][0:SD, 0:DIM]))
                v.sem_inc(dve_ok, 1)
            cells = prob[:].rearrange(heads, h=SH)
            step(v.tensor_reduce(top[:], d_ps[0:SD, :].rearrange(heads, h=SH), AX_X, ALU.max))
            step(v.tensor_tensor(cells, d_ps[0:SD, :].rearrange(heads, h=SH), top[:].unsqueeze(2).to_broadcast([SD, SH, SD]), ALU.subtract))
            v.sem_inc(act_ok, 1)
            v.wait_ge(act_ok, 2)
            step(v.tensor_reduce(total[:], cells, AX_X, ALU.add))
            step(v.reciprocal(total[:], total[:]))
            step(v.tensor_tensor(cells, cells, total[:].unsqueeze(2).to_broadcast([SD, SH, SD]), ALU.mult))
            v.sem_inc(dve_ok, 1)
            v.wait_ge(pe_ok, 4 + SH)
            step(v.tensor_copy(probT[:], c_ps[0:SD, :]))
            v.sem_inc(dve_ok, 1)
            v.wait_ge(pe_ok, 5 + SH)
            for z in range(NZ):
                step(v.tensor_copy(mix[:, z, :], e_ps[z // 2][:, z % 2, :]))

        @block.scalar
        def _(act):
            act.wait_ge(act_ok, 1)
            act.activation(prob[:], prob[:], ACT.Exp, scale=scale).then_inc(act_ok, 1)


def mix_stage(nc, st, C, A, SWT, mix, X):
    NZ = SLICES // P
    swt = st.sb("swt", [P, 2, NZ, P])
    b_row = st.sb("b_row", [P, DIM])
    y_ps = [st.ps(f"y_ps{i}", [P, DIM]) for i in range(2)]
    loads, brought, made, added, chain = (st.sem(n) for n in ("loads", "brought", "made", "added", "chain"))
    with st.block() as block:
        @block.sync
        def _(sp):
            sp.dma_start(b_row[:], A["L0_ffn_b_out"].partition_broadcast(P)).then_inc(loads, 16)
            sp.wait_ge(loads, 16)

        @block.gpsimd
        def _(pool):
            def bring(t, slot, first):
                if not first:
                    hold(pool, st.passed, made, t - 1)
                pool.tensor_copy(swt[:, slot], SWT[:, :, ds(t * P, P)]).then_inc(brought, 1)
            each_tile(pool, bring)

        @block.tensor
        def _(pe):
            def product(t, slot, first):
                hold(pe, st.passed, brought, t + 1)
                if not first:
                    hold(pe, st.passed, added, t - 1)
                for z in range(NZ):
                    ins = pe.matmul(y_ps[slot][:], swt[:, slot, z, :], mix[:, z, :], start=(z == 0), stop=(z == NZ - 1))
                ins.then_inc(made, 1)
            each_tile(pe, product)

        @block.vector
        def _(v):
            step = st.steps(v, chain)
            v.wait_ge(loads, 16)

            def add(t, slot, first):
                step.turn(t, 1)
                row = X[:, ds(t, 1), :].rearrange("p a d -> p (a d)")
                hold(v, st.passed, made, t + 1)
                step(v.tensor_tensor(row, row, y_ps[slot][:], ALU.add))
                v.tensor_tensor(row, row, b_row[:], ALU.add).then_inc(added, 1)
            each_tile(v, add)



def spread_rows_stage(nc, st, C, D, Zn, X, rows_ready):
    placed, stored = C["placed"], st.sem("stored")
    tiles = "(t p) d -> p t d"
    with st.block() as block:
        @block.gpsimd
        def _(pool):
            pool.wait_ge(rows_ready, 1)
            for t in range(TILES):
                pool.indirect_dma_start(D["ordered"], bass.IndirectOffsetOnAxis(C["rank"][:, t:t + 1], 0), Zn[:, t, :], None).then_inc(placed.sem, 16)
            pool.wait_ge(placed.sem, placed.base + 16 * TILES)

        @block.sync
        def _(sp):
            sp.wait_ge(rows_ready, 1)
            for name, rows in (("x", X), ("z", Zn)):
                sp.dma_start(D[name].rearrange(tiles, p=P), rows[:]).then_inc(stored, 16)
            sp.wait_ge(stored, 32)
    placed.base += 16 * TILES


def ordered_stage(nc, st, C, D, ZT):
    row = st.sb("row", [P, 2, DIM])
    pt = [st.ps(f"pt{i}", [P, KT, P]) for i in range(2)]
    arrived = [st.sem(f"arrived{s}") for s in range(2)]
    turned, copied = st.sem("turned"), st.sem("copied")
    with st.block() as block:
        @block.sync
        def _(sp):
            def load(t, slot, first):
                if not first:
                    hold(sp, st.passed, turned, t - 1)
                sp.dma_start(row[:, slot, :], D["ordered"][ds(t * P, P), :]).then_inc(arrived[slot], 16)
            each_tile(sp, load)

        @block.tensor
        def _(pe):
            def turn(t, slot, first):
                hold(pe, st.passed, arrived[slot], (t - slot) * 8 + 16)
                if not first:
                    hold(pe, st.passed, copied, t - 1)
                for k in range(KT):
                    ins = pe.transpose(pt[slot][:, k, :], row[:, slot, k * P:(k + 1) * P], C["ident"][:])
                ins.then_inc(turned, 1)
            each_tile(pe, turn)

        @block.scalar
        def _(act):
            def copy(t, slot, first):
                hold(act, st.passed, turned, t + 1)
                act.activation(ZT[:, :, ds(t * P, P)], pt[slot][:], ACT.Copy).then_inc(copied, 1)
            each_tile(act, copy)


def in_proj_stage(nc, st, C, A, ZT, RAW, GATE):
    w = st.sb("w", [P, KT, 2 * DIM])
    ps = [[st.ps(f"ps{s}{m}", [P, 512]) for m in range(2 * KT)] for s in range(2)]
    loads, made, raw_out, gate_out = (st.sem(n) for n in ("loads", "made", "raw_out", "gate_out"))
    with st.block() as block:
        @block.sync
        def _(sp):
            sp.dma_start(w[:], A["L1_gnn_in_proj_w"].rearrange("(k p) n -> p k n", p=P)).then_inc(loads, 16)
            sp.wait_ge(loads, 16)

        @block.tensor
        def _(pe):
            pe.wait_ge(loads, 16)

            def product(c, slot, first):
                if not first:
                    hold(pe, st.passed, raw_out, c - 1)
                    hold(pe, st.passed, gate_out, c - 1)
                for m in range(2 * KT):
                    for k in range(KT):
                        ins = pe.matmul(ps[slot][m][:, 0:CHUNK], w[:, k, m * P:(m + 1) * P], ZT[:, k, ds(c * CHUNK, CHUNK)], start=(k == 0), stop=(k == KT - 1))
                ins.then_inc(made, 1)
            each_group(pe, CHUNKS, product)

        @block.vector
        def _(v):
            for m in range(KT):
                v.memset(RAW[:, m, 0:TAPS - 1], 0.0)

            def raw(c, slot, first):
                hold(v, st.passed, made, c + 1)
                for m in range(KT):
                    ins = v.tensor_copy(RAW[:, m, ds(c * CHUNK + (TAPS - 1), CHUNK)], ps[slot][m][:, 0:CHUNK])
                ins.then_inc(raw_out, 1)
            each_group(v, CHUNKS, raw)

        @block.scalar
        def _(act):
            def gate(c, slot, first):
                hold(act, st.passed, made, c + 1)
                for m in range(KT):
                    ins = act.activation(GATE[:, m, ds(c * CHUNK, CHUNK)], ps[slot][KT + m][:, 0:CHUNK], ACT.Silu)
                ins.then_inc(gate_out, 1)
            each_group(act, CHUNKS, gate)


def conv_stage(nc, st, C, A, RAW, XC):
    w, b = st.sb("w", [P, KT, TAPS]), st.sb("b", [P, KT])
    loads, chain, summed, act_out = (st.sem(n) for n in ("loads", "chain", "summed", "act_out"))
    with st.block() as block:
        @block.sync
        def _(sp):
            sp.dma_start(w[:], A["L1_gnn_conv_w"].rearrange("(k p) n -> p k n", p=P)).then_inc(loads, 16)
            sp.dma_start(b[:], A["L1_gnn_conv_b"]).then_inc(loads, 16)
            sp.wait_ge(loads, 32)

        @block.vector
        def _(v):
            step = st.steps(v, chain)
            v.wait_ge(loads, 32)
            for m in range(KT):
                step(v.tensor_scalar(XC[:, m, :], RAW[:, m, 0:ROWS], w[:, m, 0:1], None, ALU.mult))
                for k in range(1, TAPS):
                    step(v.scalar_tensor_tensor(XC[:, m, :], RAW[:, m, k:k + ROWS], w[:, m, k:k + 1], XC[:, m, :], ALU.mult, ALU.add))
                v.sem_inc(summed, 1)

        @block.scalar
        def _(act):
            act.wait_ge(loads, 32)
            for m in range(KT):
                act.wait_ge(summed, m + 1)
                act.activation(XC[:, m, :], XC[:, m, :], ACT.Silu, bias=b[:, m:m + 1]).then_inc(act_out, 1)
            act.wait_ge(act_out, KT)


def x_proj_stage(nc, st, C, A, D, XC, DT, U):
    wx, wdt, b = st.sb("wx", [P, KT, RANK + 2 * STATES]), st.sb("wdt", [RANK, DIM]), st.sb("b", [P, KT])
    dbc = st.sb("dbc", [RANK + 2 * STATES, ROWS])
    HALF = ROWS // 2
    near, e, w, ln, short = (st.sb(n, [P, 2, HALF]) for n in ("near", "e", "w", "ln", "short"))
    SMALL = 1.0 / 64
    pieces = [(m, slice(i * HALF, (i + 1) * HALF)) for m in range(KT) for i in range(2)]
    x_ps = [st.ps(f"x_ps{i}", [RANK + 2 * STATES, 512]) for i in range(2)]
    d_ps = [[st.ps(f"d_ps{s}{m}", [P, 512]) for m in range(KT)] for s in range(2)]
    loads, made, out, steps_made, steps_out, chain, asked, answered, stored, done, series = (st.sem(n) for n in (
        "loads", "made", "out", "steps_made", "steps_out", "chain", "asked", "answered", "stored", "done", "series"))
    with st.block() as block:
        @block.sync
        def _(sp):
            sp.dma_start(wx[:], A["L1_gnn_x_proj_w"].rearrange("(k p) n -> p k n", p=P)).then_inc(loads, 16)
            sp.dma_start(wdt[:], A["L1_gnn_dt_proj_w"]).then_inc(loads, 16)
            sp.dma_start(b[:], A["L1_gnn_dt_proj_b"]).then_inc(loads, 16)
            sp.wait_ge(out, CHUNKS)
            sp.dma_start(D["bc"], dbc[RANK:RANK + 2 * STATES, :]).then_inc(stored, 16)
            sp.wait_ge(stored, 16)

        @block.tensor
        def _(pe):
            pe.wait_ge(loads, 48)

            def product(c, slot, first):
                if not first:
                    hold(pe, st.passed, out, c - 1)
                for k in range(KT):
                    ins = pe.matmul(x_ps[slot][:, 0:CHUNK], wx[:, k, :], XC[:, k, ds(c * CHUNK, CHUNK)], start=(k == 0), stop=(k == KT - 1))
                ins.then_inc(made, 1)

            def steps_of(c, slot, first):
                hold(pe, st.passed, out, c + 1)
                if not first:
                    hold(pe, st.passed, steps_out, c - 1)
                for m in range(KT):
                    ins = pe.matmul(d_ps[slot][m][:, 0:CHUNK], wdt[:, m * P:(m + 1) * P], dbc[0:RANK, ds(c * CHUNK, CHUNK)], start=True, stop=True)
                ins.then_inc(steps_made, 1)
            product(0, 0, True)
            product(1, 1, True)
            steps_of(0, 0, True)
            product(2, 0, False)
            steps_of(1, 1, True)
            with pe.Fori(1, CHUNKS // 2 - 1) as i:
                product(i * 2 + 1, 1, False)
                steps_of(i * 2, 0, False)
                product(i * 2 + 2, 0, False)
                steps_of(i * 2 + 1, 1, False)
            product(CHUNKS - 1, 1, False)
            steps_of(CHUNKS - 2, 0, False)
            steps_of(CHUNKS - 1, 1, False)

        @block.gpsimd
        def _(pool):
            for n in range(len(pieces)):
                i = n % 2
                pool.wait_ge(answered, 3 * n + 1)
                pool.tensor_scalar(short[:, i], e[:, i], -0.25, 1.0 / 3, ALU.mult, ALU.add).then_inc(series, 1)
                pool.wait_ge(series, 2 * n + 1)
                pool.tensor_tensor(short[:, i], short[:, i], e[:, i], ALU.mult).then_inc(series, 1)

        @block.scalar
        def _(act):
            def copy(c, slot, first):
                hold(act, st.passed, made, c + 1)
                act.activation(dbc[:, ds(c * CHUNK, CHUNK)], x_ps[slot][:, 0:CHUNK], ACT.Copy).then_inc(out, 1)
            each_group(act, CHUNKS, copy)
            for n in range(len(pieces)):
                act.wait_ge(asked, n + 1)
                if n >= 2:
                    act.wait_ge(done, n - 1)
                act.activation(e[:, n % 2], near[:, n % 2], ACT.Exp).then_inc(answered, 1)
                act.wait_ge(answered, 3 * n + 1)
                act.activation(w[:, n % 2], e[:, n % 2], ACT.Identity, bias=C["ones"][:, 0:1]).then_inc(answered, 1)
                act.wait_ge(answered, 3 * n + 2)
                act.activation(ln[:, n % 2], w[:, n % 2], ACT.Ln).then_inc(answered, 1)

        @block.vector
        def _(v):
            step = st.steps(v, chain)
            v.wait_ge(loads, 48)

            def add_bias(c, slot, first):
                hold(v, st.passed, steps_made, c + 1)
                for m in range(KT):
                    ins = v.tensor_scalar(DT[:, m, ds(c * CHUNK, CHUNK)], d_ps[slot][m][:, 0:CHUNK], b[:, m:m + 1], None, ALU.add)
                ins.then_inc(steps_out, 1)
            each_group(v, CHUNKS, add_bias)
            v.wait_ge(steps_out, CHUNKS)
            def ask(n):
                m, at = pieces[n]
                v.scalar_tensor_tensor(near[:, n % 2], DT[:, m, at], -1.0, DT[:, m, at], ALU.mult, ALU.min).then_inc(asked, 1)
            ask(0)
            ask(1)
            for n, (m, at) in enumerate(pieces):
                i = n % 2
                v.wait_ge(answered, 3 * n + 3)
                step(v.scalar_tensor_tensor(w[:, i], w[:, i], 1.0, e[:, i], ALU.subtract, ALU.subtract))
                step(v.tensor_tensor(ln[:, i], ln[:, i], w[:, i], ALU.subtract))
                v.wait_ge(series, 2 * n + 2)
                step(v.scalar_tensor_tensor(short[:, i], short[:, i], -0.5, e[:, i], ALU.add, ALU.mult))
                step(v.scalar_tensor_tensor(short[:, i], short[:, i], 1.0, e[:, i], ALU.add, ALU.mult))
                step(v.tensor_tensor(ln[:, i], ln[:, i], short[:, i], ALU.subtract))
                step(v.scalar_tensor_tensor(ln[:, i], e[:, i], SMALL, ln[:, i], ALU.is_ge, ALU.mult))
                step(v.tensor_tensor(ln[:, i], ln[:, i], short[:, i], ALU.add))
                step(v.scalar_tensor_tensor(DT[:, m, at], DT[:, m, at], 0.0, ln[:, i], ALU.max, ALU.add))
                v.sem_inc(done, 1)
                if n + 2 < len(pieces):
                    ask(n + 2)
            step(v.tensor_tensor(U[:], DT[:], XC[:], ALU.mult))


def scan_stage(nc, st, C, A, D, XC, DT, U, GATE):
    SPAN = ROWS // SPANS
    PIECES = SPAN // CHUNK
    a, d_par = st.sb("a", [P, KT, STATES]), st.sb("d_par", [P, KT])
    rows = st.sb("rows", [P, 2, 2, SPAN])
    decay, feed, state, seen = (st.sb(n, [P, KT, SPAN]) for n in ("decay", "feed", "state", "seen"))
    end = st.sb("end", [P, KT, STATES])
    y_ps = [[st.ps(f"y_ps{m}{c}", [P, 512]) for c in range(PIECES)] for m in range(KT)]
    b_in, c_in = ([st.sem(f"{k}_in{s}") for s in range(2)] for k in "bc")
    loads, chain, decays, feeds, scans, seens, sums, cleared, ready = (st.sem(n) for n in (
        "loads", "chain", "decays", "feeds", "scans", "seens", "sums", "cleared", "ready"))

    def each_state(eng, body):
        body(0, 0)
        body(1, 1)
        with eng.Fori(1, STATES // 2 - 1) as i:
            body(i * 2, 0)
            body(i * 2 + 1, 1)
        body(STATES - 2, 0)
        body(STATES - 1, 1)

    def fresh(span, s):
        return span == 0 and isinstance(s, int) and s < 2

    def begun(span, s):
        return span == 0 and isinstance(s, int) and s == 0

    with st.block() as block:
        @block.sync
        def _(sp):
            sp.dma_start(a[:], A["L1_gnn_A_log"].rearrange("(k p) n -> p k n", p=P)).then_inc(loads, 16)
            sp.dma_start(d_par[:], A["L1_gnn_D_param"]).then_inc(loads, 16)
            for span in range(SPANS):
                def load(s, slot):
                    n = s + span * STATES
                    for i, (used, brought) in enumerate(((feeds, b_in), (seens, c_in))):
                        if not fresh(span, s):
                            hold(sp, st.passed, used, (n - 1) * KT)
                        sp.dma_start(rows[:, slot, i, :], D["bc"][ds(s + i * STATES, 1), span * SPAN:(span + 1) * SPAN].rearrange(
                            "a n -> (a n)").partition_broadcast(P)).then_inc(brought[slot], 16)
                each_state(sp, load)

        @block.scalar
        def _(act):
            act.wait_ge(loads, 32)
            act.activation(a[:], a[:], ACT.Exp).then_inc(ready, 1)
            act.wait_ge(ready, 1)
            act.mul(a[:], a[:], -1.0).then_inc(ready, 1)
            act.wait_ge(ready, 2)
            for span in range(SPANS):
                def decay_of(s, slot):
                    for m in range(KT):
                        i = (s + span * STATES) * KT + m
                        if not begun(span, s):
                            hold(act, st.passed, scans, i - 1)
                        act.activation(decay[:, m, :], DT[:, m, span * SPAN:(span + 1) * SPAN], ACT.Exp, scale=a[:, m, ds(s, 1)]).then_inc(decays, 1)
                each_state(act, decay_of)

        @block.gpsimd
        def _(pool):
            for span in range(SPANS):
                def feed_of(s, slot):
                    n = s + span * STATES
                    hold(pool, st.passed, b_in[slot], (n - slot) * 8 + 16)
                    for m in range(KT):
                        if not begun(span, s):
                            hold(pool, st.passed, scans, n * KT + m - 1)
                        pool.tensor_tensor(feed[:, m, :], U[:, m, span * SPAN:(span + 1) * SPAN], rows[:, slot, 0, :], ALU.mult).then_inc(feeds, 1)
                each_state(pool, feed_of)

        @block.vector
        def _(v):
            step = st.steps(v, chain)
            v.wait_ge(loads, 32)
            for span in range(SPANS):
                def scan(s, slot, m):
                    i = (s + span * STATES) * KT + m
                    hold(v, st.passed, decays, i + 1)
                    hold(v, st.passed, feeds, i + 1)
                    if not begun(span, s):
                        hold(v, st.passed, seens, i - 1)
                    start = end[:, m, ds(s, 1)] if span else 0.0
                    v.tensor_tensor_scan(state[:, m, :], decay[:, m, :], feed[:, m, :], start, ALU.mult, ALU.add).then_inc(scans, 1)

                def see(s, slot, m):
                    i = (s + span * STATES) * KT + m
                    hold(v, st.passed, scans, i + 1)
                    if span < SPANS - 1:
                        v.tensor_copy(end[:, m, ds(s, 1)], state[:, m, SPAN - 1:SPAN])
                    hold(v, st.passed, c_in[slot], (s - slot) * 8 + (span * STATES * 8 + 16))
                    if not begun(span, s):
                        hold(v, st.passed, sums, i - 1)
                    v.tensor_tensor(seen[:, m, :], state[:, m, :], rows[:, slot, 1, :], ALU.mult).then_inc(seens, 1)

                def walk(s, slot, more=True):
                    scan(s, slot, 1)
                    see(s, slot, 0)
                    if more:
                        scan(s + 1, 1 - slot, 0)
                    see(s, slot, 1)
                scan(0, 0, 0)
                walk(0, 0)
                walk(1, 1)
                with v.Fori(1, STATES // 2 - 1) as i:
                    walk(i * 2, 0)
                    walk(i * 2 + 1, 1)
                walk(STATES - 2, 0)
                walk(STATES - 1, 1, False)
                v.wait_ge(sums, (span + 1) * STATES * KT)
                for m in range(KT):
                    for c in range(PIECES):
                        at = slice(span * SPAN + c * CHUNK, span * SPAN + (c + 1) * CHUNK)
                        step(v.scalar_tensor_tensor(XC[:, m, at], XC[:, m, at], d_par[:, m:m + 1], y_ps[m][c][:, 0:CHUNK], ALU.mult, ALU.add))
                v.sem_inc(cleared, 1)
                at = slice(span * SPAN, (span + 1) * SPAN)
                step(v.tensor_tensor(XC[:, :, at], XC[:, :, at], GATE[:, :, at], ALU.mult))

        @block.tensor
        def _(pe):
            for span in range(SPANS):
                if span:
                    pe.wait_ge(cleared, span)

                def add(s, slot):
                    for m in range(KT):
                        i = (s + span * STATES) * KT + m
                        hold(pe, st.passed, seens, i + 1)
                        for c in range(PIECES):
                            ins = pe.matmul(y_ps[m][c][:, 0:CHUNK], C["ident"][:], seen[:, m, c * CHUNK:(c + 1) * CHUNK],
                                            start=isinstance(s, int) and s == 0, stop=isinstance(s, int) and s == STATES - 1)
                        ins.then_inc(sums, 1)
                each_state(pe, add)


def out_proj_stage(nc, st, C, A, D, Y):
    w = st.sb("w", [P, KT, DIM])
    yt, row = st.sb("yt", [P, 2, KT, P]), st.sb("row", [P, 2, DIM])
    ps = [st.ps(f"ps{i}", [P, DIM]) for i in range(2)]
    loads, brought, made, out = (st.sem(n) for n in ("loads", "brought", "made", "out"))
    stored = [st.sem(f"stored{s}") for s in range(2)]
    with st.block() as block:
        @block.sync
        def _(sp):
            sp.dma_start(w[:], A["L1_gnn_out_proj_w"].rearrange("(k p) n -> p k n", p=P)).then_inc(loads, 16)

            def store(t, slot, first):
                hold(sp, st.passed, out, t + 1)
                sp.dma_start(D["y"][ds(t * P, P), :], row[:, slot, :]).then_inc(stored[slot], 16)
            each_tile(sp, store)
            sp.wait_ge(stored[0], 16 * (TILES - TILES // 2))
            sp.wait_ge(stored[1], 16 * (TILES // 2))

        @block.gpsimd
        def _(pool):
            def bring(t, slot, first):
                if not first:
                    hold(pool, st.passed, made, t - 1)
                pool.tensor_copy(yt[:, slot], Y[:, :, ds(t * P, P)]).then_inc(brought, 1)
            each_tile(pool, bring)

        @block.tensor
        def _(pe):
            pe.wait_ge(loads, 16)

            def product(t, slot, first):
                hold(pe, st.passed, brought, t + 1)
                if not first:
                    hold(pe, st.passed, out, t - 1)
                for k in range(KT):
                    ins = pe.matmul(ps[slot][:], yt[:, slot, k, :], w[:, k, :], start=(k == 0), stop=(k == KT - 1))
                ins.then_inc(made, 1)
            each_tile(pe, product)

        @block.scalar
        def _(act):
            def copy(t, slot, first):
                hold(act, st.passed, made, t + 1)
                if not first:
                    hold(act, st.passed, stored[slot], (t - slot) * 8)
                act.activation(row[:, slot, :], ps[slot][:], ACT.Copy).then_inc(out, 1)
            each_tile(act, copy)


def elu_stage(nc, st, C, D, HL):
    low = st.sb("low", [P, TILES // 5, DIM])
    chain, asked, answered, made, stored = (st.sem(n) for n in ("chain", "asked", "answered", "made", "stored"))
    with st.block() as block:
        @block.sync
        def _(sp):
            for q in range(5):
                part = slice(q * (TILES // 5), (q + 1) * (TILES // 5))
                sp.wait_ge(made, q + 1)
                sp.dma_start(D["hl"].rearrange("(t p) d -> p t d", p=P)[:, part, :], HL[:, part, :]).then_inc(stored, 16)
            sp.wait_ge(stored, 80)

        @block.vector
        def _(v):
            step = st.steps(v, chain)
            for q in range(5):
                part = HL[:, q * (TILES // 5):(q + 1) * (TILES // 5), :]
                step(v.tensor_scalar(low[:], part, 0.0, None, ALU.min))
                v.sem_inc(asked, 1)
                step(v.tensor_scalar(part, part, 0.0, -1.0, ALU.max, ALU.add))
                v.wait_ge(answered, q + 1)
                step(v.tensor_tensor(part, part, low[:], ALU.add))
                v.sem_inc(made, 1)

        @block.scalar
        def _(act):
            for q in range(5):
                act.wait_ge(asked, q + 1)
                act.activation(low[:], low[:], ACT.Exp).then_inc(answered, 1)


def collect_rows_stage(nc, st, C, D, X, HL, HA, hl_ready, ha_ready):
    got = st.sb("got", [P, TILES, DIM])
    loads = st.sem("loads")
    placed = C["placed"]
    tiles = "(t p) d -> p t d"
    with st.block() as block:
        @block.sync
        def _(sp):
            for sem, name, rows in ((hl_ready, "hl", HL), (loads, "z", HA), (loads, "x", X)):
                sp.dma_start(rows[:], D[name].rearrange(tiles, p=P)).then_inc(sem, 16)

        @block.gpsimd
        def _(pool):
            for t in range(TILES):
                pool.indirect_dma_start(got[:, t, :], None, D["y"], bass.IndirectOffsetOnAxis(C["rank"][:, t:t + 1], 0)).then_inc(placed.sem, 16)

        @block.vector
        def _(v):
            v.wait_ge(loads, 32)
            v.wait_ge(placed.sem, placed.base + 16 * TILES)
            v.tensor_tensor(HA[:], HA[:], got[:], ALU.add).then_inc(ha_ready, 1)
    placed.base += 16 * TILES


def gate_ff_stage(nc, st, C, A, HLT, HAT, VT):
    wl, wg = st.sb("wl", [P, KT, DIM]), st.sb("wg", [P, KT, DIM])
    w1, w2 = st.sb("w1", [P, KT, 2 * DIM]), st.sb("w2", [P, 2 * KT, DIM])
    b1, b2 = st.sb("b1", [P, 2 * KT]), st.sb("b2", [P, KT])
    gate, dif = st.sb("gate", [P, 2, KT, CHUNK]), st.sb("dif", [P, KT, CHUNK])
    h = st.sb("h", [P, 2, KT, CHUNK])
    r = st.sb("r", [P, 2 * KT, CHUNK])
    g_ps = [st.ps(f"g_ps{m}", [P, 512]) for m in range(KT)]
    f_ps = [st.ps(f"f_ps{m}", [P, 512]) for m in range(2 * KT)]
    o_ps = [st.ps(f"o_ps{m}", [P, 512]) for m in range(KT)]
    loads, chain, gated, exped, mixed, hidden, relued, made, out, powers, asked = (st.sem(n) for n in (
        "loads", "chain", "gated", "exped", "mixed", "hidden", "relued", "made", "out", "powers", "asked"))

    def each_chunk(eng, body):
        with eng.Fori(0, CHUNKS // 2 - 1) as i:
            body(i * 2, 0, True)
            body(i * 2 + 1, 1, True)
        body(CHUNKS - 2, 0, False)
        body(CHUNKS - 1, 1, False)

    with st.block() as block:
        @block.sync
        def _(sp):
            for tile, name in ((wl, "wl"), (wg, "wg"), (w1, "ff1_w"), (w2, "ff2_w")):
                sp.dma_start(tile[:], A[f"L1_gnn_{name}"].rearrange("(k p) n -> p k n", p=P)).then_inc(loads, 16)
            sp.dma_start(b1[:], A["L1_gnn_ff1_b"]).then_inc(loads, 16)
            sp.dma_start(b2[:], A["L1_gnn_ff2_b"]).then_inc(loads, 16)
            sp.wait_ge(loads, 96)

        @block.tensor
        def _(pe):
            pe.wait_ge(loads, 96)

            def gates(c):
                if not (isinstance(c, int) and c == 0):
                    hold(pe, st.passed, asked, c)
                at = ds(c * CHUNK, CHUNK)
                for m in range(KT):
                    to = slice(m * P, (m + 1) * P)
                    for n, (w, src) in enumerate(((wl, HLT), (wg, HAT))):
                        for k in range(KT):
                            ins = pe.matmul(g_ps[m][:, 0:CHUNK], w[:, k, to], src[:, k, at], start=(n + k == 0), stop=(n == 1 and k == KT - 1))
                ins.then_inc(gated, 1)

            def chunk(c, slot, more):
                hold(pe, st.passed, mixed, c + 1)
                for m in range(2 * KT):
                    for k in range(KT):
                        ins = pe.matmul(f_ps[m][:, 0:CHUNK], w1[:, k, m * P:(m + 1) * P], h[:, slot, k, :], start=(k == 0), stop=(k == KT - 1))
                ins.then_inc(hidden, 1)
                if more:
                    gates(c + 2)
                hold(pe, st.passed, relued, c + 1)
                hold(pe, st.passed, out, c + 1)
                for m in range(KT):
                    for k in range(2 * KT):
                        ins = pe.matmul(o_ps[m][:, 0:CHUNK], w2[:, k, m * P:(m + 1) * P], r[:, k, :], start=(k == 0), stop=(k == 2 * KT - 1))
                ins.then_inc(made, 1)
            gates(0)
            gates(1)
            each_chunk(pe, chunk)

        @block.scalar
        def _(act):
            act.wait_ge(loads, 96)

            def exps(c, slot):
                hold(act, st.passed, gated, c + 1)
                for m in range(KT):
                    ins = act.activation(gate[:, slot, m, :], g_ps[m][:, 0:CHUNK], ACT.Abs)
                ins.then_inc(powers, 1)
                hold(act, st.passed, powers, c * 2 + 1)
                act.activation(gate[:, slot], gate[:, slot], ACT.Exp, scale=-1.0).then_inc(powers, 1)
                hold(act, st.passed, powers, c * 2 + 2)
                act.activation(gate[:, slot], gate[:, slot], ACT.Ln, bias=C["ones"][:, 0:1]).then_inc(exped, 1)
                hold(act, st.passed, asked, c + 1)
                act.activation(gate[:, slot], gate[:, slot], ACT.Exp).then_inc(exped, 1)

            def chunk(c, slot, more):
                hold(act, st.passed, hidden, c + 1)
                for m in range(2 * KT):
                    ins = act.activation(r[:, m, :], f_ps[m][:, 0:CHUNK], ACT.Relu, bias=b1[:, m:m + 1])
                ins.then_inc(relued, 1)
                if more:
                    exps(c + 2, slot)
            exps(0, 0)
            exps(1, 1)
            each_chunk(act, chunk)

        @block.vector
        def _(v):
            step = st.steps(v, chain)
            v.wait_ge(loads, 96)

            def gate_of(c, slot):
                step.turn(c, 3)
                at = ds(c * CHUNK, CHUNK)
                step(v.tensor_tensor(dif[:], HLT[:, :, at], HAT[:, :, at], ALU.subtract))
                hold(v, st.passed, exped, c * 2 + 1)
                for m in range(KT):
                    x = g_ps[m][:, 0:CHUNK]
                    ins = v.scalar_tensor_tensor(gate[:, slot, m, :], x, 0.0, gate[:, slot, m, :], ALU.min, ALU.subtract)
                ins.then_inc(asked, 1)
                hold(v, st.passed, exped, c * 2 + 2)
                step(v.tensor_tensor(dif[:], dif[:], gate[:, slot], ALU.mult))

            def mix(c, slot):
                step(v.tensor_tensor(h[:, slot], dif[:], HAT[:, :, ds(c * CHUNK, CHUNK)], ALU.add))
                step.end_turn()
                v.sem_inc(mixed, 1)

            def chunk(c, slot, more):
                if more:
                    gate_of(c + 2, slot)
                hold(v, st.passed, made, c + 1)
                for m in range(KT):
                    ins = v.scalar_tensor_tensor(VT[:, m, ds(c * CHUNK, CHUNK)], o_ps[m][:, 0:CHUNK], b2[:, m:m + 1], h[:, slot, m, :], ALU.add, ALU.add)
                ins.then_inc(out, 1)
                if more:
                    hold(v, st.passed, out, c + 2)
                    mix(c + 2, slot)
            v.sem_inc(out, 1)
            for c in range(2):
                gate_of(c, c)
                mix(c, c)
            each_chunk(v, chunk)


def add_stage(nc, st, X, V):
    done = st.sem("done")
    with st.block() as block:
        @block.vector
        def _(v):
            v.tensor_tensor(X[:], X[:], V[:], ALU.add).then_inc(done, 1)
            v.wait_ge(done, 1)


def experts_stage(nc, st, C, A, XT, X):
    LOT = 4 * P
    LOTS = ROWS // LOT
    w1, w2, wo = (st.sb(n, [P, EXPERTS, KT, DIM]) for n in ("w1", "w2", "wo"))
    wr, br, bo = st.sb("wr", [P, KT, EXPERTS]), st.sb("br", [P, EXPERTS]), st.sb("bo", [EXPERTS, DIM])
    par = st.sb("par", [P, 2, 5, EXPERTS * KT])
    scale, shift = st.sb("scale", [P, 2, EXPERTS * KT]), st.sb("shift", [P, 2, EXPERTS * KT])
    eps = st.sb("eps", [P, 1])
    xt = st.sb("xt", [P, 2, KT, LOT])
    h1, h2 = st.sb("h1", [P, 2, KT, LOT]), st.sb("h2", [P, 2, KT, LOT])
    share, top = st.sb("share", [P, 2, 4, EXPERTS]), st.sb("top", [P, 4])
    shareT = st.sb("shareT", [EXPERTS, 4, P])
    p1 = [st.ps(f"p1{m}", [P, 512]) for m in range(KT)]
    p2 = [st.ps(f"p2{m}", [P, 512]) for m in range(KT)]
    y_ps = [st.ps(f"y_ps{i}", [P, 2, DIM]) for i in range(2)]
    r_ps = st.ps("r_ps", [P, 4, EXPERTS])
    t_ps = st.ps("t_ps", [EXPERTS, 4, P])
    loads, chain, folded, sqrts, brought, routed, shifted, exped, shared, turned, turned_out = (st.sem(n) for n in (
        "loads", "chain", "folded", "sqrts", "brought", "routed", "shifted", "exped", "shared", "turned", "turned_out"))
    made1, out1, made2, out2, made3, added, lot_done = (st.sem(n) for n in ("made1", "out1", "made2", "out2", "made3", "added", "lot_done"))

    def each_lot(eng, body):
        body(0, 4, 0)
        body(1, 4, 1)
        with eng.Fori(1, LOTS // 2) as i:
            body(i * 2, 4, 0)
            body(i * 2 + 1, 4, 1)
        body(LOTS, TILES - 4 * LOTS, 0)

    w_in = [st.sem(f"w{n}_in") for n in (1, 2, 3)]
    with st.block() as block:
        @block.sync
        def _(sp):
            sp.dma_start(wr[:], A["L1_ffn_Wr"].rearrange("(k p) n -> p k n", p=P)).then_inc(loads, 16)
            sp.dma_start(br[:], A["L1_ffn_br"].partition_broadcast(P)).then_inc(loads, 16)
            sp.dma_start(bo[:], A["L1_ffn_bo"]).then_inc(loads, 16)
            for n in range(2):
                for i, name in enumerate(("b", "g", "be", "m", "v")):
                    sp.dma_start(par[:, n, i, :], A[f"L1_ffn_{name}{n + 1}"]).then_inc(loads, 16)
            for sem, tile, name in zip(w_in, (w1, w2, wo), ("W1", "W2", "Wo")):
                sp.dma_start(tile[:], A[f"L1_ffn_{name}"].rearrange("e (k p) n -> p e k n", p=P)).then_inc(sem, 16)
            sp.wait_ge(loads, 13 * 16)
            for sem in w_in:
                sp.wait_ge(sem, 16)

        @block.gpsimd
        def _(pool):
            def bring(q, tiles, slot):
                if not isinstance(q, int) or q >= 2:
                    hold(pool, st.passed, lot_done, q - 1)
                for k in range(KT):
                    ins = pool.tensor_copy(xt[:, slot, k, 0:tiles * P], XT[:, k, ds(q * LOT, tiles * P)])
                ins.then_inc(brought, 1)
            each_lot(pool, bring)

        @block.tensor
        def _(pe):
            pe.wait_ge(loads, 13 * 16)
            pe.wait_ge(w_in[0], 16)
            pe.wait_ge(folded, 2)

            def lot(q, tiles, slot):
                n = tiles * P
                e0 = q * EXPERTS
                hold(pe, st.passed, brought, q + 1)
                for t in range(tiles):
                    for k in range(KT):
                        ins = pe.matmul(r_ps[:, t, :], xt[:, slot, k, t * P:(t + 1) * P], wr[:, k, :], start=(k == 0), stop=(k == KT - 1))
                ins.then_inc(routed, 1)

                def first(e):
                    if e:
                        hold(pe, st.passed, out1, e0 + e)
                    for m in range(KT):
                        for k in range(KT):
                            ins = pe.matmul(p1[m][:, 0:n], w1[:, e, k, m * P:(m + 1) * P], xt[:, slot, k, 0:n], start=(k == 0), stop=(k == KT - 1))
                    ins.then_inc(made1, 1)

                def second(e):
                    hold(pe, st.passed, out1, e0 + e + 1)
                    if e:
                        hold(pe, st.passed, out2, e0 + e)
                    for m in range(KT):
                        for k in range(KT):
                            ins = pe.matmul(p2[m][:, 0:n], w2[:, e, k, m * P:(m + 1) * P], h1[:, e % 2, k, 0:n], start=(k == 0), stop=(k == KT - 1))
                    ins.then_inc(made2, 1)

                def third(e):
                    hold(pe, st.passed, out2, e0 + e + 1)
                    hold(pe, st.passed, added, q * (EXPERTS + 1) + e + 1)
                    for t in range(tiles):
                        for k in range(KT):
                            ins = pe.matmul(y_ps[t // 2][:, t % 2, :], h2[:, e % 2, k, t * P:(t + 1) * P], wo[:, e, k, :], start=(k == 0), stop=(k == KT - 1))
                    ins.then_inc(made3, 1)
                first(0)
                first(1)
                hold(pe, st.passed, shared, q + 1)
                for t in range(tiles):
                    ins = pe.transpose(t_ps[:, t, :], share[:, slot, t, :], C["ident"][:])
                ins.then_inc(turned, 1)
                pe.wait_ge(w_in[1], 16)
                second(0)
                pe.wait_ge(w_in[2], 16)
                hold(pe, st.passed, turned_out, q + 1)
                if not isinstance(q, int) or q:
                    hold(pe, st.passed, added, q * (EXPERTS + 1))
                for t in range(tiles):
                    ins = pe.matmul(y_ps[t // 2][:, t % 2, :], shareT[:, t, :], bo[:], start=True, stop=True)
                ins.then_inc(made3, 1)
                for e in range(EXPERTS):
                    if e + 2 < EXPERTS:
                        first(e + 2)
                    if e + 1 < EXPERTS:
                        second(e + 1)
                    third(e)
            each_lot(pe, lot)

        @block.scalar
        def _(act):
            act.wait_ge(folded, 1)
            act.activation(scale[:], scale[:], ACT.Sqrt).then_inc(sqrts, 1)
            act.wait_ge(folded, 2)

            def lot(q, tiles, slot):
                n = tiles * P
                e0 = q * EXPERTS

                def relu(made, out, ps, h, layer, e):
                    hold(act, st.passed, made, e0 + e + 1)
                    for m in range(KT):
                        col = slice(e * KT + m, e * KT + m + 1)
                        ins = act.activation(h[:, e % 2, m, 0:n], ps[m][:, 0:n], ACT.Relu, bias=shift[:, layer, col], scale=scale[:, layer, col])
                    ins.then_inc(out, 1)
                hold(act, st.passed, shifted, q + 1)
                act.activation(share[:, slot, 0:tiles, :], share[:, slot, 0:tiles, :], ACT.Exp).then_inc(exped, 1)
                relu(made1, out1, p1, h1, 0, 0)
                relu(made1, out1, p1, h1, 0, 1)
                relu(made2, out2, p2, h2, 1, 0)
                for e in range(EXPERTS):
                    if e + 2 < EXPERTS:
                        relu(made1, out1, p1, h1, 0, e + 2)
                    if e + 1 < EXPERTS:
                        relu(made2, out2, p2, h2, 1, e + 1)
            each_lot(act, lot)

        @block.vector
        def _(v):
            step = st.steps(v, chain)
            step(v.memset(eps[:], 1.0e-3))
            v.wait_ge(loads, 13 * 16)
            for n in range(2):
                step(v.tensor_scalar(scale[:, n, :], par[:, n, 4, :], eps[:], None, ALU.add))
                step(v.tensor_tensor(shift[:, n, :], par[:, n, 0, :], par[:, n, 3, :], ALU.subtract))
            v.sem_inc(folded, 1)
            v.wait_ge(sqrts, 1)
            step(v.reciprocal(scale[:], scale[:]))
            step(v.tensor_tensor(scale[:], scale[:], par[:, :, 1, :], ALU.mult))
            step(v.tensor_tensor(shift[:], shift[:], scale[:], ALU.mult))
            step(v.tensor_tensor(shift[:], shift[:], par[:, :, 2, :], ALU.add))
            v.sem_inc(folded, 1)

            def lot(q, tiles, slot):
                step.turn(q, 5 + EXPERTS)
                sh = share[:, slot, 0:tiles, :]
                hold(v, st.passed, routed, q + 1)
                step(v.tensor_tensor(sh, r_ps[:, 0:tiles, :], br[:].unsqueeze(1).to_broadcast([P, tiles, EXPERTS]), ALU.add))
                step(v.tensor_reduce(top[:, 0:tiles], sh, AX_X, ALU.max))
                v.tensor_tensor(sh, sh, top[:, 0:tiles].unsqueeze(2).to_broadcast([P, tiles, EXPERTS]), ALU.subtract).then_inc(shifted, 1)
                hold(v, st.passed, exped, q + 1)
                step(v.tensor_reduce(top[:, 0:tiles], sh, AX_X, ALU.add))
                step.hold(v.reciprocal(top[:, 0:tiles], top[:, 0:tiles]))
                step(v.tensor_tensor(sh, sh, top[:, 0:tiles].unsqueeze(2).to_broadcast([P, tiles, EXPERTS]), ALU.mult))
                v.sem_inc(shared, 1)
                hold(v, st.passed, turned, q + 1)
                v.tensor_copy(shareT[:, 0:tiles, :], t_ps[:, 0:tiles, :]).then_inc(turned_out, 1)
                for e in range(-1, EXPERTS):
                    hold(v, st.passed, made3, q * (EXPERTS + 1) + e + 2)
                    for t in range(tiles):
                        row = X[:, ds(q * 4 + t, 1), :].rearrange("p a d -> p (a d)")
                        if e < 0:
                            ins = v.tensor_tensor(row, row, y_ps[t // 2][:, t % 2, :], ALU.add)
                        else:
                            ins = v.scalar_tensor_tensor(row, y_ps[t // 2][:, t % 2, :], share[:, slot, t, e:e + 1], row, ALU.mult, ALU.add)
                    if e < EXPERTS - 1:
                        step(ins)
                        v.sem_inc(added, 1)
                    else:
                        ins.then_inc(added, 1)
                v.sem_inc(lot_done, 1)
                step.end_turn()
            each_lot(v, lot)


def program(nc, A, out):
    def dram(name, shape, dt=F32):
        return nc.dram_tensor(name, shape, dt).ap()

    D = {
        "key": dram("key_d", (ROWS,)), "table": dram("table_d", (ROWS, HROW)), 
        "ed": dram("ed_d", (ROWS, HEADS)), "by_edge": dram("by_edge_d", (P * STREAM, HEADS)), 
        "ordered": dram("ordered_d", (ROWS, DIM)), "x": dram("x_d", (ROWS, DIM)), "z": dram("z_d", (ROWS, DIM)),
        "hl": dram("hl_d", (ROWS, DIM)), "bc": dram("bc_d", (2 * STATES, ROWS)), "y": dram("y_d", (ROWS, DIM)),
        "sums": dram("sums_d", (P * STREAM, HROW)),
    }
    with ExitStack() as whole:
        def keep(name, shape, dt=F32):
            return whole.enter_context(nc.sbuf_tensor(name, shape, dt))
        C = {
            "src_idx": keep("src_idx", [P, STREAM], I32), "dst_idx": keep("dst_idx", [P, STREAM], I32),
            "ones": keep("ones", [P, P]), "zero_row": keep("zero_row", [P, P]), "eps5": keep("eps5", [P, 1]), "ident": keep("ident", [P, P]),
            "above": keep("above", [P, P]), "below": keep("below", [P, P]), "carry": keep("carry", [P, P]),
            "not_after": keep("not_after", [P, P]), "not_before": keep("not_before", [P, P]),
            "same_prev": keep("same_prev", [P, STREAM]), "same_next": keep("same_next", [P, STREAM]),
            "cut_prev": keep("cut_prev", [P, STREAM]), "cut_next": keep("cut_next", [P, STREAM]),
            "ends_in": keep("ends_in", [P, 1]), "dst_first": keep("dst_first", [P, 1]),
            "last_edge": keep("last_edge", [P, TILES], I32), "first_edge": keep("first_edge", [P, TILES], I32),
            "has_edge": keep("has_edge", [P, TILES]), "rank": keep("rank", [P, TILES], I32),
            "carried": keep("carried", [P, HROW + 1]), "tile_start": keep("tile_start", [P, TILES]),
        }
        passed = whole.enter_context(nc.semaphore("passed"))

        def lasting(name):
            return Lasting(whole.enter_context(nc.semaphore(name)))
        C["arrived"] = [[lasting(f"arrived{s}{u}") for u in range(GROUP)] for s in range(RING)]
        C["placed"], C["ed_in"] = lasting("placed"), lasting("ed_in")

        def stage(name, f, *args):
            with ExitStack() as ctx:
                st = Stage(nc, ctx, name, passed)
                f(nc, st, *args)
                st.end()

        @contextmanager
        def together(*names):
            with ExitStack() as ctx:
                with nc.Block() as block:
                    stages = [Stage(nc, ctx, name, passed, block) for name in names]
                    yield stages
                for st in stages:
                    for sem in st.sems:
                        nc.gpsimd.sem_clear(sem)
                nc.all_engine_barrier()

        def graph_layer(name, rows, XN, XT, W, a_src, a_dst, out_rows, base, bias, global_top, beside):
            with ExitStack() as ctx:
                ed = ctx.enter_context(nc.sbuf_tensor(f"{name}_ed", [P, STREAM, HEADS], F32))
                with ExitStack() as inner:
                    esd = inner.enter_context(nc.sbuf_tensor(f"{name}_esd", [P, TILES, 2 * HEADS], F32))
                    with together(f"{name}_norm", f"{name}_table", f"{name}_beside", f"{name}_scores") as (n, t, b, e):
                        rows_ready, xt_ready, esd_ready, ed_stored = (n.sem(k) for k in ("rows_ready", "xt_ready", "esd_ready", "ed_stored"))
                        norm_stage(nc, n, C, rows, XN, XT, BANKS=2, rows_ready=rows_ready, ready=xt_ready)
                        table_stage(nc, t, C, D, XT, W, a_src, a_dst, esd, xt_ready, esd_ready, ed_stored)
                        known = beside(b, rows_ready)
                        scores_stage(nc, e, C, D, esd, ed, known, esd_ready, ed_stored)
                stage(f"{name}_sum", sum_stage, C, D, ed)
            stage(f"{name}_nodes", nodes_stage, C, D, out_rows, base, bias, global_top)

        def graph_beside(st, rows_ready):
            known = st.sem("known")
            graph_stage(nc, st, C, D, A, A["node_vec"], known)
            return known

        def slice_layer(XN, XT, X):
            with ExitStack() as ctx:
                w_log = ctx.enter_context(nc.sbuf_tensor("w_log", [P, KT, SLICES], F32))
                b_log = ctx.enter_context(nc.sbuf_tensor("b_log", [P, SLICES], F32))
                SWT = ctx.enter_context(nc.sbuf_tensor("SWT", [P, SLICES // P, ROWS], F32))
                Z = ctx.enter_context(nc.sbuf_tensor("Z", [P, SLICES // P, DIM + 16], F32))
                mix = ctx.enter_context(nc.sbuf_tensor("mix", [P, SLICES // P, DIM], F32))
                stage("slice_w", slice_weights_stage, C, A, w_log, b_log)
                stage("assign", assign_stage, C, XN, XT, w_log, b_log, SWT, Z)
                stage("slice_a", slice_attention_stage, C, A, Z, mix)
                stage("mix", mix_stage, C, A, SWT, mix, X)

        def rows_of(ctx, name):
            return ctx.enter_context(nc.sbuf_tensor(name, [P, TILES, DIM], F32))

        def columns_of(ctx, name, extra=0):
            return ctx.enter_context(nc.sbuf_tensor(name, [P, KT, ROWS + extra], F32))

        with ExitStack() as ctx:
            X, XN = rows_of(ctx, "X"), rows_of(ctx, "XN")
            stage("constants", constants_stage, C, A, X, A["x"], A["src"], A["dst"])
            with ExitStack() as inner:
                XT = columns_of(inner, "XT")
                graph_layer("g0", X, XN, XT, A["L0_gnn_W"], A["L0_gnn_a_src"], A["L0_gnn_a_dst"], X, X, None, False, graph_beside)
                stage("norm1", norm_stage, C, X, XN, XT)
                slice_layer(XN, XT, X)
            HL = rows_of(ctx, "HL")
            with ExitStack() as inner:
                XT = columns_of(inner, "XT2")
                graph_layer("g1", X, XN, XT, A["L1_gnn_gat_w"], A["L1_gnn_gat_a_src"], A["L1_gnn_gat_a_tgt"], HL, XN, A["L1_gnn_gat_b"], True,
                            lambda st, rows_ready: spread_rows_stage(nc, st, C, D, XN, X, rows_ready))
            stage("elu", elu_stage, C, D, HL)
        with ExitStack() as ctx:
            XC, GATE, RAW, DT = columns_of(ctx, "XC"), columns_of(ctx, "GATE"), columns_of(ctx, "RAW", TAPS - 1), columns_of(ctx, "DT")
            stage("ordered", ordered_stage, C, D, DT)
            stage("in_proj", in_proj_stage, C, A, DT, RAW, GATE)
            stage("conv", conv_stage, C, A, RAW, XC)
            U = RAW[:, :, 0:ROWS]
            stage("x_proj", x_proj_stage, C, A, D, XC, DT, U)
            stage("scan", scan_stage, C, A, D, XC, DT, U, GATE)
            stage("out_proj", out_proj_stage, C, A, D, XC)
        with ExitStack() as ctx:
            X = rows_of(ctx, "X2")
            with ExitStack() as inner:
                HLT, HAT = columns_of(inner, "HLT"), columns_of(inner, "HAT")
                with ExitStack() as rows:
                    HL, HA = rows_of(rows, "HL2"), rows_of(rows, "HA")
                    with together("collect", "norm_l", "norm_g") as (c, l, g):
                        hl_ready, ha_ready = c.sem("hl_ready"), c.sem("ha_ready")
                        norm_stage(nc, l, C, HL, None, HLT, A["L1_gnn_ln_local_g"], A["L1_gnn_ln_local_b"], after=(hl_ready, 16))
                        collect_rows_stage(nc, c, C, D, X, HL, HA, hl_ready, ha_ready)
                        norm_stage(nc, g, C, HA, None, HAT, A["L1_gnn_ln_global_g"], A["L1_gnn_ln_global_b"], after=(ha_ready, 1))
                VT = columns_of(inner, "VT")
                stage("gate_ff", gate_ff_stage, C, A, HLT, HAT, VT)
                V = rows_of(inner, "V")
                with together("turn", "norm3") as (t, n):
                    turned = t.sem("done")
                    turn_stage(nc, t, C, VT, V, turned)
                    norm_stage(nc, n, C, V, V, None, A["L1_gnn_ln2_g"], A["L1_gnn_ln2_b"], after=(turned, -(-TILES // 2)))
                stage("add", add_stage, X, V)
            XT = columns_of(ctx, "XT3")
            stage("norm4", norm_stage, C, X, None, XT)
            stage("experts", experts_stage, C, A, XT, X)
            finish_stage(nc, C, A, X, out, ctx)


def finish_stage(nc, C, A, X, out, ctx):
    stored = ctx.enter_context(nc.semaphore("out_stored"))
    whole = NODES // P
    with nc.Block() as block:
        @block.sync
        def _(sp):
            sp.dma_start(out[0:whole * P, :].rearrange("(t p) d -> p t d", p=P), X[:, 0:whole, :]).then_inc(stored, 16)
            sp.dma_start(out[whole * P:NODES, :], X[0:NODES - whole * P, whole, :]).then_inc(stored, 16)
            sp.wait_ge(stored, 32)


_TURNED = ("L0_ffn_W_x", "L1_gnn_gat_w", "L1_gnn_in_proj_w", "L1_gnn_x_proj_w", "L1_gnn_dt_proj_w", "L1_gnn_out_proj_w", "L1_gnn_wl",
           "L1_gnn_wg", "L1_gnn_ff1_w", "L1_gnn_ff2_w")


def kernel(**inputs):
    import numpy as np
    import concourse.bacc as bacc
    from concourse.bass_utils import run_bass_kernel_spmd

    nc = bacc.Bacc("TRN2", target_bir_lowering=False, num_devices=1)
    arrays = {}
    for name, value in inputs.items():
        a = np.asarray(value)
        if name in _TURNED:
            a = a.T
        arrays[name] = np.ascontiguousarray(a)
    del arrays["edge_weight"]
    arrays["L0_ffn_b_x"] = np.ascontiguousarray(arrays["L0_ffn_b_x"].reshape(SH, SD).T)
    for name in ("ln_local_g", "ln_local_b", "ln_global_g", "ln_global_b", "conv_b", "dt_proj_b", "D_param", "ff1_b", "ff2_b"):
        a = arrays[f"L1_gnn_{name}"]
        arrays[f"L1_gnn_{name}"] = np.ascontiguousarray(a.reshape(-1, P).T)
    for name in ("b", "g", "be", "m", "v"):
        for n in (1, 2):
            a = arrays[f"L1_ffn_{name}{n}"]
            arrays[f"L1_ffn_{name}{n}"] = np.ascontiguousarray(a.reshape(-1, P).T)
    x = np.zeros((ROWS, DIM), arrays["x"].dtype)
    x[:NODES] = arrays["x"]
    arrays["x"] = x
    noise = np.zeros((ROWS,), arrays["node_vec"].dtype)
    noise[:NODES] = arrays["node_vec"]
    arrays["node_vec"] = noise
    for name in ("src", "dst"):
        e = np.full((P * STREAM,), NODES, np.int32)
        e[:EDGES] = arrays[name]
        arrays[name] = e.reshape(P, STREAM)
    arrays["minus_one"] = np.full((1, 2), -1, np.int32)
    arrays["tile_starts"] = (np.arange(TILES, dtype=np.float32) * P)[None, :]
    A = {name: nc.dram_tensor(f"in_{name}", a.shape, mybir.dt.from_np(a.dtype), kind="ExternalInput").ap() for name, a in arrays.items()}
    out = nc.dram_tensor("out_0", (NODES, DIM), mybir.dt.float32, kind="ExternalOutput").ap()
    program(nc, A, out)
    result = run_bass_kernel_spmd(nc, [{f"in_{name}": a for name, a in arrays.items()}], core_ids=[0])
    return result.results[0]["out_0"]
```

```python
from contextlib import ExitStack, contextmanager

import concourse.bass as bass
from concourse import mybir

P = 128
NODES, DIM = 3125, 256
EDGES = 53125
TILES = -(-NODES // P)
ROWS = TILES * P
STREAM = -(-EDGES // (P * 16)) * 16
HEADS, HD = 4, 64
HSUM = HEADS * (HD + 1)
HROW = HSUM + HEADS
GROUP = 8
RING = 4
GROUPS = STREAM // GROUP
CHUNK = 400
CHUNKS = ROWS // CHUNK
KT = DIM // P
SH, SD = 8, 64
SLICES = SH * SD
TAPS, RANK, STATES, SPANS = 4, 16, 16, 2
EXPERTS = 8
BIG = 1.0e30
FAR = 200000.0

ALU = mybir.AluOpType
ACT = mybir.ActivationFunctionType
F32 = mybir.dt.float32
BF16 = mybir.dt.bfloat16
I32 = mybir.dt.int32
AX_X = mybir.AxisListType.X
RMAX = bass.bass_isa.ReduceOp.max
ds = bass.ds


class Steps:

    def __init__(self, eng, sem, passed):
        self.per, self.looping = 0, False
        self.eng, self.sem, self.passed, self.base, self.n, self.offset = eng, sem, passed, 0, 0, 0

    def turn(self, t, per):
        if not self.looping:
            self.base, self.looping = self.base + self.n, True
        self.offset, self.n, self.per = t * per, 0, per

    def end_turn(self):
        assert self.n == self.per, (self.n, self.per)

    def end_loop(self, turns):
        self.base, self.offset, self.n, self.looping = self.base + turns * self.per, 0, 0, False

    def did(self, ins):
        ins.then_inc(self.sem, 1)
        self.n += 1

    def wait(self):
        self.eng.wait_ge(self.sem, self.offset + (self.base + self.n))

    def __call__(self, ins):
        self.did(ins)
        self.wait()

    def hold_last(self, but=0):
        hold(self.eng, self.passed, self.sem, self.offset + (self.base + self.n - but))

    def hold(self, ins):
        self.did(ins)
        hold(self.eng, self.passed, self.sem, self.offset + (self.base + self.n))


def hold(eng, passed, sem, value):
    eng.wait_ge(sem, value)
    eng.sem_inc(passed, 1)


def each_tile(eng, body):
    body(0, 0, True)
    body(1, 1, True)
    with eng.Fori(1, TILES // 2) as i:
        body(i * 2, 0, False)
        body(i * 2 + 1, 1, False)
    if TILES % 2:
        body(TILES - 1, 0, False)


def each_group(eng, groups, body):
    body(0, 0, True)
    body(1, 1, True)
    with eng.Fori(1, groups // 2) as i:
        body(i * 2, 0, False)
        body(i * 2 + 1, 1, False)


class Lasting:

    def __init__(self, sem):
        self.sem, self.base = sem, 0


class Stage:

    def __init__(self, nc, ctx, name, passed, shared=None):
        self.nc, self.ctx, self.name, self.passed, self.sems, self.shared = nc, ctx, name, passed, [], shared

    @contextmanager
    def block(self):
        if self.shared is not None:
            yield self.shared
        else:
            with self.nc.Block() as block:
                yield block

    def sb(self, name, shape, dt=F32):
        return self.ctx.enter_context(self.nc.sbuf_tensor(f"{self.name}_{name}", shape, dt))

    def ps(self, name, shape, dt=F32):
        return self.ctx.enter_context(self.nc.psum_tensor(f"{self.name}_{name}", shape, dt))

    def sem(self, name):
        sem = self.ctx.enter_context(self.nc.semaphore(f"{self.name}_{name}"))
        self.sems.append(sem)
        return sem

    def end(self):
        for sem in self.sems:
            self.nc.gpsimd.sem_clear(sem)
        self.nc.all_engine_barrier()

    def steps(self, eng, sem):
        return Steps(eng, sem, self.passed)


def constants_stage(nc, st, C, G, X, x, src, dst):
    load, made = st.sem("load"), st.sem("made")
    with st.block() as block:
        @block.sync
        def _(sp):
            sp.dma_start(X[:], x.rearrange("(t p) d -> p t d", p=P)).then_inc(load, 16)
            sp.dma_start(C["src_idx"][:], src).then_inc(load, 16)
            sp.dma_start(C["dst_idx"][:], dst).then_inc(load, 16)
            sp.dma_start(C["tile_start"][:], G["tile_starts"].rearrange("a t -> (a t)").partition_broadcast(P)).then_inc(load, 16)
            sp.wait_ge(load, 64)

        @block.gpsimd
        def _(pool):
            step = st.steps(pool, made)
            pool.memset(C["ones"][:], 1.0)
            pool.memset(C["eps5"][:], 1.0e-5)
            step(pool.memset(C["ident"][:], 0.0))
            step(pool.affine_select(out=C["ident"][:], in_=C["ident"][:], compare_op=ALU.not_equal, fill=1.0,
                                    base=0, pattern=[[-1, P]], channel_multiplier=1))
            step(pool.affine_select(out=C["above"][:], in_=C["ones"][:], compare_op=ALU.is_gt, fill=0.0,
                                    base=0, pattern=[[1, P]], channel_multiplier=-1))
            step(pool.affine_select(out=C["below"][:], in_=C["ones"][:], compare_op=ALU.is_gt, fill=0.0,
                                    base=0, pattern=[[-1, P]], channel_multiplier=1))


def norm_stage(nc, st, C, src, XN=None, XT=None, gain=None, shift=None, BANKS=4, after=None, ready=None):
    SLOTS, SPAN = 4, 2
    raw, mv = st.sb("raw", [P, TILES, 6]), st.sb("mv", [P, TILES, 2])
    rstd, std = st.sb("rstd", [P, TILES]), st.sb("std", [P, TILES])
    rows = XN if XN is not None else st.sb("rows", [P, SLOTS, DIM])
    slot_of = lambda t: t if XN is not None else t % SLOTS
    affine = gain is not None
    assert not (affine and XN is not None and XT is not None)
    if affine:
        extent = [P, DIM] if XN is not None else [P, KT]
        gain_row, shift_row = st.sb("gain_row", extent), st.sb("shift_row", extent)
    pt = [st.ps(f"pt{i}", [P, KT, SPAN, P]) for i in range(BANKS)] if XT is not None else None
    chain, stats, means, std_ok, loads, normed, turned = (st.sem(n) for n in (
        "chain", "stats", "means", "std_ok", "loads", "normed", "turned"))
    copied = ready if ready is not None else st.sem("copied")
    spans = [(t, min(SPAN, TILES - t)) for t in range(0, TILES, SPAN)]
    with st.block() as block:
        @block.sync
        def _(sp):
            if affine:
                sp.dma_start(gain_row[:], gain.partition_broadcast(P) if XN is not None else gain).then_inc(loads, 16)
                sp.dma_start(shift_row[:], shift.partition_broadcast(P) if XN is not None else shift).then_inc(loads, 16)
                sp.wait_ge(loads, 32)

        @block.vector
        def _(v):
            step = st.steps(v, chain)
            if after is not None:
                v.wait_ge(*after)
            for t in range(TILES):
                v.bn_stats(raw[:, t, :], src[:, t, :]).then_inc(stats, 1)
            for t in range(TILES):
                v.wait_ge(stats, t + 1)
                v.bn_aggr(mv[:, t, :], raw[:, t, :]).then_inc(means, 1)
            v.wait_ge(std_ok, 1)
            step(v.reciprocal(rstd[:], std[:]))
            for t in range(TILES):
                if XN is None and t >= SLOTS:
                    v.wait_ge(turned, t - SLOTS + 1)
                v.tensor_scalar(rows[:, slot_of(t), :], src[:, t, :], mv[:, t, 0:1], rstd[:, t:t + 1], ALU.subtract, ALU.mult).then_inc(normed, 1)
            if affine and XN is not None:
                v.wait_ge(loads, 32)
                v.wait_ge(normed, TILES)
                step(v.tensor_tensor(XN[:], XN[:], gain_row[:].unsqueeze(1).to_broadcast([P, TILES, DIM]), ALU.mult))
                step(v.tensor_tensor(XN[:], XN[:], shift_row[:].unsqueeze(1).to_broadcast([P, TILES, DIM]), ALU.add))

        @block.scalar
        def _(act):
            act.wait_ge(means, TILES)
            act.activation(std[:], mv[:, :, 1], ACT.Sqrt, bias=C["eps5"][:]).then_inc(std_ok, 1)
            if XT is None:
                return
            if affine:
                act.wait_ge(loads, 32)
            for n, (t, tiles) in enumerate(spans):
                act.wait_ge(turned, t + tiles)
                bank, cols = pt[n % BANKS], slice(t * P, (t + tiles) * P)
                if affine:
                    for k in range(KT):
                        ins = act.activation(XT[:, k, cols], bank[:, k, 0:tiles, :].rearrange("p s n -> p (s n)"), ACT.Identity,
                                             scale=gain_row[:, k:k + 1], bias=shift_row[:, k:k + 1])
                else:
                    ins = act.activation(XT[:, :, cols], bank[:, :, 0:tiles, :].rearrange("p k s n -> p k (s n)"), ACT.Copy)
                ins.then_inc(copied, 1)

        @block.tensor
        def _(pe):
            if XT is None:
                return
            for n, (t0, tiles) in enumerate(spans):
                if n >= BANKS:
                    pe.wait_ge(copied, n - BANKS + 1)
                for i in range(tiles):
                    pe.wait_ge(normed, t0 + i + 1)
                    for k in range(KT):
                        ins = pe.transpose(pt[n % BANKS][:, k, i, :], rows[:, slot_of(t0 + i), k * P:(k + 1) * P], C["ident"][:])
                    ins.then_inc(turned, 1)


def turn_stage(nc, st, C, XT, rows_out, done):
    BANKS, SPAN = 4, 2
    pt = [st.ps(f"pt{i}", [P, SPAN, KT, P]) for i in range(BANKS)]
    turned = st.sem("turned")
    spans = [(t, min(SPAN, TILES - t)) for t in range(0, TILES, SPAN)]
    with st.block() as block:
        @block.tensor
        def _(pe):
            for n, (t0, tiles) in enumerate(spans):
                if n >= BANKS:
                    pe.wait_ge(done, n - BANKS + 1)
                for i in range(tiles):
                    for k in range(KT):
                        ins = pe.transpose(pt[n % BANKS][:, i, k, :], XT[:, k, (t0 + i) * P:(t0 + i + 1) * P], C["ident"][:])
                ins.then_inc(turned, 1)

        @block.scalar
        def _(act):
            for n, (t0, tiles) in enumerate(spans):
                act.wait_ge(turned, n + 1)
                act.activation(rows_out[:, t0:t0 + tiles, :], pt[n % BANKS][:, 0:tiles].rearrange("p s k n -> p s (k n)"), ACT.Copy).then_inc(done, 1)


def graph_stage(nc, st, C, D, G, node_vec, known):
    lo = {k: st.sb(f"{k}_lo", [P, STREAM], I32) for k in ("src", "dst")}
    hi = {k: st.sb(f"{k}_hi", [P, STREAM], I32) for k in ("src", "dst")}
    lo16 = {k: st.sb(f"{k}_lo16", [P, STREAM], BF16) for k in ("src", "dst")}
    hi16 = {k: st.sb(f"{k}_hi16", [P, STREAM], BF16) for k in ("src", "dst")}
    iota16 = st.sb("iota16", [P, P], BF16)
    iota32 = st.sb("iota32", [P, P], I32)
    hot_lo = {k: st.sb(f"{k}_hot_lo", [P, 2, GROUP, P], BF16) for k in ("src", "dst")}
    hot_hi = {k: st.sb(f"{k}_hot_hi", [P, 2, GROUP, TILES], BF16) for k in ("src", "dst")}
    zero16 = st.sb("zero16", [P, P], BF16)
    hist_ps = {k: st.ps(f"{k}_hist_ps", [TILES, P]) for k in ("src", "dst")}
    tab = st.sb("tab", [TILES, 4, P])
    count = st.sb("count", [TILES, P])
    cum = st.sb("cum", [TILES, P])
    none = st.sb("none", [TILES, P])
    off = st.sb("off", [TILES, 1])
    noise = st.sb("noise", [TILES, P])
    small_ps = st.ps("small_ps", [P, 512])
    off_ps, tab_ps, row_ps = small_ps[0:TILES, 0:1], small_ps[:, 128:256].rearrange("p (a t) -> p a t", a=4), small_ps[:, 256:384]
    tabT = st.sb("tabT", [P, 4, TILES])
    dst_next = st.sb("dst_next", [P, 2], I32)
    edge3 = st.sb("edge3", [P, 3])
    spread = st.sb("spread", [P, P])
    gt = st.sb("gt", [P, P])
    loads, chain, setup, hots, used, counted = (st.sem(n) for n in ("loads", "chain", "setup", "hots", "used", "counted"))
    pe_done, keys, stored, iotas = (st.sem(n) for n in ("pe_done", "keys", "stored", "iotas"))
    dve_done = st.sem("dve_done")
    with st.block() as block:
        @block.sync
        def _(sp):
            sp.dma_start(noise[:], node_vec.rearrange("(t p) -> t p", p=P)).then_inc(loads, 16)
            sp.dma_start(dst_next[0:P - 1, :], G["dst"][1:P, 0:2]).then_inc(loads, 16)
            sp.dma_start(dst_next[P - 1:P, :], G["minus_one"]).then_inc(loads, 16)
            sp.wait_ge(keys, 1)
            sp.dma_start(D["key"].rearrange("(t p) -> t p", p=P), tab[:, 3, :]).then_inc(stored, 16)
            sp.wait_ge(stored, 16)

        @block.gpsimd
        def _(pool):
            pool.iota(iota32[:], [[1, P]], base=0, channel_multiplier=0).then_inc(iotas, 1)
            pool.wait_ge(dve_done, 1)
            pool.affine_select(out=tab[:, 3, :], in_=tab[:, 3, :], compare_op=ALU.is_ge, fill=3.0e38,
                               base=NODES - 1, pattern=[[-1, P]], channel_multiplier=-P).then_inc(keys, 1)

        @block.vector
        def _(v):
            step = st.steps(v, chain)
            v.memset(zero16[:], 0.0).then_inc(setup, 1)
            for k in ("src", "dst"):
                v.tensor_scalar(lo[k][:], C[f"{k}_idx"][:], P - 1, None, ALU.bitwise_and)
                step(v.tensor_scalar(hi[k][:], C[f"{k}_idx"][:], 7, None, ALU.logical_shift_right))
                v.tensor_copy(hi16[k][:], hi[k][:])
                step(v.tensor_copy(lo16[k][:], lo[k][:]))
            v.wait_ge(iotas, 1)
            step(v.tensor_copy(iota16[:], iota32[:]))

            def one_hots(g, slot, first):
                if not first:
                    hold(v, st.passed, used, g - 1)
                for k in ("src", "dst"):
                    v.tensor_tensor(hot_lo[k][:, slot], lo16[k][:, ds(g * GROUP, GROUP)].unsqueeze(2).to_broadcast([P, GROUP, P]),
                                    iota16[:].unsqueeze(1).to_broadcast([P, GROUP, P]), ALU.is_equal).then_inc(hots, 1)
                    v.tensor_tensor(hot_hi[k][:, slot], hi16[k][:, ds(g * GROUP, GROUP)].unsqueeze(2).to_broadcast([P, GROUP, TILES]),
                                    iota16[:, 0:TILES].unsqueeze(1).to_broadcast([P, GROUP, TILES]), ALU.is_equal).then_inc(hots, 1)
            each_group(v, GROUPS, one_hots)
            step(v.memset(C["same_prev"][:, 0:1], 0.0))
            step(v.tensor_tensor(C["same_prev"][:, 1:STREAM], C["dst_idx"][:, 1:STREAM], C["dst_idx"][:, 0:STREAM - 1], ALU.is_equal))
            step(v.tensor_scalar(C["cut_prev"][:], C["same_prev"][:], 1.0, BIG, ALU.subtract, ALU.mult))
            step(v.memset(C["cut_prev"][:, 0:1], 0.0))
            v.wait_ge(loads, 48)
            v.tensor_copy(edge3[:, 0:1], C["dst_idx"][:, 0:1])
            v.tensor_copy(edge3[:, 1:2], C["dst_idx"][:, STREAM - 1:STREAM])
            step(v.tensor_copy(edge3[:, 2:3], dst_next[:, 0:1]))
            step(v.tensor_tensor(C["ends_in"][:], edge3[:, 2:3], edge3[:, 0:1], ALU.not_equal))
            step(v.tensor_copy(C["dst_first"][:], edge3[:, 0:1]))
            step(v.tensor_scalar(spread[:], C["ones"][:], edge3[:, 1:2], None, ALU.mult))
            v.sem_inc(setup, 1)
            v.wait_ge(counted, 1)
            v.tensor_copy(count[:], hist_ps["dst"][:])
            step(v.tensor_copy(tab[:, 3, :], hist_ps["src"][:]))
            step(v.tensor_tensor(tab[:, 3, :], tab[:, 3, :], noise[:], ALU.add))
            v.sem_inc(dve_done, 1)
            step(v.tensor_tensor_scan(cum[:], C["ones"][0:TILES, :], count[:], 0.0, ALU.mult, ALU.add))
            v.sem_inc(setup, 1)
            v.wait_ge(pe_done, 1)
            step(v.tensor_copy(off[:], off_ps[:]))
            step(v.tensor_scalar(cum[:], cum[:], off[:], None, ALU.add))
            step(v.tensor_scalar(tab[:, 0, :], cum[:], 1.0, 0.0, ALU.subtract, ALU.max))
            step(v.tensor_tensor(tab[:, 1, :], cum[:], count[:], ALU.subtract))
            step(v.tensor_scalar(none[:], count[:], 0.0, FAR, ALU.is_equal, ALU.mult))
            step(v.tensor_tensor(tab[:, 1, :], tab[:, 1, :], none[:], ALU.add))
            step(v.tensor_scalar(tab[:, 2, :], count[:], 0.0, None, ALU.is_gt))
            v.sem_inc(setup, 1)
            v.wait_ge(pe_done, 2)
            step(v.tensor_copy(tabT[:], tab_ps[:, :, 0:TILES]))
            v.tensor_copy(C["last_edge"][:], tabT[:, 0, :])
            v.tensor_copy(C["first_edge"][:], tabT[:, 1, :]).then_inc(known, 1)
            v.tensor_copy(C["has_edge"][:], tabT[:, 2, :])
            v.tensor_copy(C["key"][:], tabT[:, 3, :])
            step(v.scalar_tensor_tensor(gt[:], row_ps[:], edge3[:, 0:1], C["below"][:], ALU.is_equal, ALU.mult))
            step(v.tensor_scalar(C["not_before"][:], gt[:], 1.0, BIG, ALU.subtract, ALU.mult))

        @block.tensor
        def _(pe):
            pe.wait_ge(setup, 1)
            for k in ("src", "dst"):
                pe.matmul(hist_ps[k][:], zero16[:, 0:TILES], zero16[:], start=True, stop=False, skip_group_check=True)

            def add_counts(g, slot, first):
                hold(pe, st.passed, hots, g * 4 + 4)
                for u in range(GROUP):
                    for k in ("src", "dst"):
                        ins = pe.matmul(hist_ps[k][:], hot_hi[k][:, slot, u, :], hot_lo[k][:, slot, u, :], start=False, stop=False, skip_group_check=True)
                ins.then_inc(used, 1)
            each_group(pe, GROUPS, add_counts)
            for k in ("src", "dst"):
                ins = pe.matmul(hist_ps[k][:], zero16[:, 0:TILES], zero16[:], start=False, stop=True, skip_group_check=True)
            ins.then_inc(counted, 1)
            pe.wait_ge(setup, 3)
            pe.matmul(off_ps[:], C["above"][0:TILES, 0:TILES], cum[:, P - 1:P], start=True, stop=True).then_inc(pe_done, 1)
            pe.wait_ge(setup, 4)
            pe.wait_ge(keys, 1)
            for a in range(4):
                pe.transpose(tab_ps[:, a, 0:TILES], tab[:, a, :], C["ident"][0:TILES, 0:TILES])
            pe.matmul(row_ps[:], spread[:], C["ident"][:], start=True, stop=True).then_inc(pe_done, 1)


def key_row_stage(nc, st, D):
    key_row, back = st.sb("key_row", [P, ROWS]), st.sem("back")
    with st.block() as block:
        @block.sync
        def _(sp):
            sp.dma_start(key_row[:], D["key"].partition_broadcast(P)).then_inc(back, 16)
    return key_row, back


def rank_stage(nc, st, C, key_row, back, tiles):
    junk, rank, ties = st.sb("junk", [P, ROWS]), st.sb("rank", [P, TILES]), st.sb("ties", [P, P])
    part, chain = C["rank_parts"], st.sem("rank_chain")
    with st.block() as block:
        @block.vector
        def _(v):
            step = st.steps(v, chain)
            v.wait_ge(back, 16)
            if 0 in tiles:
                step(v.memset(part[:, 0, 0:1], 0.0))
            for i in tiles:
                own = C["key"][:, i:i + 1]
                if i:
                    step.did(v.tensor_scalar(junk[:, 0:i * P], key_row[:, 0:i * P], own, None, ALU.is_le, ALU.add, accum_out=part[:, 0, i:i + 1]))
                step.did(v.tensor_scalar(junk[:, i * P:ROWS], key_row[:, i * P:ROWS], own, None, ALU.is_lt, ALU.add, accum_out=part[:, 1, i:i + 1]))
                step(v.scalar_tensor_tensor(ties[:], key_row[:, i * P:(i + 1) * P], own, C["below"][:], ALU.is_equal, ALU.mult, accum_out=part[:, 2, i:i + 1]))
            if TILES - 1 in tiles:
                step(v.tensor_tensor(rank[:], part[:, 0, :], part[:, 1, :], ALU.add))
                step(v.tensor_tensor(rank[:], rank[:], part[:, 2, :], ALU.add))
                step(v.tensor_copy(C["rank"][:], rank[:]))


def table_stage(nc, st, C, D, XT, W, a_src, a_dst, esd, xt_ready, esd_ready, ed_stored):
    SLOTS, BANKS = 4, 2
    w_raw = st.sb("w_raw", [P, KT, DIM])
    w = st.sb("w", [P, KT, DIM + 2 * HEADS])
    a_row = st.sb("a_row", [P, 2, DIM])
    prod = st.sb("prod", [P, KT, DIM])
    rows = st.sb("rows", [P, SLOTS, HROW])
    pj = [st.ps(f"pj{i}", [P, DIM + 2 * HEADS]) for i in range(BANKS)]
    loads, chain, ready, projected = (st.sem(n) for n in ("loads", "chain", "ready", "projected"))
    copied = esd_ready
    out = [st.sem(f"out{i}") for i in range(SLOTS)]
    with st.block() as block:
        @block.sync
        def _(sp):
            sp.dma_start(w_raw[:], W.rearrange("(k p) n -> p k n", p=P)).then_inc(loads, 16)
            sp.dma_start(a_row[:, 0, :], a_src.rearrange("h d -> (h d)").partition_broadcast(P)).then_inc(loads, 16)
            sp.dma_start(a_row[:, 1, :], a_dst.rearrange("h d -> (h d)").partition_broadcast(P)).then_inc(loads, 16)
            for t in range(TILES):
                sp.wait_ge(copied, t * 3 + 3)
                sp.dma_start(D["table"][t * P:(t + 1) * P, :], rows[:, t % SLOTS, :]).then_inc(out[t % SLOTS], 16)
            sp.dma_start(D["ed"].rearrange("(t p) h -> p t h", p=P), esd[:, :, HEADS:2 * HEADS]).then_inc(ed_stored, 16)
            for slot in range(SLOTS):
                sp.wait_ge(out[slot], 16 * len(range(slot, TILES, SLOTS)))
            sp.wait_ge(ed_stored, 16)

        @block.vector
        def _(v):
            step = st.steps(v, chain)
            step(v.memset(rows[:], 1.0))
            v.wait_ge(loads, 48)
            step(v.tensor_copy(w[:, :, 0:DIM], w_raw[:]))
            for a in range(2):
                step(v.tensor_tensor(prod[:], w_raw[:], a_row[:, a:a + 1, :].to_broadcast([P, KT, DIM]), ALU.mult))
                for k in range(KT):
                    step(v.tensor_reduce(w[:, k, DIM + a * HEADS:DIM + (a + 1) * HEADS],
                                         prod[:, k, :].rearrange("p (h d) -> p h d", h=HEADS), AX_X, ALU.add))
            v.sem_inc(ready, 1)

        @block.scalar
        def _(act):
            act.wait_ge(ready, 1)
            for t in range(TILES):
                act.wait_ge(projected, t + 1)
                if t >= SLOTS:
                    act.wait_ge(out[t % SLOTS], 16 * (t // SLOTS))
                bank, row = pj[t % BANKS], rows[:, t % SLOTS, :]
                act.activation(row[:, HSUM:HROW], bank[:, DIM:DIM + HEADS], ACT.Copy).then_inc(copied, 1)
                act.activation(row[:, 0:HSUM].rearrange("p (h d) -> p h d", h=HEADS)[:, :, 0:HD], bank[:, 0:DIM].rearrange("p (h d) -> p h d", h=HEADS), ACT.Copy).then_inc(copied, 1)
                act.activation(esd[:, t, :], bank[:, DIM:DIM + 2 * HEADS], ACT.Copy).then_inc(copied, 1)

        @block.tensor
        def _(pe):
            pe.wait_ge(ready, 1)
            for t in range(TILES):
                pe.wait_ge(xt_ready, t // 2 + 1)
                if t >= BANKS:
                    pe.wait_ge(copied, 3 * (t - BANKS + 1))
                for k in range(KT):
                    ins = pe.matmul(pj[t % BANKS][:], XT[:, k, t * P:(t + 1) * P], w[:, k, :], start=(k == 0), stop=(k == KT - 1))
                ins.then_inc(projected, 1)


def clear_stage(nc, st, D, raw, zeroed):
    cleared = st.sem("cleared")
    with st.block() as block:
        @block.gpsimd
        def _(pool):
            pool.memset(raw[:], 0.0).then_inc(cleared, 1)

        @block.sync
        def _(sp):
            sp.wait_ge(cleared, 1)
            sp.dma_start(D["by_edge"].rearrange("(p j) h -> p (j h)", p=P), raw[:].rearrange("p j h -> p (j h)")).then_inc(zeroed, 16)


def scores_stage(nc, st, C, D, esd, ed, raw, zeroed, known, esd_ready, ed_stored):
    ed_first = st.sb("ed_first", [P, HEADS])
    placed, ed_in = C["placed"], C["ed_in"]
    loads, chain = st.sem("loads"), st.sem("chain")
    with st.block() as block:
        @block.sync
        def _(sp):
            sp.wait_ge(placed.sem, placed.base + 16 * TILES)
            sp.dma_start(raw[:].rearrange("p j h -> p (j h)"), D["by_edge"].rearrange("(p j) h -> p (j h)", p=P)).then_inc(loads, 16)
            sp.wait_ge(loads, 16)

        @block.gpsimd
        def _(pool):
            pool.wait_ge(zeroed, 16)
            if known is not None:
                pool.wait_ge(known, 1)
            for t in range(TILES):
                pool.wait_ge(esd_ready, 3 * t + 3)
                pool.indirect_dma_start(D["by_edge"], bass.IndirectOffsetOnAxis(C["first_edge"][:, t:t + 1], 0),
                                        esd[:, t, HEADS:2 * HEADS], None, bounds_check=P * STREAM - 1, oob_is_err=False).then_inc(placed.sem, 16)
            pool.wait_ge(ed_stored, 16)
            pool.indirect_dma_start(ed_first[:], None, D["ed"], bass.IndirectOffsetOnAxis(C["dst_idx"][:, 0:1], 0)).then_inc(ed_in.sem, 16)

        @block.vector
        def _(v):
            step = st.steps(v, chain)
            v.wait_ge(loads, 16)
            v.wait_ge(ed_in.sem, ed_in.base + 16)
            step(v.tensor_copy(raw[:, 0, :], ed_first[:]))
            for h in range(HEADS):
                step(v.tensor_tensor_scan(ed[:, :, h], C["same_prev"][:], raw[:, :, h], 0.0, ALU.mult, ALU.add))
    placed.base += 16 * TILES
    ed_in.base += 16


def sum_stage(nc, st, C, D, ed):
    got = st.sb("got", [P, RING, GROUP, HROW])
    weighed = st.sb("weighed", [P, 2, GROUP, HSUM])
    run = st.sb("run", [P, 2, GROUP, HROW])
    scaled = st.sb("scaled", [P, HSUM])
    idx = st.sb("idx", [P, RING, GROUP], I32)
    cut = st.sb("cut", [P, 2, GROUP + 2])
    score = st.sb("score", [P, 2, GROUP + 1, HEADS])
    ahead = st.sb("ahead", [P, 2, GROUP + 1, HEADS])
    top = st.sb("top", [P, 2, GROUP + 1, HEADS])
    less = st.sb("less", [P, 2, GROUP + 1, HEADS])
    weight = st.sb("weight", [P, 2, GROUP + 1, HEADS])
    wide = st.sb("wide", [P, HEADS, P])
    masked = st.sb("masked", [P, HEADS, P])
    masked_t = st.sb("masked_t", [P, HEADS, P])
    row_ps = st.ps("row_ps", [P, HEADS, P])
    turn_ps = st.ps("turn_ps", [P, HEADS, P])
    carry_ps = st.ps("carry_ps", [P, HSUM])
    arrived = C["arrived"]
    stored = [st.sem(f"stored{s}") for s in range(2)]
    names = ("staged", "summed", "chain", "adds", "argued", "exped", "weighs", "carried", "crossing", "shifted", "powers")
    staged, summed, chain, adds, argued, exped, weighs, carried, crossing, shifted, powers = (st.sem(n) for n in names)
    sums = D["sums"].rearrange("(p j) n -> p (j n)", p=P)
    with st.block() as block:
        @block.sync
        def _(sp):
            def store(g, slot, first):
                hold(sp, st.passed, summed, g + 1)
                sp.dma_start(sums[:, ds(g * (GROUP * HROW), GROUP * HROW)], run[:, slot].rearrange("p u n -> p (u n)")).then_inc(stored[slot], 16)
            each_group(sp, GROUPS, store)
            for s in range(2):
                sp.wait_ge(stored[s], 16 * (GROUPS // 2))

        @block.gpsimd
        def _(pool):
            def fetch(g, slot):
                hold(pool, st.passed, staged, g + 1)
                for u in range(GROUP):
                    pool.indirect_dma_start(got[:, slot, u, :], None, D["table"], bass.IndirectOffsetOnAxis(idx[:, slot, u:u + 1], 0)).then_inc(arrived[slot][u].sem, 16)
            with pool.Fori(0, GROUPS // RING) as i:
                for slot in range(RING):
                    fetch(i * RING + slot, slot)

        @block.scalar
        def _(act):
            def power(g, slot, first):
                hold(act, st.passed, argued, g + 1)
                act.activation(weight[:, slot], less[:, slot], ACT.Exp).then_inc(exped, 1)
            each_group(act, GROUPS, power)
            act.wait_ge(shifted, 1)
            act.activation(masked[:], masked[:], ACT.Exp).then_inc(powers, 1)

        @block.vector
        def _(v):
            step = st.steps(v, chain)
            add = st.steps(v, adds)
            step(v.memset(run[:, 1, GROUP - 1, :], 0.0))
            step(v.memset(top[:, 1, GROUP, :], -BIG))
            step(v.memset(cut[:], -BIG))

            def stage(g, slot):
                v.tensor_copy(idx[:, slot, :], C["src_idx"][:, ds(g * GROUP, GROUP)]).then_inc(staged, 1)
            for slot in range(RING):
                stage(slot, slot)

            def tops(g, slot):
                s = slot % 2
                return (
                    lambda: v.tensor_copy(cut[:, s, 1:GROUP + 1], C["cut_prev"][:, ds(g * GROUP, GROUP)]),
                    lambda: v.tensor_tensor(score[:, s, 1:, :], got[:, slot, :, HSUM:], ed[:, ds(g * GROUP, GROUP), :], ALU.add),
                    lambda: v.scalar_tensor_tensor(score[:, s, 1:, :], score[:, s, 1:, :], 0.2, score[:, s, 1:, :], ALU.mult, ALU.max),
                    lambda: v.tensor_copy(score[:, s, 0, :], top[:, 1 - s, GROUP, :]),
                    lambda: [v.tensor_tensor_scan(ahead[:, s, :, h], cut[:, s, 0:GROUP + 1], score[:, s, :, h], -BIG, ALU.add, ALU.max) for h in range(HEADS)][-1],
                    lambda: [v.tensor_tensor_scan(top[:, s, ::-1, h], cut[:, s, GROUP + 1:0:-1], ahead[:, s, ::-1, h], -BIG, ALU.add, ALU.max) for h in range(HEADS)][-1],
                    lambda: v.tensor_tensor(less[:, s], score[:, s], top[:, s], ALU.subtract),
                )

            def arrive(i, slot):
                for u in range(GROUP):
                    hold(v, st.passed, arrived[slot][u].sem, i * 16 + (arrived[slot][u].base + 16))

            def weigh(u, slot):
                s = slot % 2
                v.tensor_tensor(weighed[:, s, u, :].rearrange("p (h d) -> p h d", h=HEADS), got[:, slot, u, 0:HSUM].rearrange("p (h d) -> p h d", h=HEADS),
                                weight[:, s, u + 1, :].unsqueeze(2).to_broadcast([P, HEADS, HD + 1]), ALU.mult).then_inc(weighs, 1)

            def group(i, slot, first=False, last=False):
                g, s = i * RING + slot, slot % 2
                find = not (last and slot >= RING - 2)
                weighs_next = not (last and slot == RING - 1)
                then, next_slot = (i + 1, slot - 2) if slot >= 2 else (i, slot + 2)
                if find:
                    step.turn(g + 2, TOPS)
                    pending = list(tops(g + 2, next_slot))
                add.turn(g, GROUP + 2)
                hold(v, st.passed, weighs, g * GROUP + GROUP)
                if not last:
                    stage(g + RING, slot)
                if not (first and slot < 2):
                    hold(v, st.passed, stored[s], i * (16 * RING // 2) + slot // 2 * 16)
                add.did(v.tensor_copy(run[:, s, :, HSUM:], top[:, s, 1:, :]))
                add.did(v.tensor_tensor(scaled[:].rearrange("p (h d) -> p h d", h=HEADS), run[:, 1 - s, GROUP - 1, 0:HSUM].rearrange("p (h d) -> p h d", h=HEADS),
                                        weight[:, s, 0, :].unsqueeze(2).to_broadcast([P, HEADS, HD + 1]), ALU.mult))
                if weighs_next:
                    hold(v, st.passed, exped, g + 2)
                if find:
                    arrive(then, next_slot)
                for u in range(GROUP):
                    if find and u < TOPS:
                        if u:
                            step.wait()
                        step.did(pending[u]())
                    if weighs_next:
                        weigh(u, (slot + 1) % RING)
                    before = run[:, s, u - 1, 0:HSUM] if u else scaled[:]
                    add.hold_last()
                    add.did(v.scalar_tensor_tensor(run[:, s, u, 0:HSUM], before, C["same_prev"][:, ds(g * GROUP + u, 1)], weighed[:, s, u, :], ALU.mult, ALU.add))
                if find:
                    step.wait()
                    step.end_turn()
                    v.sem_inc(argued, 1)
                add.hold_last()
                add.end_turn()
                v.sem_inc(summed, 1)

            TOPS = 7
            for g in range(2):
                step.turn(g, TOPS)
                arrive(0, g)
                for f in tops(g, g):
                    step(f())
                v.sem_inc(argued, 1)
            v.wait_ge(exped, 1)
            for u in range(GROUP):
                weigh(u, 0)
            for slot in range(RING):
                group(0, slot, first=True)
            with v.Fori(1, GROUPS // RING - 1) as i:
                for slot in range(RING):
                    group(i, slot)
            for slot in range(RING):
                group(GROUPS // RING - 1, slot, last=True)
            step.end_loop(GROUPS)
            step(v.tensor_copy(wide[:], top[:, 1, GROUP, :].unsqueeze(2).to_broadcast([P, HEADS, P])))
            v.sem_inc(crossing, 1)
            v.wait_ge(carried, 1)
            mask = C["not_before"][:].unsqueeze(1).to_broadcast([P, HEADS, P])
            step(v.tensor_tensor(masked[:], row_ps[:], mask, ALU.add))
            step(v.tensor_reduce(C["carried"][:, HSUM:HROW], masked[:], AX_X, ALU.max))
            step(v.tensor_tensor(masked[:], masked[:], C["carried"][:, HSUM:HROW].unsqueeze(2).to_broadcast([P, HEADS, P]), ALU.subtract))
            v.sem_inc(shifted, 1)
            v.wait_ge(powers, 1)
            step(v.scalar_tensor_tensor(masked[:], mask, -1.0, masked[:], ALU.is_ge, ALU.mult))
            v.sem_inc(crossing, 1)
            v.wait_ge(carried, 2)
            step(v.tensor_copy(masked_t[:], turn_ps[:]))
            v.sem_inc(crossing, 1)
            v.wait_ge(carried, 3)
            step(v.tensor_copy(C["carried"][:, 0:HSUM], carry_ps[:]))
            step(v.memset(C["carried"][:, HROW:HROW + 1], 1.0))

        @block.tensor
        def _(pe):
            pe.wait_ge(crossing, 1)
            for h in range(HEADS):
                ins = pe.matmul(row_ps[:, h, :], wide[:, h, :], C["ident"][:], start=True, stop=True)
            ins.then_inc(carried, 1)
            pe.wait_ge(crossing, 2)
            for h in range(HEADS):
                ins = pe.transpose(turn_ps[:, h, :], masked[:, h, :], C["ident"][:])
            ins.then_inc(carried, 1)
            pe.wait_ge(crossing, 3)
            pe.wait_ge(summed, GROUPS)
            for h in range(HEADS):
                cells = slice(h * (HD + 1), (h + 1) * (HD + 1))
                ins = pe.matmul(carry_ps[:, cells], masked_t[:, h, :], run[:, 1, GROUP - 1, cells], start=True, stop=True)
            ins.then_inc(carried, 1)
    for s in arrived:
        for u in s:
            u.base += GROUPS // RING * 16


def nodes_stage(nc, st, C, D, out, base, bias, global_top):
    numbers = st.sb("numbers", [P, P], I32)
    number = st.sb("number", [P, P])
    gate = st.sb("gate", [P, 2, P])
    at = st.sb("at", [P, TILES])
    got = st.sb("got", [P, TILES, HROW])
    into = st.sb("into", [P, TILES, HROW + 1])
    less = st.sb("less", [P, 2, TILES, HEADS])
    top = st.sb("top", [P, TILES, HEADS])
    den = st.sb("den", [P, TILES, HEADS])
    miss = st.sb("miss", [P, TILES])
    bias_row = st.sb("bias_row", [P, DIM])
    peak, peaks = st.sb("peak", [P, 1]), st.sb("peaks", [P, 1])
    in_ps = [st.ps(f"in_ps{i}", [P, HROW + 1]) for i in range(4)]
    LOT = 5
    arrived = C["arrived"][0][0:TILES // LOT]
    names = ("iotas", "loads", "chain", "gated", "crossed", "copied", "lessed", "exped", "topped", "selected")
    iotas, loads, chain, gated, crossed, copied, lessed, exped, topped, selected = (st.sem(n) for n in names)
    with st.block() as block:
        @block.sync
        def _(sp):
            if bias is not None:
                sp.dma_start(bias_row[:], bias.partition_broadcast(P)).then_inc(loads, 16)
                sp.wait_ge(loads, 16)

        @block.gpsimd
        def _(pool):
            pool.iota(numbers[:], [[1, P]], base=0, channel_multiplier=0).then_inc(iotas, 1)
            for t in range(TILES):
                pool.indirect_dma_start(got[:, t, :], None, D["sums"], bass.IndirectOffsetOnAxis(C["last_edge"][:, t:t + 1], 0)).then_inc(arrived[t // LOT].sem, 16)
            if global_top:
                pool.wait_ge(topped, 1)
                pool.affine_select(out=den[:], in_=den[:], compare_op=ALU.is_ge, fill=-BIG, base=NODES - 1,
                                   pattern=[[-P, TILES], [0, HEADS]], channel_multiplier=-1).then_inc(selected, 1)
                pool.wait_ge(topped, 2)
                pool.partition_all_reduce(peaks[:], peak[:], P, RMAX).then_inc(selected, 1)

        @block.vector
        def _(v):
            step = st.steps(v, chain)
            v.wait_ge(iotas, 1)
            step(v.tensor_copy(number[:], numbers[:]))
            step(v.tensor_scalar(at[:], C["tile_start"][:], -1.0, C["dst_first"][:], ALU.mult, ALU.add))
            for t in range(TILES):
                if t >= 2:
                    v.wait_ge(crossed, t - 1)
                v.tensor_scalar(gate[:, t % 2, :], number[:], at[:, t:t + 1], C["ends_in"][:], ALU.is_equal, ALU.mult).then_inc(gated, 1)
            cells = lambda a: a[:, :, 0:HSUM].rearrange("p t (h d) -> p t h d", h=HEADS)
            for q in range(TILES // LOT):
                lot = slice(q * LOT, (q + 1) * LOT)
                v.wait_ge(copied, (q + 1) * LOT)
                v.wait_ge(arrived[q].sem, arrived[q].base + 16 * LOT)
                step(v.tensor_scalar(miss[:, lot], into[:, lot, HROW], 1.0, BIG, ALU.subtract, ALU.mult))
                step(v.tensor_tensor(less[:, 0, lot], into[:, lot, HSUM:HROW], miss[:, lot].unsqueeze(2).to_broadcast([P, LOT, HEADS]), ALU.add))
                step(v.tensor_tensor(top[:, lot], less[:, 0, lot], got[:, lot, HSUM:HROW], ALU.max))
                step.did(v.tensor_tensor(less[:, 0, lot], less[:, 0, lot], top[:, lot], ALU.subtract))
                step(v.tensor_tensor(less[:, 1, lot], got[:, lot, HSUM:HROW], top[:, lot], ALU.subtract))
                v.sem_inc(lessed, 1)
                v.wait_ge(exped, q + 1)
                for a, each in ((0, into), (1, got)):
                    step.did(v.tensor_tensor(cells(each[:, lot]), cells(each[:, lot]), less[:, a, lot].unsqueeze(3).to_broadcast([P, LOT, HEADS, HD + 1]), ALU.mult))
                step.wait()
                step(v.tensor_tensor(got[:, lot, 0:HSUM], got[:, lot, 0:HSUM], into[:, lot, 0:HSUM], ALU.add))
            if global_top:
                step(v.tensor_scalar(miss[:], C["has_edge"][:], 1.0, BIG, ALU.subtract, ALU.mult))
                step(v.tensor_tensor(den[:], top[:], miss[:].unsqueeze(2).to_broadcast([P, TILES, HEADS]), ALU.add))
                v.sem_inc(topped, 1)
                v.wait_ge(selected, 1)
                step(v.tensor_reduce(peak[:], den[:].rearrange("p t h -> p (t h)"), AX_X, ALU.max))
                v.sem_inc(topped, 1)
                v.wait_ge(selected, 2)
                step(v.tensor_scalar(top[:], top[:], -1.0, peaks[:], ALU.mult, ALU.add))
                v.sem_inc(topped, 1)
            if global_top:
                v.wait_ge(exped, TILES // LOT + 1)
                step(v.scalar_tensor_tensor(den[:], top[:], 1.0e-16, cells(got[:])[:, :, :, HD], ALU.mult, ALU.add))
            else:
                step(v.tensor_scalar(den[:], cells(got[:])[:, :, :, HD], 1.0e-16, None, ALU.add))
            step(v.reciprocal(den[:], den[:]))
            step(v.tensor_tensor(den[:], den[:], C["has_edge"][:].unsqueeze(2).to_broadcast([P, TILES, HEADS]), ALU.mult))
            step(v.tensor_tensor(cells(got[:]), cells(got[:]), den[:].unsqueeze(3).to_broadcast([P, TILES, HEADS, HD + 1]), ALU.mult))
            heads = lambda a: a[:].rearrange("p t (h d) -> p t h d", h=HEADS)
            step(v.tensor_tensor(heads(out), heads(base), cells(got[:])[:, :, :, 0:HD], ALU.add))
            if bias is not None:
                v.wait_ge(loads, 16)
                step(v.tensor_tensor(out[:], out[:], bias_row[:].unsqueeze(1).to_broadcast([P, TILES, DIM]), ALU.add))

        @block.scalar
        def _(act):
            for t in range(TILES):
                act.wait_ge(crossed, t + 1)
                act.activation(into[:, t, :], in_ps[t % 4][:], ACT.Copy).then_inc(copied, 1)
            for q in range(TILES // LOT):
                act.wait_ge(lessed, q + 1)
                at = less[:, :, q * LOT:(q + 1) * LOT, :]
                act.activation(at, at, ACT.Exp).then_inc(exped, 1)
            if global_top:
                act.wait_ge(topped, 3)
                act.activation(top[:], top[:], ACT.Exp).then_inc(exped, 1)

        @block.tensor
        def _(pe):
            for t in range(TILES):
                pe.wait_ge(gated, t + 1)
                if t >= 4:
                    pe.wait_ge(copied, t - 3)
                pe.matmul(in_ps[t % 4][:], gate[:, t % 2, :], C["carried"][:], start=True, stop=True).then_inc(crossed, 1)
    for a in arrived:
        a.base += 16 * LOT



def slice_weights_stage(nc, st, C, A, w_log, b_log):
    wxT = st.sb("wxT", [SD, SH, DIM])
    wsl = st.sb("wsl", [SD, SD])
    bx = st.sb("bx", [SD, SH])
    bx_wide = st.sb("bx_wide", [SD, SH, P])
    bsl = st.sb("bsl", [P, SD])
    temp = st.sb("temp", [P, SH])
    w_ps = [st.ps(f"w_ps{k}", [P, SLICES]) for k in range(KT)]
    b_ps = st.ps("b_ps", [P, SLICES])
    loads, chain, wide, made = (st.sem(n) for n in ("loads", "chain", "wide", "made"))
    heads = "p (h g) -> p h g"
    with st.block() as block:
        @block.sync
        def _(sp):
            sp.dma_start(wxT[:], A["L0_ffn_W_x"].rearrange("(h c) k -> c h k", c=SD)).then_inc(loads, 16)
            sp.dma_start(wsl[:], A["L0_ffn_W_slice"]).then_inc(loads, 16)
            sp.dma_start(bx[:], A["L0_ffn_b_x"]).then_inc(loads, 16)
            sp.dma_start(bsl[:], A["L0_ffn_b_slice"].partition_broadcast(P)).then_inc(loads, 16)
            sp.dma_start(temp[:], A["L0_ffn_temperature"].rearrange("a h b c -> (a h b c)").partition_broadcast(P)).then_inc(loads, 16)
            sp.wait_ge(loads, 80)

        @block.vector
        def _(v):
            step = st.steps(v, chain)
            v.wait_ge(loads, 80)
            step(v.tensor_copy(bx_wide[:], bx[:].unsqueeze(2).to_broadcast([SD, SH, P])))
            v.sem_inc(wide, 1)
            step(v.tensor_scalar(temp[:], temp[:], 0.1, 5.0, ALU.max, ALU.min))
            step(v.reciprocal(temp[:], temp[:]))
            v.wait_ge(made, 1)
            by_temp = temp[:].unsqueeze(2).to_broadcast([P, SH, SD])
            for k in range(KT):
                step(v.tensor_tensor(w_log[:, k, :].rearrange(heads, h=SH), w_ps[k][:].rearrange(heads, h=SH), by_temp, ALU.mult))
            step(v.tensor_tensor(b_log[:].rearrange(heads, h=SH), b_ps[:].rearrange(heads, h=SH), bsl[:].unsqueeze(1).to_broadcast([P, SH, SD]), ALU.add))
            step(v.tensor_tensor(b_log[:].rearrange(heads, h=SH), b_log[:].rearrange(heads, h=SH), by_temp, ALU.mult))

        @block.tensor
        def _(pe):
            pe.wait_ge(wide, 1)
            for h in range(SH):
                at = slice(h * SD, (h + 1) * SD)
                for k in range(KT):
                    pe.matmul(w_ps[k][:, at], wxT[:, h, k * P:(k + 1) * P], wsl[:], start=True, stop=True)
                ins = pe.matmul(b_ps[:, at], bx_wide[:, h, :], wsl[:], start=True, stop=True)
            ins.then_inc(made, 1)


def assign_stage(nc, st, C, XN, XT, w_log, b_log, SWT, Z):
    xt = st.sb("xt", [P, 2, KT, P])
    sw = st.sb("sw", [P, 2, SLICES])
    raw = st.sb("raw", [P, 2, SLICES])
    top, total = st.sb("top", [P, 2, SH]), st.sb("total", [P, 2, SH])
    NZ = SLICES // P
    log_ps = [st.ps(f"log_ps{i}", [P, SLICES]) for i in range(2)]
    turn_ps = [st.ps(f"turn_ps{i}", [P, NZ, P]) for i in range(2)]
    z_ps = [st.ps(f"z_ps{i}", [P, DIM + 1]) for i in range(NZ)]
    brought, logits, chain, shifted, exped, weighed, summed, copied, norm_chain = (st.sem(n) for n in (
        "brought", "logits", "chain", "shifted", "exped", "weighed", "summed", "copied", "norm_chain"))
    last_rows = NODES - (TILES - 1) * P
    heads = "p (h g) -> p h g"
    with st.block() as block:
        @block.gpsimd
        def _(pool):
            def bring(t, slot, first):
                if not first:
                    hold(pool, st.passed, logits, t - 1)
                pool.tensor_copy(xt[:, slot], XT[:, :, ds(t * P, P)]).then_inc(brought, 1)
            each_tile(pool, bring)

        @block.tensor
        def _(pe):
            def score(t, slot, first):
                hold(pe, st.passed, brought, t + 1)
                if not first:
                    hold(pe, st.passed, shifted, t - 1)
                for k in range(KT):
                    ins = pe.matmul(log_ps[slot][:], xt[:, slot, k, :], w_log[:, k, :], start=(k == 0), stop=(k == KT - 1))
                ins.then_inc(logits, 1)

            def collect(t, slot, first):
                hold(pe, st.passed, weighed, t + 1)
                if not first:
                    hold(pe, st.passed, copied, t - 1)
                for z in range(NZ):
                    pe.transpose(turn_ps[slot][:, z, :], sw[:, slot, z * P:(z + 1) * P], C["ident"][:])
                n = last_rows if isinstance(t, int) and t == TILES - 1 else P
                begins, ends = isinstance(t, int) and t == 0, isinstance(t, int) and t == TILES - 1
                for z in range(NZ):
                    mine = sw[0:n, slot, z * P:(z + 1) * P]
                    pe.matmul(z_ps[z][:, 0:DIM], mine, XN[0:n, ds(t, 1), :].rearrange("p a d -> p (a d)"), start=begins, stop=False)
                    ins = pe.matmul(z_ps[z][:, DIM:DIM + 1], mine, C["ones"][0:n, 0:1], start=False, stop=ends)
                ins.then_inc(summed, 1)
            score(0, 0, True)
            score(1, 1, True)
            score(2, 0, False)
            collect(0, 0, True)
            score(3, 1, False)
            collect(1, 1, True)
            with pe.Fori(1, TILES // 2 - 1) as i:
                score(i * 2 + 2, 0, False)
                collect(i * 2, 0, False)
                score(i * 2 + 3, 1, False)
                collect(i * 2 + 1, 1, False)
            score(TILES - 1, 0, False)
            collect(TILES - 3, 0, False)
            collect(TILES - 2, 1, False)
            collect(TILES - 1, 0, False)

        @block.vector
        def _(v):
            step = st.steps(v, chain)

            def shift(t, slot, first):
                step.turn(t, 2)
                hold(v, st.passed, logits, t + 1)
                if not first:
                    hold(v, st.passed, weighed, t - 1)
                cells = raw[:, slot, :].rearrange(heads, h=SH)
                step(v.tensor_tensor(raw[:, slot, :], log_ps[slot][:], b_log[:], ALU.add))
                step(v.tensor_reduce(top[:, slot, :], cells, AX_X, ALU.max))
                v.tensor_tensor(cells, cells, top[:, slot, :].unsqueeze(2).to_broadcast([P, SH, SD]), ALU.subtract).then_inc(shifted, 1)
                step.end_turn()

            chain2 = st.steps(v, norm_chain)

            def normalize(t, slot, first):
                chain2.turn(t, 2)
                hold(v, st.passed, exped, t + 1)
                cells = raw[:, slot, :].rearrange(heads, h=SH)
                chain2(v.tensor_reduce(total[:, slot, :], cells, AX_X, ALU.add))
                chain2(v.reciprocal(total[:, slot, :], total[:, slot, :]))
                if not first:
                    hold(v, st.passed, summed, t - 1)
                v.tensor_tensor(sw[:, slot, :].rearrange(heads, h=SH), cells, total[:, slot, :].unsqueeze(2).to_broadcast([P, SH, SD]), ALU.mult).then_inc(weighed, 1)
                chain2.end_turn()
            shift(0, 0, True)
            shift(1, 1, True)
            normalize(0, 0, True)
            with v.Fori(1, TILES // 2) as i:
                shift(i * 2, 0, False)
                normalize(i * 2 - 1, 1, False)
                shift(i * 2 + 1, 1, False)
                normalize(i * 2, 0, False)
            shift(TILES - 1, 0, False)
            normalize(TILES - 2, 1, False)
            normalize(TILES - 1, 0, False)
            v.wait_ge(summed, TILES)
            step2 = st.steps(v, norm_chain)
            step2.base = 2 * TILES
            for z in range(NZ):
                step2(v.tensor_copy(Z[:, z, 0:DIM + 1], z_ps[z][:]))

        @block.scalar
        def _(act):
            def exps(t, slot, first):
                hold(act, st.passed, shifted, t + 1)
                act.activation(raw[:, slot, :], raw[:, slot, :], ACT.Exp).then_inc(exped, 1)

            def copy(t, slot, first):
                hold(act, st.passed, summed, t + 1)
                act.activation(SWT[:, :, ds(t * P, P)], turn_ps[slot][:], ACT.Copy).then_inc(copied, 1)
            exps(0, 0, True)
            exps(1, 1, True)
            copy(0, 0, True)
            with act.Fori(1, TILES // 2) as i:
                exps(i * 2, 0, False)
                copy(i * 2 - 1, 1, False)
                exps(i * 2 + 1, 1, False)
                copy(i * 2, 0, False)
            exps(TILES - 1, 0, False)
            copy(TILES - 2, 1, False)
            copy(TILES - 1, 0, False)


def slice_attention_stage(nc, st, C, A, Z, mix):
    NZ = SLICES // P
    w_fx, w_q, w_k, w_v = st.sb("w_fx", [P, KT, SLICES]), st.sb("w_q", [SD, SD]), st.sb("w_k", [SD, SD]), st.sb("w_v", [SD, SD])
    w_out, b_fx = st.sb("w_out", [SD, SH, DIM]), st.sb("b_fx", [1, SLICES])
    ZT, norm_row = st.sb("ZT", [P, KT, SLICES]), st.sb("norm_row", [1, SLICES])
    inv_row, tokT = st.sb("inv_row", [1, SLICES]), st.sb("tokT", [SD, SLICES])
    inv = st.sb("inv", [SD, SLICES])
    qT, kT, vT = (st.sb(n, [SD, SLICES]) for n in ("qT", "kT", "vT"))
    prob, probT = st.sb("prob", [SD, SLICES]), st.sb("probT", [SD, SLICES])
    top, total = st.sb("top", [SD, SH]), st.sb("total", [SD, SH])
    vw = st.sb("vw", [SD, SH, DIM])
    a_ps, b_ps, c_ps, d_ps = (st.ps(n, [P, 512]) for n in ("a_ps", "b_ps", "c_ps", "d_ps"))
    e_ps = [st.ps(f"e_ps{i}", [P, 2, DIM]) for i in range(2)]
    pairs = [a_ps[:].rearrange("p (a n) -> p a n", a=2), b_ps[:].rearrange("p (a n) -> p a n", a=2), e_ps[0], e_ps[1]]
    values, values_out = st.sem("values"), st.sem("values_out")
    loads, chain, pe_ok, dve_ok, act_ok = (st.sem(n) for n in ("loads", "chain", "pe_ok", "dve_ok", "act_ok"))
    heads = "p (h g) -> p h g"
    scale = float(SD) ** -0.5
    with st.block() as block:
        @block.sync
        def _(sp):
            sp.dma_start(w_fx[:], A["L0_ffn_W_fx"].rearrange("(k p) n -> p k n", p=P)).then_inc(loads, 16)
            for tile, name in ((w_q, "W_q"), (w_k, "W_k"), (w_v, "W_v")):
                sp.dma_start(tile[:], A[f"L0_ffn_{name}"]).then_inc(loads, 16)
            sp.dma_start(w_out[:], A["L0_ffn_W_out"].rearrange("(h c) n -> c h n", c=SD)).then_inc(loads, 16)
            sp.dma_start(b_fx[:], A["L0_ffn_b_fx"].rearrange("(a n) -> a n", a=1)).then_inc(loads, 16)
            sp.wait_ge(loads, 96)

        @block.tensor
        def _(pe):
            pe.wait_ge(loads, 96)
            for k in range(KT):
                for z in range(NZ):
                    pe.transpose((a_ps, b_ps)[k][:, z * P:(z + 1) * P], Z[:, z, k * P:(k + 1) * P], C["ident"][:])
            for z in range(NZ):
                ins = pe.transpose(c_ps[0:1, z * P:(z + 1) * P], Z[:, z, DIM:DIM + 1], C["ident"][:])
            ins.then_inc(pe_ok, 1)
            pe.wait_ge(dve_ok, 1)
            for h in range(SH):
                at = slice(h * SD, (h + 1) * SD)
                for k in range(KT):
                    pe.matmul(d_ps[0:SD, at], w_fx[:, k, at], ZT[:, k, at], start=(k == 0), stop=False)
                pe.matmul(d_ps[0:SD, at], b_fx[0:1, at], norm_row[0:1, at], start=False, stop=True)
            pe.matmul(c_ps[0:SD, :], C["ones"][0:1, 0:SD], inv_row[:], start=True, stop=True).then_inc(pe_ok, 1)
            pe.wait_ge(dve_ok, 2)
            for ps, w in ((a_ps, w_q), (b_ps, w_k), (c_ps, w_v)):
                ins = pe.matmul(ps[0:SD, :], w[:], tokT[:], start=True, stop=True)
            ins.then_inc(pe_ok, 1)
            pe.wait_ge(dve_ok, 3)
            for h in range(SH):
                at = slice(h * SD, (h + 1) * SD)
                ins = pe.matmul(d_ps[0:SD, at], qT[:, at], kT[:, at], start=True, stop=True)
            ins.then_inc(pe_ok, 1)
            for h in range(SH):
                ins = pe.matmul(pairs[h // 2][0:SD, h % 2, :], vT[:, h * SD:(h + 1) * SD], w_out[:, h, :], start=True, stop=True)
            ins.then_inc(values, 1)
            pe.wait_ge(dve_ok, 4)
            for h in range(SH):
                at = slice(h * SD, (h + 1) * SD)
                ins = pe.transpose(c_ps[0:SD, at], prob[:, at], C["ident"][0:SD, 0:SD])
            ins.then_inc(pe_ok, 1)
            pe.wait_ge(dve_ok, 5)
            pe.wait_ge(values_out, len(pairs))
            for h in range(SH):
                half = slice((h % 2) * SD, (h % 2 + 1) * SD)
                ins = pe.matmul(e_ps[h // 4][half, (h // 2) % 2, :], probT[:, h * SD:(h + 1) * SD], vw[:, h, :], start=True, stop=True)
            ins.then_inc(pe_ok, 1)

        @block.vector
        def _(v):
            step = st.steps(v, chain)
            v.wait_ge(pe_ok, 1)
            step(v.tensor_copy(ZT[:, 0, :], a_ps[:]))
            step(v.tensor_copy(ZT[:, 1, :], b_ps[:]))
            step(v.tensor_copy(norm_row[:], c_ps[0:1, :]))
            step(v.tensor_scalar(inv_row[:], norm_row[:], 1.0e-5, None, ALU.add))
            step(v.reciprocal(inv_row[:], inv_row[:]))
            v.sem_inc(dve_ok, 1)
            v.wait_ge(pe_ok, 2)
            step(v.tensor_copy(inv[:], c_ps[0:SD, :]))
            step(v.tensor_tensor(tokT[:], d_ps[0:SD, :], inv[:], ALU.mult))
            v.sem_inc(dve_ok, 1)
            v.wait_ge(pe_ok, 3)
            for tile, ps in ((qT, a_ps), (kT, b_ps), (vT, c_ps)):
                step.did(v.tensor_copy(tile[:], ps[0:SD, :]))
            step.wait()
            v.sem_inc(dve_ok, 1)
            v.wait_ge(pe_ok, 4)
            cells = prob[:].rearrange(heads, h=SH)
            step(v.tensor_reduce(top[:], d_ps[0:SD, :].rearrange(heads, h=SH), AX_X, ALU.max))
            step(v.tensor_tensor(cells, d_ps[0:SD, :].rearrange(heads, h=SH), top[:].unsqueeze(2).to_broadcast([SD, SH, SD]), ALU.subtract))
            v.sem_inc(act_ok, 1)
            v.wait_ge(act_ok, 2)
            step(v.tensor_reduce(total[:], cells, AX_X, ALU.add))
            step(v.reciprocal(total[:], total[:]))
            step(v.tensor_tensor(cells, cells, total[:].unsqueeze(2).to_broadcast([SD, SH, SD]), ALU.mult))
            v.sem_inc(dve_ok, 1)
            v.wait_ge(pe_ok, 5)
            step(v.tensor_copy(probT[:], c_ps[0:SD, :]))
            v.sem_inc(dve_ok, 1)
            v.wait_ge(pe_ok, 6)
            for z in range(NZ):
                step.did(v.tensor_copy(mix[:, z, :], e_ps[z // 2][:, z % 2, :]))

        @block.scalar
        def _(act):
            act.wait_ge(act_ok, 1)
            act.activation(prob[:], prob[:], ACT.Exp, scale=scale).then_inc(act_ok, 1)
            act.wait_ge(values, 1)
            for i, pair in enumerate(pairs):
                act.activation(vw[:, 2 * i:2 * i + 2, :], pair[0:SD], ACT.Copy).then_inc(values_out, 1)


def mix_stage(nc, st, C, A, SWT, mix, X):
    NZ = SLICES // P
    b_row = st.sb("b_row", [P, DIM])
    y_ps = [st.ps(f"y_ps{i}", [P, DIM]) for i in range(2)]
    loads, made, added, chain = (st.sem(n) for n in ("loads", "made", "added", "chain"))
    with st.block() as block:
        @block.sync
        def _(sp):
            sp.dma_start(b_row[:], A["L0_ffn_b_out"].partition_broadcast(P)).then_inc(loads, 16)
            sp.wait_ge(loads, 16)

        @block.tensor
        def _(pe):
            for t in range(TILES):
                if t >= 2:
                    pe.wait_ge(added, t - 1)
                for z in range(NZ):
                    ins = pe.matmul(y_ps[t % 2][:], SWT[:, z, t * P:(t + 1) * P], mix[:, z, :], start=(z == 0), stop=(z == NZ - 1))
                ins.then_inc(made, 1)

        @block.vector
        def _(v):
            step = st.steps(v, chain)
            v.wait_ge(loads, 16)

            def add(t, slot, first):
                step.turn(t, 1)
                row = X[:, ds(t, 1), :].rearrange("p a d -> p (a d)")
                hold(v, st.passed, made, t + 1)
                step(v.tensor_tensor(row, row, y_ps[slot][:], ALU.add))
                v.tensor_tensor(row, row, b_row[:], ALU.add).then_inc(added, 1)
            each_tile(v, add)



def keep_rows_stage(nc, st, D, name, rows, stored):
    with st.block() as block:
        @block.sync
        def _(sp):
            sp.dma_start(D[name].rearrange("(t p) d -> p t d", p=P), rows[:]).then_inc(stored, 16)


def spread_rows_stage(nc, st, C, D, Zn):
    placed = C["placed"]
    with st.block() as block:
        @block.gpsimd
        def _(pool):
            for t in range(TILES):
                pool.indirect_dma_start(D["ordered"], bass.IndirectOffsetOnAxis(C["rank"][:, t:t + 1], 0), Zn[:, t, :], None).then_inc(placed.sem, 16)
            pool.wait_ge(placed.sem, placed.base + 16 * TILES)
    placed.base += 16 * TILES


def sequence_stage(nc, st, C, A, D, ZT, RAW, GATE, XC):
    LOT = 5
    row = st.sb("row", [P, LOT, LOT, DIM])
    w, w_conv, b = st.sb("w", [P, KT, 2 * DIM]), st.sb("w_conv", [P, KT, TAPS]), st.sb("b", [P, KT])
    ps = [[st.ps(f"ps{s}{m}", [P, 512]) for m in range(2 * KT)] for s in range(2)]
    arrived = [st.sem(f"arrived{q}") for q in range(LOT)]
    loads, turned, copied, made, raw_out, gate_out, chain, summed, act_out = (st.sem(n) for n in (
        "loads", "turned", "copied", "made", "raw_out", "gate_out", "chain", "summed", "act_out"))
    spans = [(t, min(2, TILES - t)) for t in range(0, TILES, 2)]
    with st.block() as block:
        @block.sync
        def _(sp):
            for q in range(LOT):
                sp.dma_start(row[:, q], D["ordered"].rearrange("(t p) d -> p t d", p=P)[:, q * LOT:(q + 1) * LOT, :]).then_inc(arrived[q], 16)
            sp.dma_start(w[:], A["L1_gnn_in_proj_w"].rearrange("(k p) n -> p k n", p=P)).then_inc(loads, 16)
            sp.dma_start(w_conv[:], A["L1_gnn_conv_w"].rearrange("(k p) n -> p k n", p=P)).then_inc(loads, 16)
            sp.dma_start(b[:], A["L1_gnn_conv_b"]).then_inc(loads, 16)
            sp.wait_ge(loads, 48)

        @block.tensor
        def _(pe):
            for n, (t0, tiles) in enumerate(spans):
                if n >= 4:
                    pe.wait_ge(copied, n - 3)
                bank = ps[0][n % 4][:].rearrange("p (k s n) -> p k s n", k=KT, s=2)
                for i in range(tiles):
                    q, t = divmod(t0 + i, LOT)
                    pe.wait_ge(arrived[q], 16)
                    for k in range(KT):
                        ins = pe.transpose(bank[:, k, i, :], row[:, q, t, k * P:(k + 1) * P], C["ident"][:])
                ins.then_inc(turned, 1)
            pe.wait_ge(loads, 48)
            pe.wait_ge(copied, len(spans))

            def product(c, slot, first):
                if not first:
                    hold(pe, st.passed, raw_out, c - 1)
                    hold(pe, st.passed, gate_out, c - 1)
                for m in range(2 * KT):
                    for k in range(KT):
                        ins = pe.matmul(ps[slot][m][:, 0:CHUNK], w[:, k, m * P:(m + 1) * P], ZT[:, k, ds(c * CHUNK, CHUNK)], start=(k == 0), stop=(k == KT - 1))
                ins.then_inc(made, 1)
            each_group(pe, CHUNKS, product)

        @block.vector
        def _(v):
            step = st.steps(v, chain)
            for m in range(KT):
                step(v.memset(RAW[:, m, 0:TAPS - 1], 0.0))
            v.wait_ge(loads, 48)

            def convolve(c, slot, first):
                step.turn(c, KT * TAPS)
                hold(v, st.passed, made, c + 1)
                for m in range(KT):
                    ins = v.tensor_copy(RAW[:, m, ds(c * CHUNK + (TAPS - 1), CHUNK)], ps[slot][m][:, 0:CHUNK])
                ins.then_inc(raw_out, 1)
                hold(v, st.passed, raw_out, c + 1)
                for k in range(TAPS):
                    for m in range(KT):
                        out, tap = XC[:, m, ds(c * CHUNK, CHUNK)], RAW[:, m, ds(c * CHUNK + k, CHUNK)]
                        if k == 0:
                            step.did(v.tensor_scalar(out, tap, w_conv[:, m, 0:1], None, ALU.mult))
                        else:
                            step.hold_last(1)
                            step.did(v.scalar_tensor_tensor(out, tap, w_conv[:, m, k:k + 1], out, ALU.mult, ALU.add))
                step.hold_last()
                step.end_turn()
                v.sem_inc(summed, 1)
            each_group(v, CHUNKS, convolve)

        @block.scalar
        def _(act):
            for n, (t0, tiles) in enumerate(spans):
                act.wait_ge(turned, n + 1)
                bank = ps[0][n % 4][:].rearrange("p (k s n) -> p k (s n)", k=KT, s=2)
                act.activation(ZT[:, :, t0 * P:(t0 + tiles) * P], bank[:, :, 0:tiles * P], ACT.Copy).then_inc(copied, 1)
            act.wait_ge(loads, 48)

            def gate(c, slot, first):
                hold(act, st.passed, made, c + 1)
                for m in range(KT):
                    ins = act.activation(GATE[:, m, ds(c * CHUNK, CHUNK)], ps[slot][KT + m][:, 0:CHUNK], ACT.Silu)
                ins.then_inc(gate_out, 1)
                hold(act, st.passed, summed, c + 1)
                for m in range(KT):
                    at = XC[:, m, ds(c * CHUNK, CHUNK)]
                    ins = act.activation(at, at, ACT.Silu, bias=b[:, m:m + 1])
                ins.then_inc(act_out, 1)
            each_group(act, CHUNKS, gate)
            act.wait_ge(act_out, CHUNKS)


def x_proj_stage(nc, st, C, A, D, XC, DT, U):
    wx, wdt, b = st.sb("wx", [P, KT, RANK + 2 * STATES]), st.sb("wdt", [RANK, DIM]), st.sb("b", [P, KT])
    dbc = st.sb("dbc", [RANK + 2 * STATES, ROWS])
    HALF = ROWS // 2
    near, e, w, ln, short = (st.sb(n, [P, 2, HALF]) for n in ("near", "e", "w", "ln", "short"))
    SMALL = 1.0 / 64
    pieces = [(m, slice(i * HALF, (i + 1) * HALF)) for i in range(2) for m in range(KT)]
    x_ps = [st.ps(f"x_ps{i}", [RANK + 2 * STATES, 512]) for i in range(2)]
    d_ps = [[st.ps(f"d_ps{s}{m}", [P, 512]) for m in range(KT)] for s in range(2)]
    loads, made, out, steps_made, steps_out, chain, asked, answered, stored, done, series = (st.sem(n) for n in (
        "loads", "made", "out", "steps_made", "steps_out", "chain", "asked", "answered", "stored", "done", "series"))
    with st.block() as block:
        @block.sync
        def _(sp):
            sp.dma_start(wx[:], A["L1_gnn_x_proj_w"].rearrange("(k p) n -> p k n", p=P)).then_inc(loads, 16)
            sp.dma_start(wdt[:], A["L1_gnn_dt_proj_w"]).then_inc(loads, 16)
            sp.dma_start(b[:], A["L1_gnn_dt_proj_b"]).then_inc(loads, 16)
            sp.wait_ge(out, CHUNKS)
            sp.dma_start(D["bc"], dbc[RANK:RANK + 2 * STATES, :]).then_inc(stored, 16)
            sp.wait_ge(stored, 16)

        @block.tensor
        def _(pe):
            pe.wait_ge(loads, 48)

            def product(c, slot, first):
                if not first:
                    hold(pe, st.passed, out, c - 1)
                for k in range(KT):
                    ins = pe.matmul(x_ps[slot][:, 0:CHUNK], wx[:, k, :], XC[:, k, ds(c * CHUNK, CHUNK)], start=(k == 0), stop=(k == KT - 1))
                ins.then_inc(made, 1)

            def steps_of(c, slot, first):
                hold(pe, st.passed, out, c + 1)
                if not first:
                    hold(pe, st.passed, steps_out, c - 1)
                for m in range(KT):
                    ins = pe.matmul(d_ps[slot][m][:, 0:CHUNK], wdt[:, m * P:(m + 1) * P], dbc[0:RANK, ds(c * CHUNK, CHUNK)], start=True, stop=True)
                ins.then_inc(steps_made, 1)
            product(0, 0, True)
            product(1, 1, True)
            steps_of(0, 0, True)
            product(2, 0, False)
            steps_of(1, 1, True)
            with pe.Fori(1, CHUNKS // 2 - 1) as i:
                product(i * 2 + 1, 1, False)
                steps_of(i * 2, 0, False)
                product(i * 2 + 2, 0, False)
                steps_of(i * 2 + 1, 1, False)
            product(CHUNKS - 1, 1, False)
            steps_of(CHUNKS - 2, 0, False)
            steps_of(CHUNKS - 1, 1, False)

        @block.gpsimd
        def _(pool):
            def feed(n):
                m, at = pieces[n]
                pool.wait_ge(done, n + 1)
                pool.tensor_tensor(U[:, m, at], DT[:, m, at], XC[:, m, at], ALU.mult)
            for n in range(len(pieces)):
                i = n % 2
                pool.wait_ge(answered, 3 * n + 1)
                pool.tensor_scalar(short[:, i], e[:, i], -0.25, 1.0 / 3, ALU.mult, ALU.add).then_inc(series, 1)
                pool.wait_ge(series, 2 * n + 1)
                pool.tensor_tensor(short[:, i], short[:, i], e[:, i], ALU.mult).then_inc(series, 1)
                if n:
                    feed(n - 1)
            feed(len(pieces) - 1)

        @block.scalar
        def _(act):
            def copy(c, slot, first):
                hold(act, st.passed, made, c + 1)
                act.activation(dbc[:, ds(c * CHUNK, CHUNK)], x_ps[slot][:, 0:CHUNK], ACT.Copy).then_inc(out, 1)
            each_group(act, CHUNKS, copy)
            for n in range(len(pieces)):
                act.wait_ge(asked, n + 1)
                if n >= 2:
                    act.wait_ge(done, n - 1)
                act.activation(e[:, n % 2], near[:, n % 2], ACT.Exp).then_inc(answered, 1)
                act.wait_ge(answered, 3 * n + 1)
                act.activation(w[:, n % 2], e[:, n % 2], ACT.Identity, bias=C["ones"][:, 0:1]).then_inc(answered, 1)
                act.wait_ge(answered, 3 * n + 2)
                act.activation(ln[:, n % 2], w[:, n % 2], ACT.Ln).then_inc(answered, 1)

        @block.vector
        def _(v):
            step = st.steps(v, chain)
            v.wait_ge(loads, 48)

            def add_bias(c):
                v.wait_ge(steps_made, c + 1)
                for m in range(KT):
                    ins = v.tensor_scalar(DT[:, m, c * CHUNK:(c + 1) * CHUNK], d_ps[c % 2][m][:, 0:CHUNK], b[:, m:m + 1], None, ALU.add)
                ins.then_inc(steps_out, 1)
            for c in range(CHUNKS // 2):
                add_bias(c)
            v.wait_ge(steps_out, CHUNKS // 2)
            def ask(n):
                m, at = pieces[n]
                v.scalar_tensor_tensor(near[:, n % 2], DT[:, m, at], -1.0, DT[:, m, at], ALU.mult, ALU.min).then_inc(asked, 1)
            ask(0)
            ask(1)
            for c in range(CHUNKS // 2, CHUNKS):
                add_bias(c)
            v.wait_ge(steps_out, CHUNKS)
            for n, (m, at) in enumerate(pieces):
                i = n % 2
                v.wait_ge(answered, 3 * n + 3)
                step(v.scalar_tensor_tensor(w[:, i], w[:, i], 1.0, e[:, i], ALU.subtract, ALU.subtract))
                step(v.tensor_tensor(ln[:, i], ln[:, i], w[:, i], ALU.subtract))
                v.wait_ge(series, 2 * n + 2)
                step(v.scalar_tensor_tensor(short[:, i], short[:, i], -0.5, e[:, i], ALU.add, ALU.mult))
                step(v.scalar_tensor_tensor(short[:, i], short[:, i], 1.0, e[:, i], ALU.add, ALU.mult))
                step(v.tensor_tensor(ln[:, i], ln[:, i], short[:, i], ALU.subtract))
                step(v.scalar_tensor_tensor(ln[:, i], e[:, i], SMALL, ln[:, i], ALU.is_ge, ALU.mult))
                step(v.tensor_tensor(ln[:, i], ln[:, i], short[:, i], ALU.add))
                step(v.scalar_tensor_tensor(DT[:, m, at], DT[:, m, at], 0.0, ln[:, i], ALU.max, ALU.add))
                v.sem_inc(done, 1)
                if n + 2 < len(pieces):
                    ask(n + 2)


def scan_stage(nc, st, C, A, D, XC, DT, U, GATE):
    SPAN = ROWS // SPANS
    PIECES = SPAN // CHUNK
    a, d_par = st.sb("a", [P, KT, STATES]), st.sb("d_par", [P, KT])
    rows = st.sb("rows", [P, 2, 2, SPAN])
    decay, feed, state, seen = (st.sb(n, [P, KT, SPAN]) for n in ("decay", "feed", "state", "seen"))
    end = st.sb("end", [P, KT, STATES])
    y_ps = [[st.ps(f"y_ps{m}{c}", [P, 512]) for c in range(PIECES)] for m in range(KT)]
    b_in, c_in = ([st.sem(f"{k}_in{s}") for s in range(2)] for k in "bc")
    loads, chain, decays, feeds, scans, seens, sums, cleared, ready = (st.sem(n) for n in (
        "loads", "chain", "decays", "feeds", "scans", "seens", "sums", "cleared", "ready"))

    def each_state(eng, body):
        body(0, 0)
        body(1, 1)
        with eng.Fori(1, STATES // 2 - 1) as i:
            body(i * 2, 0)
            body(i * 2 + 1, 1)
        body(STATES - 2, 0)
        body(STATES - 1, 1)

    def fresh(span, s):
        return span == 0 and isinstance(s, int) and s < 2

    def begun(span, s):
        return span == 0 and isinstance(s, int) and s == 0

    with st.block() as block:
        @block.sync
        def _(sp):
            sp.dma_start(a[:], A["L1_gnn_A_log"].rearrange("(k p) n -> p k n", p=P)).then_inc(loads, 16)
            sp.dma_start(d_par[:], A["L1_gnn_D_param"]).then_inc(loads, 16)
            for span in range(SPANS):
                def load(s, slot):
                    n = s + span * STATES
                    for i, (used, brought) in enumerate(((feeds, b_in), (seens, c_in))):
                        if not fresh(span, s):
                            hold(sp, st.passed, used, (n - 1) * KT)
                        sp.dma_start(rows[:, slot, i, :], D["bc"][ds(s + i * STATES, 1), span * SPAN:(span + 1) * SPAN].rearrange(
                            "a n -> (a n)").partition_broadcast(P)).then_inc(brought[slot], 16)
                each_state(sp, load)

        @block.scalar
        def _(act):
            act.wait_ge(loads, 32)
            act.activation(a[:], a[:], ACT.Exp).then_inc(ready, 1)
            act.wait_ge(ready, 1)
            act.mul(a[:], a[:], -1.0).then_inc(ready, 1)
            act.wait_ge(ready, 2)
            for span in range(SPANS):
                def decay_of(s, slot):
                    for m in range(KT):
                        i = (s + span * STATES) * KT + m
                        if not begun(span, s):
                            hold(act, st.passed, scans, i - 1)
                        act.activation(decay[:, m, :], DT[:, m, span * SPAN:(span + 1) * SPAN], ACT.Exp, scale=a[:, m, ds(s, 1)]).then_inc(decays, 1)
                each_state(act, decay_of)

        @block.gpsimd
        def _(pool):
            for span in range(SPANS):
                def feed_of(s, slot):
                    n = s + span * STATES
                    hold(pool, st.passed, b_in[slot], (n - slot) * 8 + 16)
                    for m in range(KT):
                        if not begun(span, s):
                            hold(pool, st.passed, scans, n * KT + m - 1)
                        pool.tensor_tensor(feed[:, m, :], U[:, m, span * SPAN:(span + 1) * SPAN], rows[:, slot, 0, :], ALU.mult).then_inc(feeds, 1)
                each_state(pool, feed_of)

        @block.vector
        def _(v):
            step = st.steps(v, chain)
            v.wait_ge(loads, 32)
            for span in range(SPANS):
                def scan(s, slot, m):
                    i = (s + span * STATES) * KT + m
                    hold(v, st.passed, decays, i + 1)
                    hold(v, st.passed, feeds, i + 1)
                    if not begun(span, s):
                        hold(v, st.passed, seens, i - 1)
                    start = end[:, m, ds(s, 1)] if span else 0.0
                    v.tensor_tensor_scan(state[:, m, :], decay[:, m, :], feed[:, m, :], start, ALU.mult, ALU.add).then_inc(scans, 1)

                def see(s, slot, m):
                    i = (s + span * STATES) * KT + m
                    hold(v, st.passed, scans, i + 1)
                    if span < SPANS - 1:
                        v.tensor_copy(end[:, m, ds(s, 1)], state[:, m, SPAN - 1:SPAN])
                    hold(v, st.passed, c_in[slot], (s - slot) * 8 + (span * STATES * 8 + 16))
                    if not begun(span, s):
                        hold(v, st.passed, sums, i - 1)
                    v.tensor_tensor(seen[:, m, :], state[:, m, :], rows[:, slot, 1, :], ALU.mult).then_inc(seens, 1)

                def walk(s, slot, more=True):
                    scan(s, slot, 1)
                    see(s, slot, 0)
                    if more:
                        scan(s + 1, 1 - slot, 0)
                    see(s, slot, 1)
                scan(0, 0, 0)
                walk(0, 0)
                walk(1, 1)
                with v.Fori(1, STATES // 2 - 1) as i:
                    walk(i * 2, 0)
                    walk(i * 2 + 1, 1)
                walk(STATES - 2, 0)
                walk(STATES - 1, 1, False)
                v.wait_ge(sums, (span + 1) * STATES * KT)
                for m in range(KT):
                    for c in range(PIECES):
                        at = slice(span * SPAN + c * CHUNK, span * SPAN + (c + 1) * CHUNK)
                        step(v.scalar_tensor_tensor(XC[:, m, at], XC[:, m, at], d_par[:, m:m + 1], y_ps[m][c][:, 0:CHUNK], ALU.mult, ALU.add))
                v.sem_inc(cleared, 1)
                at = slice(span * SPAN, (span + 1) * SPAN)
                step(v.tensor_tensor(XC[:, :, at], XC[:, :, at], GATE[:, :, at], ALU.mult))

        @block.tensor
        def _(pe):
            for span in range(SPANS):
                if span:
                    pe.wait_ge(cleared, span)

                def add(s, slot):
                    for m in range(KT):
                        i = (s + span * STATES) * KT + m
                        hold(pe, st.passed, seens, i + 1)
                        for c in range(PIECES):
                            ins = pe.matmul(y_ps[m][c][:, 0:CHUNK], C["ident"][:], seen[:, m, c * CHUNK:(c + 1) * CHUNK],
                                            start=isinstance(s, int) and s == 0, stop=isinstance(s, int) and s == STATES - 1)
                        ins.then_inc(sums, 1)
                each_state(pe, add)


def out_proj_stage(nc, st, C, A, D, Y):
    BANKS = 4
    w = st.sb("w", [P, KT, DIM])
    row = st.sb("row", [P, BANKS, DIM])
    ps = [st.ps(f"ps{i}", [P, DIM]) for i in range(BANKS)]
    loads, made, out = (st.sem(n) for n in ("loads", "made", "out"))
    stored = [st.sem(f"stored{s}") for s in range(BANKS)]
    with st.block() as block:
        @block.sync
        def _(sp):
            sp.dma_start(w[:], A["L1_gnn_out_proj_w"].rearrange("(k p) n -> p k n", p=P)).then_inc(loads, 16)

            for t in range(TILES):
                sp.wait_ge(out, t + 1)
                sp.dma_start(D["y"][t * P:(t + 1) * P, :], row[:, t % BANKS, :]).then_inc(stored[t % BANKS], 16)
            for slot in range(BANKS):
                sp.wait_ge(stored[slot], 16 * len(range(slot, TILES, BANKS)))

        @block.tensor
        def _(pe):
            pe.wait_ge(loads, 16)

            for t in range(TILES):
                if t >= BANKS:
                    pe.wait_ge(out, t - BANKS + 1)
                for k in range(KT):
                    ins = pe.matmul(ps[t % BANKS][:], Y[:, k, t * P:(t + 1) * P], w[:, k, :], start=(k == 0), stop=(k == KT - 1))
                ins.then_inc(made, 1)

        @block.scalar
        def _(act):
            for t in range(TILES):
                act.wait_ge(made, t + 1)
                if t >= BANKS:
                    act.wait_ge(stored[t % BANKS], t // BANKS * 16)
                act.activation(row[:, t % BANKS, :], ps[t % BANKS][:], ACT.Copy).then_inc(out, 1)


def elu_stage(nc, st, C, D, HL):
    low = st.sb("low", [P, TILES // 5, DIM])
    chain, asked, answered, made, stored = (st.sem(n) for n in ("chain", "asked", "answered", "made", "stored"))
    with st.block() as block:
        @block.sync
        def _(sp):
            for q in range(5):
                part = slice(q * (TILES // 5), (q + 1) * (TILES // 5))
                sp.wait_ge(made, q + 1)
                sp.dma_start(D["hl"].rearrange("(t p) d -> p t d", p=P)[:, part, :], HL[:, part, :]).then_inc(stored, 16)
            sp.wait_ge(stored, 80)

        @block.vector
        def _(v):
            step = st.steps(v, chain)
            for q in range(5):
                part = HL[:, q * (TILES // 5):(q + 1) * (TILES // 5), :]
                step(v.tensor_scalar(low[:], part, 0.0, None, ALU.min))
                v.sem_inc(asked, 1)
                step(v.tensor_scalar(part, part, 0.0, -1.0, ALU.max, ALU.add))
                v.wait_ge(answered, q + 1)
                step(v.tensor_tensor(part, part, low[:], ALU.add))
                v.sem_inc(made, 1)

        @block.scalar
        def _(act):
            for q in range(5):
                act.wait_ge(asked, q + 1)
                act.activation(low[:], low[:], ACT.Exp).then_inc(answered, 1)


def collect_rows_stage(nc, st, C, D, X, HL, HA, HAT, hl_ready, ha_ready):
    got = HAT[:].rearrange("p k n -> p (k n)").rearrange("p (t d) -> p t d", t=TILES)
    loads = st.sem("loads")
    placed = C["placed"]
    tiles = "(t p) d -> p t d"
    with st.block() as block:
        @block.sync
        def _(sp):
            for sem, name, rows in ((hl_ready, "hl", HL), (loads, "z", HA), (loads, "x", X)):
                sp.dma_start(rows[:], D[name].rearrange(tiles, p=P)).then_inc(sem, 16)

        @block.gpsimd
        def _(pool):
            for t in range(TILES):
                pool.indirect_dma_start(got[:, t, :], None, D["y"], bass.IndirectOffsetOnAxis(C["rank"][:, t:t + 1], 0)).then_inc(placed.sem, 16)

        @block.vector
        def _(v):
            v.wait_ge(loads, 32)
            v.wait_ge(placed.sem, placed.base + 16 * TILES)
            v.tensor_tensor(HA[:], HA[:], got[:], ALU.add).then_inc(ha_ready, 1)
    placed.base += 16 * TILES


def gate_ff_stage(nc, st, C, A, HLT, HAT, VT):
    wl, wg = st.sb("wl", [P, KT, DIM]), st.sb("wg", [P, KT, DIM])
    w1, w2 = st.sb("w1", [P, KT, 2 * DIM]), st.sb("w2", [P, 2 * KT, DIM])
    b1, b2 = st.sb("b1", [P, 2 * KT]), st.sb("b2", [P, KT])
    gate, dif = st.sb("gate", [P, 2, KT, CHUNK]), st.sb("dif", [P, KT, CHUNK])
    h = st.sb("h", [P, 2, KT, CHUNK])
    r = st.sb("r", [P, 2 * KT, CHUNK])
    g_ps = [st.ps(f"g_ps{m}", [P, 512]) for m in range(KT)]
    f_ps = [st.ps(f"f_ps{m}", [P, 512]) for m in range(2 * KT)]
    o_ps = [st.ps(f"o_ps{m}", [P, 512]) for m in range(KT)]
    loads, chain, gated, exped, mixed, hidden, relued, made, out, powers, asked = (st.sem(n) for n in (
        "loads", "chain", "gated", "exped", "mixed", "hidden", "relued", "made", "out", "powers", "asked"))

    def each_chunk(eng, body):
        with eng.Fori(0, CHUNKS // 2 - 1) as i:
            body(i * 2, 0, True)
            body(i * 2 + 1, 1, True)
        body(CHUNKS - 2, 0, False)
        body(CHUNKS - 1, 1, False)

    with st.block() as block:
        @block.sync
        def _(sp):
            for tile, name in ((wl, "wl"), (wg, "wg"), (w1, "ff1_w"), (w2, "ff2_w")):
                sp.dma_start(tile[:], A[f"L1_gnn_{name}"].rearrange("(k p) n -> p k n", p=P)).then_inc(loads, 16)
            sp.dma_start(b1[:], A["L1_gnn_ff1_b"]).then_inc(loads, 16)
            sp.dma_start(b2[:], A["L1_gnn_ff2_b"]).then_inc(loads, 16)
            sp.wait_ge(loads, 96)

        @block.tensor
        def _(pe):
            pe.wait_ge(loads, 96)

            def gates(c):
                if not (isinstance(c, int) and c == 0):
                    hold(pe, st.passed, asked, c)
                at = ds(c * CHUNK, CHUNK)
                for m in range(KT):
                    to = slice(m * P, (m + 1) * P)
                    for n, (w, src) in enumerate(((wl, HLT), (wg, HAT))):
                        for k in range(KT):
                            ins = pe.matmul(g_ps[m][:, 0:CHUNK], w[:, k, to], src[:, k, at], start=(n + k == 0), stop=(n == 1 and k == KT - 1))
                ins.then_inc(gated, 1)

            def chunk(c, slot, more):
                hold(pe, st.passed, mixed, c + 1)
                for m in range(2 * KT):
                    for k in range(KT):
                        ins = pe.matmul(f_ps[m][:, 0:CHUNK], w1[:, k, m * P:(m + 1) * P], h[:, slot, k, :], start=(k == 0), stop=(k == KT - 1))
                ins.then_inc(hidden, 1)
                if more:
                    gates(c + 2)
                hold(pe, st.passed, relued, c + 1)
                hold(pe, st.passed, out, c + 1)
                for m in range(KT):
                    for k in range(2 * KT):
                        ins = pe.matmul(o_ps[m][:, 0:CHUNK], w2[:, k, m * P:(m + 1) * P], r[:, k, :], start=(k == 0), stop=(k == 2 * KT - 1))
                ins.then_inc(made, 1)
            gates(0)
            gates(1)
            each_chunk(pe, chunk)

        @block.scalar
        def _(act):
            act.wait_ge(loads, 96)

            def exps(c, slot):
                hold(act, st.passed, gated, c + 1)
                for m in range(KT):
                    ins = act.activation(gate[:, slot, m, :], g_ps[m][:, 0:CHUNK], ACT.Abs)
                ins.then_inc(powers, 1)
                hold(act, st.passed, powers, c * 2 + 1)
                act.activation(gate[:, slot], gate[:, slot], ACT.Exp, scale=-1.0).then_inc(powers, 1)
                hold(act, st.passed, powers, c * 2 + 2)
                act.activation(gate[:, slot], gate[:, slot], ACT.Ln, bias=C["ones"][:, 0:1]).then_inc(exped, 1)
                hold(act, st.passed, asked, c + 1)
                act.activation(gate[:, slot], gate[:, slot], ACT.Exp).then_inc(exped, 1)

            def chunk(c, slot, more):
                hold(act, st.passed, hidden, c + 1)
                for m in range(2 * KT):
                    ins = act.activation(r[:, m, :], f_ps[m][:, 0:CHUNK], ACT.Relu, bias=b1[:, m:m + 1])
                ins.then_inc(relued, 1)
                if more:
                    exps(c + 2, slot)
            exps(0, 0)
            exps(1, 1)
            each_chunk(act, chunk)

        @block.vector
        def _(v):
            step = st.steps(v, chain)
            v.wait_ge(loads, 96)

            def gate_of(c, slot):
                step.turn(c, 3)
                at = ds(c * CHUNK, CHUNK)
                step(v.tensor_tensor(dif[:], HLT[:, :, at], HAT[:, :, at], ALU.subtract))
                hold(v, st.passed, exped, c * 2 + 1)
                for m in range(KT):
                    x = g_ps[m][:, 0:CHUNK]
                    ins = v.scalar_tensor_tensor(gate[:, slot, m, :], x, 0.0, gate[:, slot, m, :], ALU.min, ALU.subtract)
                ins.then_inc(asked, 1)
                hold(v, st.passed, exped, c * 2 + 2)
                step(v.tensor_tensor(dif[:], dif[:], gate[:, slot], ALU.mult))

            def mix(c, slot):
                step(v.tensor_tensor(h[:, slot], dif[:], HAT[:, :, ds(c * CHUNK, CHUNK)], ALU.add))
                step.end_turn()
                v.sem_inc(mixed, 1)

            def chunk(c, slot, more):
                if more:
                    gate_of(c + 2, slot)
                hold(v, st.passed, made, c + 1)
                for m in range(KT):
                    ins = v.scalar_tensor_tensor(VT[:, m, ds(c * CHUNK, CHUNK)], o_ps[m][:, 0:CHUNK], b2[:, m:m + 1], h[:, slot, m, :], ALU.add, ALU.add)
                ins.then_inc(out, 1)
                if more:
                    hold(v, st.passed, out, c + 2)
                    mix(c + 2, slot)
            v.sem_inc(out, 1)
            for c in range(2):
                gate_of(c, c)
                mix(c, c)
            each_chunk(v, chunk)


def add_stage(st, X, V, added):
    with st.block() as block:
        @block.vector
        def _(v):
            v.tensor_tensor(X[:], X[:], V[:], ALU.add).then_inc(added, 1)


def expert_weights_stage(nc, st, A, weights):
    w1, w2, wo, wr, br, bo, par = weights
    loads = st.sem("loads")
    with st.block() as block:
        @block.sync
        def _(sp):
            for tile, name in zip((w1, w2, wo), ("W1", "W2", "Wo")):
                sp.dma_start(tile[:], A[f"L1_ffn_{name}"].rearrange("e (k p) n -> p e k n", p=P)).then_inc(loads, 16)
            sp.dma_start(wr[:], A["L1_ffn_Wr"].rearrange("(k p) n -> p k n", p=P)).then_inc(loads, 16)
            sp.dma_start(br[:], A["L1_ffn_br"].partition_broadcast(P)).then_inc(loads, 16)
            sp.dma_start(bo[:], A["L1_ffn_bo"]).then_inc(loads, 16)
            for n in range(2):
                for i, name in enumerate(("b", "g", "be", "m", "v")):
                    sp.dma_start(par[:, n, i, :], A[f"L1_ffn_{name}{n + 1}"]).then_inc(loads, 16)
            sp.wait_ge(loads, 16 * 16)


def experts_stage(nc, st, C, A, XT, X, weights, out):
    LOT = 4 * P
    LOTS = ROWS // LOT
    w1, w2, wo, wr, br, bo, par = weights
    scale, shift = st.sb("scale", [P, 2, EXPERTS * KT]), st.sb("shift", [P, 2, EXPERTS * KT])
    eps = st.sb("eps", [P, 1])
    xt = st.sb("xt", [P, 2, KT, LOT])
    h1, h2 = st.sb("h1", [P, 2, KT, LOT]), st.sb("h2", [P, 2, KT, LOT])
    share, top = st.sb("share", [P, 2, 4, EXPERTS]), st.sb("top", [P, 4])
    shareT = st.sb("shareT", [EXPERTS, 4, P])
    stored = st.sem("stored")
    p1 = [st.ps(f"p1{m}", [P, 512]) for m in range(KT)]
    p2 = [st.ps(f"p2{m}", [P, 512]) for m in range(KT)]
    y_ps = [st.ps(f"y_ps{i}", [P, 2, DIM]) for i in range(2)]
    r_ps = st.ps("r_ps", [P, 4, EXPERTS])
    t_ps = st.ps("t_ps", [EXPERTS, 4, P])
    chain, folded, sqrts, brought, routed, shifted, exped, shared, turned, turned_out = (st.sem(n) for n in (
        "chain", "folded", "sqrts", "brought", "routed", "shifted", "exped", "shared", "turned", "turned_out"))
    made1, out1, made2, out2, made3, added, lot_done = (st.sem(n) for n in ("made1", "out1", "made2", "out2", "made3", "added", "lot_done"))

    def each_lot(eng, body):
        body(0, 4, 0)
        body(1, 4, 1)
        with eng.Fori(1, LOTS // 2) as i:
            body(i * 2, 4, 0)
            body(i * 2 + 1, 4, 1)
        body(LOTS, TILES - 4 * LOTS, 0)

    with st.block() as block:
        @block.sync
        def _(sp):
            def store(q, tiles, slot):
                hold(sp, st.passed, added, (q + 1) * (EXPERTS + 1))
                if tiles == 4:
                    sp.dma_start(out[ds(q * LOT, LOT), :].rearrange("(t p) d -> p t d", p=P), X[:, ds(q * 4, 4), :]).then_inc(stored, 16)
                else:
                    sp.dma_start(out[LOTS * LOT:NODES, :], X[0:NODES - LOTS * LOT, TILES - 1, :]).then_inc(stored, 16)
            each_lot(sp, store)
            sp.wait_ge(stored, 16 * (LOTS + 1))

        @block.gpsimd
        def _(pool):
            def bring(q, tiles, slot):
                if not isinstance(q, int) or q >= 2:
                    hold(pool, st.passed, lot_done, q - 1)
                for k in range(KT):
                    ins = pool.tensor_copy(xt[:, slot, k, 0:tiles * P], XT[:, k, ds(q * LOT, tiles * P)])
                ins.then_inc(brought, 1)
            each_lot(pool, bring)

        @block.tensor
        def _(pe):
            pe.wait_ge(folded, 2)

            def lot(q, tiles, slot):
                n = tiles * P
                e0 = q * EXPERTS
                hold(pe, st.passed, brought, q + 1)
                for t in range(tiles):
                    for k in range(KT):
                        ins = pe.matmul(r_ps[:, t, :], xt[:, slot, k, t * P:(t + 1) * P], wr[:, k, :], start=(k == 0), stop=(k == KT - 1))
                ins.then_inc(routed, 1)

                def first(e):
                    if e:
                        hold(pe, st.passed, out1, e0 + e)
                    for m in range(KT):
                        for k in range(KT):
                            ins = pe.matmul(p1[m][:, 0:n], w1[:, e, k, m * P:(m + 1) * P], xt[:, slot, k, 0:n], start=(k == 0), stop=(k == KT - 1))
                    ins.then_inc(made1, 1)

                def second(e):
                    hold(pe, st.passed, out1, e0 + e + 1)
                    if e:
                        hold(pe, st.passed, out2, e0 + e)
                    for m in range(KT):
                        for k in range(KT):
                            ins = pe.matmul(p2[m][:, 0:n], w2[:, e, k, m * P:(m + 1) * P], h1[:, e % 2, k, 0:n], start=(k == 0), stop=(k == KT - 1))
                    ins.then_inc(made2, 1)

                def third(e):
                    hold(pe, st.passed, out2, e0 + e + 1)
                    hold(pe, st.passed, added, q * (EXPERTS + 1) + e + 1)
                    for t in range(tiles):
                        for k in range(KT):
                            ins = pe.matmul(y_ps[t // 2][:, t % 2, :], h2[:, e % 2, k, t * P:(t + 1) * P], wo[:, e, k, :], start=(k == 0), stop=(k == KT - 1))
                    ins.then_inc(made3, 1)
                first(0)
                first(1)
                hold(pe, st.passed, shared, q + 1)
                for t in range(tiles):
                    ins = pe.transpose(t_ps[:, t, :], share[:, slot, t, :], C["ident"][:])
                ins.then_inc(turned, 1)
                second(0)
                hold(pe, st.passed, turned_out, q + 1)
                if not isinstance(q, int) or q:
                    hold(pe, st.passed, added, q * (EXPERTS + 1))
                for t in range(tiles):
                    ins = pe.matmul(y_ps[t // 2][:, t % 2, :], shareT[:, t, :], bo[:], start=True, stop=True)
                ins.then_inc(made3, 1)
                for e in range(EXPERTS):
                    if e + 2 < EXPERTS:
                        first(e + 2)
                    if e + 1 < EXPERTS:
                        second(e + 1)
                    third(e)
            each_lot(pe, lot)

        @block.scalar
        def _(act):
            act.wait_ge(folded, 1)
            act.activation(scale[:], scale[:], ACT.Sqrt).then_inc(sqrts, 1)
            act.wait_ge(folded, 2)

            def lot(q, tiles, slot):
                n = tiles * P
                e0 = q * EXPERTS

                def relu(made, out, ps, h, layer, e):
                    hold(act, st.passed, made, e0 + e + 1)
                    for m in range(KT):
                        col = slice(e * KT + m, e * KT + m + 1)
                        ins = act.activation(h[:, e % 2, m, 0:n], ps[m][:, 0:n], ACT.Relu, bias=shift[:, layer, col], scale=scale[:, layer, col])
                    ins.then_inc(out, 1)
                hold(act, st.passed, shifted, q + 1)
                act.activation(share[:, slot, 0:tiles, :], share[:, slot, 0:tiles, :], ACT.Exp).then_inc(exped, 1)
                relu(made1, out1, p1, h1, 0, 0)
                relu(made1, out1, p1, h1, 0, 1)
                relu(made2, out2, p2, h2, 1, 0)
                for e in range(EXPERTS):
                    if e + 2 < EXPERTS:
                        relu(made1, out1, p1, h1, 0, e + 2)
                    if e + 1 < EXPERTS:
                        relu(made2, out2, p2, h2, 1, e + 1)
            each_lot(act, lot)

        @block.vector
        def _(v):
            step = st.steps(v, chain)
            step(v.memset(eps[:], 1.0e-3))
            for n in range(2):
                step(v.tensor_scalar(scale[:, n, :], par[:, n, 4, :], eps[:], None, ALU.add))
                step(v.tensor_tensor(shift[:, n, :], par[:, n, 0, :], par[:, n, 3, :], ALU.subtract))
            v.sem_inc(folded, 1)
            v.wait_ge(sqrts, 1)
            step(v.reciprocal(scale[:], scale[:]))
            step(v.tensor_tensor(scale[:], scale[:], par[:, :, 1, :], ALU.mult))
            step(v.tensor_tensor(shift[:], shift[:], scale[:], ALU.mult))
            step(v.tensor_tensor(shift[:], shift[:], par[:, :, 2, :], ALU.add))
            v.sem_inc(folded, 1)

            def lot(q, tiles, slot):
                step.turn(q, 5 + EXPERTS)
                sh = share[:, slot, 0:tiles, :]
                hold(v, st.passed, routed, q + 1)
                step(v.tensor_tensor(sh, r_ps[:, 0:tiles, :], br[:].unsqueeze(1).to_broadcast([P, tiles, EXPERTS]), ALU.add))
                step(v.tensor_reduce(top[:, 0:tiles], sh, AX_X, ALU.max))
                v.tensor_tensor(sh, sh, top[:, 0:tiles].unsqueeze(2).to_broadcast([P, tiles, EXPERTS]), ALU.subtract).then_inc(shifted, 1)
                hold(v, st.passed, exped, q + 1)
                step(v.tensor_reduce(top[:, 0:tiles], sh, AX_X, ALU.add))
                step.hold(v.reciprocal(top[:, 0:tiles], top[:, 0:tiles]))
                step(v.tensor_tensor(sh, sh, top[:, 0:tiles].unsqueeze(2).to_broadcast([P, tiles, EXPERTS]), ALU.mult))
                v.sem_inc(shared, 1)
                hold(v, st.passed, turned, q + 1)
                v.tensor_copy(shareT[:, 0:tiles, :], t_ps[:, 0:tiles, :]).then_inc(turned_out, 1)
                for e in range(-1, EXPERTS):
                    hold(v, st.passed, made3, q * (EXPERTS + 1) + e + 2)
                    for t in range(tiles):
                        row = X[:, ds(q * 4 + t, 1), :].rearrange("p a d -> p (a d)")
                        if e < 0:
                            ins = v.tensor_tensor(row, row, y_ps[t // 2][:, t % 2, :], ALU.add)
                        else:
                            ins = v.scalar_tensor_tensor(row, y_ps[t // 2][:, t % 2, :], share[:, slot, t, e:e + 1], row, ALU.mult, ALU.add)
                    if e < EXPERTS - 1:
                        step(ins)
                        v.sem_inc(added, 1)
                    else:
                        ins.then_inc(added, 1)
                v.sem_inc(lot_done, 1)
                step.end_turn()
            each_lot(v, lot)


def program(nc, A, out):
    def dram(name, shape, dt=F32):
        return nc.dram_tensor(name, shape, dt).ap()

    D = {
        "key": dram("key_d", (ROWS,)), "table": dram("table_d", (ROWS, HROW)),
        "ed": dram("ed_d", (ROWS, HEADS)), "by_edge": dram("by_edge_d", (P * STREAM, HEADS)),
        "ordered": dram("ordered_d", (ROWS, DIM)), "x": dram("x_d", (ROWS, DIM)), "z": dram("z_d", (ROWS, DIM)),
        "hl": dram("hl_d", (ROWS, DIM)), "bc": dram("bc_d", (2 * STATES, ROWS)), "y": dram("y_d", (ROWS, DIM)),
        "sums": dram("sums_d", (P * STREAM, HROW)),
    }
    with ExitStack() as whole:
        def keep(name, shape, dt=F32):
            return whole.enter_context(nc.sbuf_tensor(name, shape, dt))
        C = {
            "src_idx": keep("src_idx", [P, STREAM], I32), "dst_idx": keep("dst_idx", [P, STREAM], I32),
            "ones": keep("ones", [P, P]), "eps5": keep("eps5", [P, 1]), "ident": keep("ident", [P, P]),
            "above": keep("above", [P, P]), "below": keep("below", [P, P]),
            "not_before": keep("not_before", [P, P]),
            "same_prev": keep("same_prev", [P, STREAM]), "cut_prev": keep("cut_prev", [P, STREAM]), "key": keep("key", [P, TILES]),
            "rank_parts": keep("rank_parts", [P, 3, TILES]),
            "ends_in": keep("ends_in", [P, 1]), "dst_first": keep("dst_first", [P, 1]),
            "last_edge": keep("last_edge", [P, TILES], I32), "first_edge": keep("first_edge", [P, TILES], I32),
            "has_edge": keep("has_edge", [P, TILES]), "rank": keep("rank", [P, TILES], I32),
            "carried": keep("carried", [P, HROW + 1]), "tile_start": keep("tile_start", [P, TILES]),
        }
        passed = whole.enter_context(nc.semaphore("passed"))

        def lasting(name):
            return Lasting(whole.enter_context(nc.semaphore(name)))
        C["arrived"] = [[lasting(f"arrived{s}{u}") for u in range(GROUP)] for s in range(RING)]
        C["placed"], C["ed_in"] = lasting("placed"), lasting("ed_in")

        def stage(name, f, *args):
            with ExitStack() as ctx:
                st = Stage(nc, ctx, name, passed)
                f(nc, st, *args)
                st.end()

        @contextmanager
        def together(*names):
            with ExitStack() as ctx:
                with nc.Block() as block:
                    stages = [Stage(nc, ctx, name, passed, block) for name in names]
                    yield stages
                for st in stages:
                    for sem in st.sems:
                        nc.gpsimd.sem_clear(sem)
                nc.all_engine_barrier()

        def graph_layer(name, rows, XN, XT, W, a_src, a_dst, out_rows, base, bias, global_top, early, graph, keep={}):
            with ExitStack() as ctx:
                ed = ctx.enter_context(nc.sbuf_tensor(f"{name}_ed", [P, STREAM, HEADS], F32))
                with ExitStack() as inner:
                    esd = inner.enter_context(nc.sbuf_tensor(f"{name}_esd", [P, TILES, 2 * HEADS], F32))
                    raw = inner.enter_context(nc.sbuf_tensor(f"{name}_raw", [P, STREAM, HEADS], F32))
                    with together(f"{name}_norm", f"{name}_table", f"{name}_beside", f"{name}_scores") as (n, t, b, e):
                        zeroed = e.sem("zeroed")
                        begun = early(b)
                        clear_stage(nc, e, D, raw, zeroed)
                        xt_ready, esd_ready, ed_stored = (n.sem(k) for k in ("xt_ready", "esd_ready", "ed_stored"))
                        norm_stage(nc, n, C, rows, XN, XT, BANKS=2, ready=xt_ready)
                        table_stage(nc, t, C, D, XT, W, a_src, a_dst, esd, xt_ready, esd_ready, ed_stored)
                        known = graph(b, begun)
                        scores_stage(nc, e, C, D, esd, ed, raw, zeroed, known, esd_ready, ed_stored)
                stage(f"{name}_sum", sum_stage, C, D, ed)
            with together(f"{name}_nodes", f"{name}_keep") as (n, b):
                kept = b.sem("kept")
                for key, kept_rows in keep.items():
                    keep_rows_stage(nc, b, D, key, kept_rows, kept)
                nodes_stage(nc, n, C, D, out_rows, base, bias, global_top)
                if keep:
                    @b.shared.sync
                    def _(sp):
                        sp.wait_ge(kept, 16 * len(keep))

        RANKED = TILES // 3

        def find_edges(st, early):
            known = st.sem("known")
            graph_stage(nc, st, C, D, A, A["node_vec"], known)
            rank_stage(nc, st, C, *key_row_stage(nc, st, D), range(RANKED))
            return known

        def slice_layer(XN, XT, X):
            with ExitStack() as ctx:
                w_log = ctx.enter_context(nc.sbuf_tensor("w_log", [P, KT, SLICES], F32))
                b_log = ctx.enter_context(nc.sbuf_tensor("b_log", [P, SLICES], F32))
                SWT = ctx.enter_context(nc.sbuf_tensor("SWT", [P, SLICES // P, ROWS], F32))
                Z = ctx.enter_context(nc.sbuf_tensor("Z", [P, SLICES // P, DIM + 16], F32))
                mix = ctx.enter_context(nc.sbuf_tensor("mix", [P, SLICES // P, DIM], F32))
                with together("norm1", "slice_w") as (n, w):
                    norm_stage(nc, n, C, X, XN, XT, BANKS=2)
                    slice_weights_stage(nc, w, C, A, w_log, b_log)
                stage("assign", assign_stage, C, XN, XT, w_log, b_log, SWT, Z)
                stage("slice_a", slice_attention_stage, C, A, Z, mix)
                stage("mix", mix_stage, C, A, SWT, mix, X)

        def rows_of(ctx, name):
            return ctx.enter_context(nc.sbuf_tensor(name, [P, TILES, DIM], F32))

        def columns_of(ctx, name, extra=0):
            return ctx.enter_context(nc.sbuf_tensor(name, [P, KT, ROWS + extra], F32))

        with ExitStack() as ctx:
            X, XN = rows_of(ctx, "X"), rows_of(ctx, "XN")
            stage("constants", constants_stage, C, A, X, A["x"], A["src"], A["dst"])
            with ExitStack() as inner:
                XT = columns_of(inner, "XT")
                graph_layer("g0", X, XN, XT, A["L0_gnn_W"], A["L0_gnn_a_src"], A["L0_gnn_a_dst"], X, X, None, False, lambda st: None, find_edges)
                slice_layer(XN, XT, X)
            HL = rows_of(ctx, "HL")
            with ExitStack() as inner:
                XT = columns_of(inner, "XT2")
                graph_layer("g1", X, XN, XT, A["L1_gnn_gat_w"], A["L1_gnn_gat_a_src"], A["L1_gnn_gat_a_tgt"], HL, XN, A["L1_gnn_gat_b"], True,
                            lambda st: key_row_stage(nc, st, D),
                            lambda st, row: rank_stage(nc, st, C, *row, range(RANKED, TILES)), keep={"x": X, "z": XN})
            with together("elu", "spread") as (e, b):
                elu_stage(nc, e, C, D, HL)
                spread_rows_stage(nc, b, C, D, XN)
        with ExitStack() as ctx:
            XC, GATE, RAW, DT = columns_of(ctx, "XC"), columns_of(ctx, "GATE"), columns_of(ctx, "RAW", TAPS - 1), columns_of(ctx, "DT")
            stage("sequence", sequence_stage, C, A, D, DT, RAW, GATE, XC)
            U = RAW[:, :, 0:ROWS]
            stage("x_proj", x_proj_stage, C, A, D, XC, DT, U)
            stage("scan", scan_stage, C, A, D, XC, DT, U, GATE)
            stage("out_proj", out_proj_stage, C, A, D, XC)
        with ExitStack() as ctx:
            X = rows_of(ctx, "X2")
            HLT = columns_of(ctx, "HLT")
            layer = [P, EXPERTS, KT, DIM]
            weights = [ctx.enter_context(nc.sbuf_tensor(f"expert_{n}", shape, F32)) for n, shape in (
                ("w1", layer), ("w2", layer), ("wo", layer), ("wr", [P, KT, EXPERTS]), ("br", [P, EXPERTS]), ("bo", [EXPERTS, DIM]),
                ("par", [P, 2, 5, EXPERTS * KT]))]
            with ExitStack() as inner:
                HAT = columns_of(inner, "HAT")
                with ExitStack() as rows:
                    HL, HA = rows_of(rows, "HL2"), rows_of(rows, "HA")
                    with together("collect", "norm_l", "norm_g") as (c, l, g):
                        hl_ready, ha_ready = c.sem("hl_ready"), c.sem("ha_ready")
                        norm_stage(nc, l, C, HL, None, HLT, A["L1_gnn_ln_local_g"], A["L1_gnn_ln_local_b"], after=(hl_ready, 16))
                        collect_rows_stage(nc, c, C, D, X, HL, HA, HAT, hl_ready, ha_ready)
                        norm_stage(nc, g, C, HA, None, HAT, A["L1_gnn_ln_global_g"], A["L1_gnn_ln_global_b"], after=(ha_ready, 1))
                VT = columns_of(inner, "VT")
                stage("gate_ff", gate_ff_stage, C, A, HLT, HAT, VT)
                V = rows_of(inner, "V")
                XT = HLT
                with together("expert_weights", "turn", "norm3", "add", "norm4") as (w, t, n, a, m):
                    turned, added = t.sem("done"), a.sem("added")
                    expert_weights_stage(nc, w, A, weights)
                    turn_stage(nc, t, C, VT, V, turned)
                    norm_stage(nc, n, C, V, V, None, A["L1_gnn_ln2_g"], A["L1_gnn_ln2_b"], after=(turned, -(-TILES // 2)))
                    add_stage(a, X, V, added)
                    norm_stage(nc, m, C, X, None, XT, after=(added, 1))
            stage("experts", experts_stage, C, A, XT, X, weights, out)


_TURNED = ("L0_ffn_W_x", "L1_gnn_gat_w", "L1_gnn_in_proj_w", "L1_gnn_x_proj_w", "L1_gnn_dt_proj_w", "L1_gnn_out_proj_w", "L1_gnn_wl",
           "L1_gnn_wg", "L1_gnn_ff1_w", "L1_gnn_ff2_w")


def kernel(**inputs):
    import numpy as np
    import concourse.bacc as bacc
    from concourse.bass_utils import run_bass_kernel_spmd

    nc = bacc.Bacc("TRN2", target_bir_lowering=False, num_devices=1)
    arrays = {}
    for name, value in inputs.items():
        a = np.asarray(value)
        if name in _TURNED:
            a = a.T
        arrays[name] = np.ascontiguousarray(a)
    del arrays["edge_weight"]
    arrays["L0_ffn_b_x"] = np.ascontiguousarray(arrays["L0_ffn_b_x"].reshape(SH, SD).T)
    for name in ("ln_local_g", "ln_local_b", "ln_global_g", "ln_global_b", "conv_b", "dt_proj_b", "D_param", "ff1_b", "ff2_b"):
        a = arrays[f"L1_gnn_{name}"]
        arrays[f"L1_gnn_{name}"] = np.ascontiguousarray(a.reshape(-1, P).T)
    for name in ("b", "g", "be", "m", "v"):
        for n in (1, 2):
            a = arrays[f"L1_ffn_{name}{n}"]
            arrays[f"L1_ffn_{name}{n}"] = np.ascontiguousarray(a.reshape(-1, P).T)
    x = np.zeros((ROWS, DIM), arrays["x"].dtype)
    x[:NODES] = arrays["x"]
    arrays["x"] = x
    noise = np.zeros((ROWS,), arrays["node_vec"].dtype)
    noise[:NODES] = arrays["node_vec"]
    arrays["node_vec"] = noise
    for name in ("src", "dst"):
        e = np.full((P * STREAM,), NODES, np.int32)
        e[:EDGES] = arrays[name]
        arrays[name] = e.reshape(P, STREAM)
    arrays["minus_one"] = np.full((1, 2), -1, np.int32)
    arrays["tile_starts"] = (np.arange(TILES, dtype=np.float32) * P)[None, :]
    A = {name: nc.dram_tensor(f"in_{name}", a.shape, mybir.dt.from_np(a.dtype), kind="ExternalInput").ap() for name, a in arrays.items()}
    out = nc.dram_tensor("out_0", (NODES, DIM), mybir.dt.float32, kind="ExternalOutput").ap()
    program(nc, A, out)
    result = run_bass_kernel_spmd(nc, [{f"in_{name}": a for name, a in arrays.items()}], core_ids=[0])
    return result.results[0]["out_0"]
```
